# Optimizing a Trainium2 kernel written in Bass

```python
import numpy as np
import jax
import jax.numpy as jnp

def _softmax(x, axis=-1):
    return jax.nn.softmax(x, axis=axis)

def _gelu(x):
    return jax.nn.gelu(x, approximate=True)

def _silu(x):
    return jax.nn.silu(x)

def _sigmoid(x):
    return jax.nn.sigmoid(x)

def _layernorm(x, axis=-1, eps=1e-05):
    m = jnp.mean(x, axis=axis, keepdims=True)
    v = jnp.var(x, axis=axis, keepdims=True)
    return (x - m) / jnp.sqrt(v + eps)

def _scatter_add(tgt, idx, src, axis=0):
    return tgt.at[idx].add(src)

def _segment_sum(src, seg, n):
    return jax.ops.segment_sum(src, seg, n)
kernel_name = 'mk_lm_tower_d2_tok_ids768_r4_352e3c'

def setup_inputs(seed: int=0):
    np.random.seed(seed)
    _w = jnp.asarray

    def _rec_inputs():
        import jax
        import jax.numpy as jnp
        _rk = jax.random.key(seed)
        x = jax.random.randint(jax.random.fold_in(_rk, 1), (16, 256), 0, 12564, jnp.int32)
        return x
    x = _rec_inputs()

    def _L0_tok_setup():
        import jax, jax.numpy as jnp
        import numpy as np
        VOCAB = 50257
        DIM = 192
        RANK = 16
        ALPHA = 32.0
        SCALING = ALPHA / RANK
        key = jax.random.key(seed)
        k1, k2, k3, k4 = jax.random.split(key, 4)
        inputs = jax.random.randint(k1, (8, 512), 0, VOCAB, dtype=jnp.int32)
        embeddings = jax.random.uniform(k2, (VOCAB, DIM), dtype=jnp.float32, minval=-0.05, maxval=0.05)
        limit = float(np.sqrt(6.0 / VOCAB))
        lora_a = jax.random.uniform(k3, (VOCAB, RANK), dtype=jnp.float32, minval=-limit, maxval=limit)
        lora_b = jax.random.normal(k4, (RANK, DIM), dtype=jnp.float32) * 0.01
        magnitude = jnp.ones((DIM,), dtype=jnp.float32)
        return {'inputs': inputs, 'embeddings': embeddings, 'lora_a': lora_a, 'lora_b': lora_b, 'magnitude': magnitude}
    _L0_tok_all = _L0_tok_setup()
    _L0_tok_in = {k: v for k, v in _L0_tok_all.items() if k in ('embeddings', 'lora_a', 'lora_b', 'magnitude')}
    del _L0_tok_all

    def _L0_attn_setup():
        import jax, jax.numpy as jnp
        import numpy as np
        EPS = 1e-05
        B, T, C = (8, 512, 192)
        H = 4 * C
        LAYER_ID, N_LAYER = (4, 12)

        def _ln(x, w, b):
            mu = x.mean(-1, keepdims=True)
            var = ((x - mu) ** 2).mean(-1, keepdims=True)
            return (x - mu) / jnp.sqrt(var + EPS) * w + b

        def _wkv_scan(w, k, v):
            a0 = jnp.zeros(k.shape[1:], k.dtype)
            b0 = jnp.zeros_like(a0)
            m0 = jnp.full_like(a0, -1e+38)

            def step(carry, kv):
                a, b, m = carry
                kt, vt = kv
                mm = jnp.maximum(m + w, kt)
                e1 = jnp.exp(m + w - mm)
                e2 = jnp.exp(kt - mm)
                return ((e1 * a + e2 * vt, e1 * b + e2, mm), (a, b, m))
            _, (A, Bd, M) = jax.lax.scan(step, (a0, b0, m0), (k, v))
            return (A, Bd, M)

        def bi_wkv(w, u, k, v):
            kt = jnp.swapaxes(k, 0, 1)
            vt = jnp.swapaxes(v, 0, 1)
            af, bf, mf = _wkv_scan(w, kt, vt)
            ab, bb, mb = _wkv_scan(w, kt[::-1], vt[::-1])
            ab, bb, mb = (ab[::-1], bb[::-1], mb[::-1])
            kk = kt + u
            M = jnp.maximum(jnp.maximum(mf, mb), kk)
            ef = jnp.exp(mf - M)
            eb = jnp.exp(mb - M)
            ec = jnp.exp(kk - M)
            y = (ef * af + eb * ab + ec * vt) / (ef * bf + eb * bb + ec)
            return jnp.swapaxes(y, 0, 1)
        key = jax.random.key(seed)
        ks = jax.random.split(key, 9)
        x = jax.random.normal(ks[0], (B, T, C), jnp.float32)
        r01 = LAYER_ID / (N_LAYER - 1)
        h = np.arange(C, dtype=np.float64)
        decay = (-5.0 + 8.0 * (h / (C - 1)) ** (0.7 + 1.3 * r01)).astype(np.float32)
        zigzag = ((np.arange(C) + 1) % 3 - 1).astype(np.float32) * 0.5
        first = (np.float32(np.log(0.3)) + zigzag).astype(np.float32)
        s = 0.02
        return {'x': x, 'ln1_w': jnp.ones((C,), jnp.float32), 'ln1_b': jnp.zeros((C,), jnp.float32), 'ln2_w': jnp.ones((C,), jnp.float32), 'ln2_b': jnp.zeros((C,), jnp.float32), 'decay': jnp.asarray(decay), 'first': jnp.asarray(first), 'Wk_a': s * jax.random.normal(ks[1], (C, C), jnp.float32), 'Wv_a': s * jax.random.normal(ks[2], (C, C), jnp.float32), 'Wr_a': s * jax.random.normal(ks[3], (C, C), jnp.float32), 'Wo_a': s * jax.random.normal(ks[4], (C, C), jnp.float32), 'Wk_f': s * jax.random.normal(ks[5], (H, C), jnp.float32), 'Wv_f': s * jax.random.normal(ks[6], (C, H), jnp.float32), 'Wr_f': s * jax.random.normal(ks[7], (C, C), jnp.float32)}
    _L0_attn_all = _L0_attn_setup()
    _L0_attn_in = {k: v for k, v in _L0_attn_all.items() if k in ('ln1_w', 'ln1_b', 'ln2_w', 'ln2_b', 'decay', 'first', 'Wk_a', 'Wv_a', 'Wr_a', 'Wo_a', 'Wk_f', 'Wv_f', 'Wr_f')}
    del _L0_attn_all

    def _L0_ffn_setup():
        import jax, jax.numpy as jnp
        import numpy as np
        B, S, H = (4, 2048, 192)
        E, K = (8, 2)
        key = jax.random.key(seed)
        ks = jax.random.split(key, 5)
        scale = 1.0 / np.sqrt(H)
        x = jax.random.normal(ks[0], (B, S, H), dtype=jnp.float32)
        router_w = jax.random.uniform(ks[1], (E, H), jnp.float32, -scale, scale)
        router_b = jax.random.uniform(ks[2], (E,), jnp.float32, -scale, scale)
        expert_w = jax.random.uniform(ks[3], (E, H, H), jnp.float32, -scale, scale)
        expert_b = jax.random.uniform(ks[4], (E, H), jnp.float32, -scale, scale)
        return {'x': x, 'router_w': router_w, 'router_b': router_b, 'expert_w': expert_w, 'expert_b': expert_b}
    _L0_ffn_all = _L0_ffn_setup()
    _L0_ffn_in = {k: v for k, v in _L0_ffn_all.items() if k in ('router_w', 'router_b', 'expert_w', 'expert_b')}
    del _L0_ffn_all

    def _L1_attn_setup():
        import jax, jax.numpy as jnp
        import numpy as np
        EPS = 0.0001
        LN_EPS = 1e-05

        def _layernorm(x, g, b):
            m = jnp.mean(x, axis=-1, keepdims=True)
            v = jnp.mean(jnp.square(x - m), axis=-1, keepdims=True)
            return (x - m) * jax.lax.rsqrt(v + LN_EPS) * g + b

        def _softmax_features(x, proj, is_query):
            d = x.shape[-1]
            xn = x * d ** (-0.25)
            u = jnp.einsum('bhnd,md->bhnm', xn, proj)
            diag = 0.5 * jnp.sum(jnp.square(xn), axis=-1, keepdims=True)
            if is_query:
                stab = jnp.max(u, axis=-1, keepdims=True)
            else:
                stab = jnp.max(u, axis=(-2, -1), keepdims=True)
            ratio = proj.shape[0] ** (-0.5)
            return ratio * (jnp.exp(u - diag - stab) + EPS)
        B, N, E, H, M, F = (4, 512, 192, 12, 64, 768)
        Dh = E // H
        key = jax.random.key(seed)
        ks = jax.random.split(key, 4)
        return {'x': jax.random.normal(ks[0], (B, N, E), jnp.float32), 'proj': jax.random.normal(ks[1], (M, Dh), jnp.float32), 'ln1_g': jnp.ones((E,), jnp.float32), 'ln1_b': jnp.zeros((E,), jnp.float32), 'ln2_g': jnp.ones((E,), jnp.float32), 'ln2_b': jnp.zeros((E,), jnp.float32), 'W1': jax.random.normal(ks[2], (E, F), jnp.float32) * 0.02, 'b1': jnp.zeros((F,), jnp.float32), 'W2': jax.random.normal(ks[3], (F, E), jnp.float32) * 0.02, 'b2': jnp.zeros((E,), jnp.float32)}
    _L1_attn_all = _L1_attn_setup()
    _L1_attn_in = {k: v for k, v in _L1_attn_all.items() if k in ('proj', 'ln1_g', 'ln1_b', 'ln2_g', 'ln2_b', 'W1', 'b1', 'W2', 'b2')}
    del _L1_attn_all

    def _L1_ffn_setup():
        import jax, jax.numpy as jnp
        import numpy as np
        B, S, H, I = (4, 512, 192, 384)
        E, K = (3, 2)
        INIT = 0.02

        def _expert(x, gw, uw, dw):
            return jax.nn.silu(x @ gw) * (x @ uw) @ dw
        key = jax.random.key(seed)
        ks = jax.random.split(key, 8)
        f32 = jnp.float32
        return {'x': jax.random.normal(ks[0], (B, S, H), f32), 'shared_gate': jax.random.normal(ks[1], (H, I), f32) * INIT, 'shared_up': jax.random.normal(ks[2], (H, I), f32) * INIT, 'shared_down': jax.random.normal(ks[3], (I, H), f32) * INIT, 'routed_gate': jax.random.normal(ks[4], (E, H, I), f32) * INIT, 'routed_up': jax.random.normal(ks[5], (E, H, I), f32) * INIT, 'routed_down': jax.random.normal(ks[6], (E, I, H), f32) * INIT, 'router_w': jax.random.normal(ks[7], (H, E), f32) * INIT, 'routing_bias': jnp.zeros((E,), f32)}
    _L1_ffn_all = _L1_ffn_setup()
    _L1_ffn_in = {k: v for k, v in _L1_ffn_all.items() if k in ('shared_gate', 'shared_up', 'shared_down', 'routed_gate', 'routed_up', 'routed_down', 'router_w', 'routing_bias')}
    del _L1_ffn_all
    return {'x': x, 'L0_tok_embeddings': _L0_tok_in['embeddings'], 'L0_tok_lora_a': _L0_tok_in['lora_a'], 'L0_tok_lora_b': _L0_tok_in['lora_b'], 'L0_tok_magnitude': _L0_tok_in['magnitude'], 'L0_attn_ln1_w': _L0_attn_in['ln1_w'], 'L0_attn_ln1_b': _L0_attn_in['ln1_b'], 'L0_attn_ln2_w': _L0_attn_in['ln2_w'], 'L0_attn_ln2_b': _L0_attn_in['ln2_b'], 'L0_attn_decay': _L0_attn_in['decay'], 'L0_attn_first': _L0_attn_in['first'], 'L0_attn_Wk_a': _L0_attn_in['Wk_a'], 'L0_attn_Wv_a': _L0_attn_in['Wv_a'], 'L0_attn_Wr_a': _L0_attn_in['Wr_a'], 'L0_attn_Wo_a': _L0_attn_in['Wo_a'], 'L0_attn_Wk_f': _L0_attn_in['Wk_f'], 'L0_attn_Wv_f': _L0_attn_in['Wv_f'], 'L0_attn_Wr_f': _L0_attn_in['Wr_f'], 'L0_ffn_router_w': _L0_ffn_in['router_w'], 'L0_ffn_router_b': _L0_ffn_in['router_b'], 'L0_ffn_expert_w': _L0_ffn_in['expert_w'], 'L0_ffn_expert_b': _L0_ffn_in['expert_b'], 'L1_attn_proj': _L1_attn_in['proj'], 'L1_attn_ln1_g': _L1_attn_in['ln1_g'], 'L1_attn_ln1_b': _L1_attn_in['ln1_b'], 'L1_attn_ln2_g': _L1_attn_in['ln2_g'], 'L1_attn_ln2_b': _L1_attn_in['ln2_b'], 'L1_attn_W1': _L1_attn_in['W1'], 'L1_attn_b1': _L1_attn_in['b1'], 'L1_attn_W2': _L1_attn_in['W2'], 'L1_attn_b2': _L1_attn_in['b2'], 'L1_ffn_shared_gate': _L1_ffn_in['shared_gate'], 'L1_ffn_shared_up': _L1_ffn_in['shared_up'], 'L1_ffn_shared_down': _L1_ffn_in['shared_down'], 'L1_ffn_routed_gate': _L1_ffn_in['routed_gate'], 'L1_ffn_routed_up': _L1_ffn_in['routed_up'], 'L1_ffn_routed_down': _L1_ffn_in['routed_down'], 'L1_ffn_router_w': _L1_ffn_in['router_w'], 'L1_ffn_routing_bias': _L1_ffn_in['routing_bias']}

def reference(x, L0_tok_embeddings, L0_tok_lora_a, L0_tok_lora_b, L0_tok_magnitude, L0_attn_ln1_w, L0_attn_ln1_b, L0_attn_ln2_w, L0_attn_ln2_b, L0_attn_decay, L0_attn_first, L0_attn_Wk_a, L0_attn_Wv_a, L0_attn_Wr_a, L0_attn_Wo_a, L0_attn_Wk_f, L0_attn_Wv_f, L0_attn_Wr_f, L0_ffn_router_w, L0_ffn_router_b, L0_ffn_expert_w, L0_ffn_expert_b, L1_attn_proj, L1_attn_ln1_g, L1_attn_ln1_b, L1_attn_ln2_g, L1_attn_ln2_b, L1_attn_W1, L1_attn_b1, L1_attn_W2, L1_attn_b2, L1_ffn_shared_gate, L1_ffn_shared_up, L1_ffn_shared_down, L1_ffn_routed_gate, L1_ffn_routed_up, L1_ffn_routed_down, L1_ffn_router_w, L1_ffn_routing_bias):
    import jax
    import jax.numpy as jnp

    def _L0_tok_ref(inputs, embeddings, lora_a, lora_b, magnitude):
        import jax, jax.numpy as jnp
        import numpy as np
        VOCAB = 50257
        DIM = 192
        RANK = 16
        ALPHA = 32.0
        SCALING = ALPHA / RANK
        combined = embeddings + jnp.matmul(lora_a, lora_b) * SCALING
        col_norms = jnp.sqrt(jnp.sum(jnp.square(combined), axis=0, keepdims=True))
        col_norms = jnp.maximum(col_norms, 1e-08)
        dora_table = combined / col_norms * magnitude[None, :]
        return jnp.take(dora_table, inputs, axis=0)

    def _L0_attn_ref(x, ln1_w, ln1_b, ln2_w, ln2_b, decay, first, Wk_a, Wv_a, Wr_a, Wo_a, Wk_f, Wv_f, Wr_f):
        import jax, jax.numpy as jnp
        import numpy as np
        EPS = 1e-05
        B, T, C = (8, 512, 192)
        H = 4 * C
        LAYER_ID, N_LAYER = (4, 12)

        def _ln(x, w, b):
            mu = x.mean(-1, keepdims=True)
            var = ((x - mu) ** 2).mean(-1, keepdims=True)
            return (x - mu) / jnp.sqrt(var + EPS) * w + b

        def _wkv_scan(w, k, v):
            a0 = jnp.zeros(k.shape[1:], k.dtype)
            b0 = jnp.zeros_like(a0)
            m0 = jnp.full_like(a0, -1e+38)

            def step(carry, kv):
                a, b, m = carry
                kt, vt = kv
                mm = jnp.maximum(m + w, kt)
                e1 = jnp.exp(m + w - mm)
                e2 = jnp.exp(kt - mm)
                return ((e1 * a + e2 * vt, e1 * b + e2, mm), (a, b, m))
            _, (A, Bd, M) = jax.lax.scan(step, (a0, b0, m0), (k, v))
            return (A, Bd, M)

        def bi_wkv(w, u, k, v):
            kt = jnp.swapaxes(k, 0, 1)
            vt = jnp.swapaxes(v, 0, 1)
            af, bf, mf = _wkv_scan(w, kt, vt)
            ab, bb, mb = _wkv_scan(w, kt[::-1], vt[::-1])
            ab, bb, mb = (ab[::-1], bb[::-1], mb[::-1])
            kk = kt + u
            M = jnp.maximum(jnp.maximum(mf, mb), kk)
            ef = jnp.exp(mf - M)
            eb = jnp.exp(mb - M)
            ec = jnp.exp(kk - M)
            y = (ef * af + eb * ab + ec * vt) / (ef * bf + eb * bb + ec)
            return jnp.swapaxes(y, 0, 1)
        Bn, Tn, Cn = x.shape
        h = _ln(x, ln1_w, ln1_b)
        k = h @ Wk_a.T
        v = h @ Wv_a.T
        sr = jax.nn.sigmoid(h @ Wr_a.T)
        y = bi_wkv(decay / Tn, first / Tn, k, v)
        x = x + sr * y @ Wo_a.T
        h = _ln(x, ln2_w, ln2_b)
        kf = jnp.square(jax.nn.relu(h @ Wk_f.T))
        x = x + jax.nn.sigmoid(h @ Wr_f.T) * (kf @ Wv_f.T)
        return x

    def _L0_ffn_ref(x, router_w, router_b, expert_w, expert_b):
        import jax, jax.numpy as jnp
        import numpy as np
        B, S, H = (4, 2048, 192)
        E, K = (8, 2)
        scores = jnp.einsum('bsh,eh->bse', x, router_w) + router_b
        probs = jax.nn.softmax(scores, axis=-1)
        top_probs, expert_ids = jax.lax.top_k(probs, K)
        y = jnp.einsum('bsh,edh->bsed', x, expert_w) + expert_b
        out_k = jnp.take_along_axis(y, expert_ids[..., None], axis=2)
        w = top_probs / (jnp.sum(top_probs, axis=-1, keepdims=True) + 1e-09)
        out = jnp.einsum('bsk,bskh->bsh', w, out_k)
        return out

    def _L1_attn_ref(x, proj, ln1_g, ln1_b, ln2_g, ln2_b, W1, b1, W2, b2):
        import jax, jax.numpy as jnp
        import numpy as np
        EPS = 0.0001
        LN_EPS = 1e-05

        def _layernorm(x, g, b):
            m = jnp.mean(x, axis=-1, keepdims=True)
            v = jnp.mean(jnp.square(x - m), axis=-1, keepdims=True)
            return (x - m) * jax.lax.rsqrt(v + LN_EPS) * g + b

        def _softmax_features(x, proj, is_query):
            d = x.shape[-1]
            xn = x * d ** (-0.25)
            u = jnp.einsum('bhnd,md->bhnm', xn, proj)
            diag = 0.5 * jnp.sum(jnp.square(xn), axis=-1, keepdims=True)
            if is_query:
                stab = jnp.max(u, axis=-1, keepdims=True)
            else:
                stab = jnp.max(u, axis=(-2, -1), keepdims=True)
            ratio = proj.shape[0] ** (-0.5)
            return ratio * (jnp.exp(u - diag - stab) + EPS)
        B, N, E = x.shape
        M, Dh = proj.shape
        H = E // Dh
        h = _layernorm(x, ln1_g, ln1_b)
        qkv = h.reshape(B, N, H, Dh).transpose(0, 2, 1, 3)
        q_p = _softmax_features(qkv, proj, is_query=True)
        k_p = _softmax_features(qkv, proj, is_query=False)
        k_sum = jnp.sum(k_p, axis=-2)
        d_inv = 1.0 / jnp.einsum('bhnm,bhm->bhn', q_p, k_sum)
        ctx = jnp.einsum('bhnm,bhnd->bhmd', k_p, qkv)
        attn = jnp.einsum('bhnm,bhmd,bhn->bhnd', q_p, ctx, d_inv)
        attn = attn.transpose(0, 2, 1, 3).reshape(B, N, E)
        x = x + attn
        h2 = _layernorm(x, ln2_g, ln2_b)
        h2 = jax.nn.gelu(h2 @ W1 + b1, approximate=False) @ W2 + b2
        return x + h2

    def _L1_ffn_ref(x, shared_gate, shared_up, shared_down, routed_gate, routed_up, routed_down, router_w, routing_bias):
        import jax, jax.numpy as jnp
        import numpy as np
        B, S, H, I = (4, 512, 192, 384)
        E, K = (3, 2)
        INIT = 0.02

        def _expert(x, gw, uw, dw):
            return jax.nn.silu(x @ gw) * (x @ uw) @ dw
        shared_out = _expert(x, shared_gate, shared_up, shared_down)
        routing_probs = jax.nn.sigmoid(x @ router_w + routing_bias)
        scores, indices = jax.lax.top_k(routing_probs, K)
        scores = scores / scores.sum(axis=-1, keepdims=True)
        combine_w = (jax.nn.one_hot(indices, E, dtype=x.dtype) * scores[..., None]).sum(axis=-2)
        g = jnp.einsum('bsh,ehi->ebsi', x, routed_gate)
        u = jnp.einsum('bsh,ehi->ebsi', x, routed_up)
        h = jax.nn.silu(g) * u
        out_e = jnp.einsum('ebsi,eih->ebsh', h, routed_down)
        combined = jnp.einsum('ebsh,bse->bsh', out_e, combine_w)
        return shared_out + combined
    h = _L0_tok_ref(x, L0_tok_embeddings, L0_tok_lora_a, L0_tok_lora_b, L0_tok_magnitude)
    h = h + _L0_attn_ref(_layernorm(h, axis=-1), L0_attn_ln1_w, L0_attn_ln1_b, L0_attn_ln2_w, L0_attn_ln2_b, L0_attn_decay, L0_attn_first, L0_attn_Wk_a, L0_attn_Wv_a, L0_attn_Wr_a, L0_attn_Wo_a, L0_attn_Wk_f, L0_attn_Wv_f, L0_attn_Wr_f)
    h = h + _L0_ffn_ref(_layernorm(h, axis=-1), L0_ffn_router_w, L0_ffn_router_b, L0_ffn_expert_w, L0_ffn_expert_b)
    h = h + _L1_attn_ref(_layernorm(h, axis=-1), L1_attn_proj, L1_attn_ln1_g, L1_attn_ln1_b, L1_attn_ln2_g, L1_attn_ln2_b, L1_attn_W1, L1_attn_b1, L1_attn_W2, L1_attn_b2)
    h = h + _L1_ffn_ref(_layernorm(h, axis=-1), L1_ffn_shared_gate, L1_ffn_shared_up, L1_ffn_shared_down, L1_ffn_routed_gate, L1_ffn_routed_up, L1_ffn_routed_down, L1_ffn_router_w, L1_ffn_routing_bias)
    return h

_drawn_inputs = setup_inputs


def setup_inputs(seed=0):
    import zlib

    import numpy as np

    out = dict(_drawn_inputs(seed))
    spreads = {'L0_tok_magnitude': (1.0, 0.2),
     'L0_attn_ln1_w': (1.0, 0.6),
     'L0_attn_ln1_b': (0.0, 0.297),
     'L0_attn_ln2_w': (1.0, 0.2),
     'L0_attn_ln2_b': (0.0, 0.31),
     'L1_attn_ln1_g': (1.0, 0.2),
     'L1_attn_ln1_b': (0.0, 0.1),
     'L1_attn_ln2_g': (1.0, 0.6),
     'L1_attn_ln2_b': (0.0, 0.8),
     'L1_attn_b1': (0.0, 0.573),
     'L1_attn_b2': (0.0, 0.1),
     'L1_ffn_routing_bias': (0.0, 0.8)}
    factors = {'L0_attn_decay': 4.146,
     'L0_attn_first': 8.0,
     'L0_attn_Wk_a': 4.359,
     'L0_attn_Wr_a': 6.927,
     'L1_ffn_shared_gate': 7.74,
     'L1_ffn_shared_up': 7.662,
     'L1_ffn_shared_down': 7.677,
     'L1_ffn_routed_gate': 8.0,
     'L1_ffn_routed_up': 8.0,
     'L1_ffn_routed_down': 8.0,
     'L1_ffn_router_w': 8.0}
    for name, (base, spread) in spreads.items():
        noise = np.random.default_rng([zlib.crc32(name.encode()), seed]).standard_normal(out[name].shape)
        drawn = base * np.exp(spread * noise) if base else spread * noise
        out[name] = jnp.asarray(drawn.astype(out[name].dtype))
    for name, factor in factors.items():
        out[name] = (out[name] * factor).astype(out[name].dtype)
    return out
```

```python
from contextlib import ExitStack

import concourse.bass as bass
from concourse import mybir

F32 = mybir.dt.float32
I32 = mybir.dt.int32
U32 = mybir.dt.uint32
ALU = mybir.AluOpType
ACT = mybir.ActivationFunctionType
AX = mybir.AxisListType

P = 128
UNIT = 128
STREAMS = 2
TILES = 4
CHUNK = TILES * P
NEG = -1e38
LN_EPS = 1e-5
FEAT_EPS = 1e-4


def lm_tower(nc, a, out):
    V, C = a["embeddings"].shape
    RANK = a["lora_a"].shape[1]
    TOKENS = out.shape[0]
    SEQ = a["SEQ"]
    PASSES = TOKENS // (STREAMS * CHUNK)
    LORA_SCALE = 32.0 / RANK
    FF = a["WkfT"].shape[1]
    FT = FF // P
    E0 = a["router0T"].shape[1]
    MF, DH = a["proj_shape"]
    HEADS = C // DH
    HK0 = P // DH
    E1 = a["router1"].shape[1]
    I1 = a["gate_up"].shape[1] // (2 * (E1 + 1))
    IT = I1 // P
    C1 = C - P
    SEGS = CHUNK // SEQ + 1
    SEGW = SEQ + 2
    assert CHUNK == 2 * SEQ and C1 * 2 == P and FT == 6 and SEGS == 3 and 2 * MF == P

    ROWS = 14
    RING = 4
    MAIN = V // P // ROWS * ROWS
    LOADS = MAIN // ROWS
    TAIL = V - MAIN * P
    CR = C + RANK
    assert LOADS % RING == 0 and 0 < TAIL <= P

    with ExitStack() as ctx:
        def sb(name, shape, dt=F32):
            return ctx.enter_context(nc.sbuf_tensor(name, shape, dt))

        def sem(name):
            return ctx.enter_context(nc.semaphore(name))

        class Steps:

            def __init__(self, name, per):
                self.sems, self.per, self.made = [sem(f"{name}_{s}") for s in range(STREAMS)], per, [0] * STREAMS

            def step(self, s):
                self.made[s] += 1
                return self.sems[s], (1 if self.made[s] < self.per else UNIT - self.per + 1)

            def __call__(self, s, u, k):
                return self.sems[s], u + (k + 1 if k < self.per else UNIT + 1)

            def credit(self, eng):
                for q in self.sems:
                    eng.sem_inc(q, 1)

        ident = sb("ident", [P, P])
        ones = sb("ones", [P, P])
        feat_eps = sb("feat_eps", [P, P])
        wk = sb("wk", [P, 2, C])
        wv = sb("wv", [P, 2, C])
        wr = sb("wr", [P, 2, C])
        wo = sb("wo", [P, 2, C])
        wkf = sb("wkf", [P, 2, FF])
        wvf = sb("wvf", [P, FT, C])
        wrf = sb("wrf", [P, 2, C])
        router0 = sb("router0", [P, 2, E0])
        router0_b = sb("router0_b", [1, E0])
        experts = sb("experts", [P, 2, E0 * C])
        bias_rows = sb("bias_rows", [33, C])
        experts_b, b2 = bias_rows[0:E0, :], bias_rows[32:33, :]
        projbd = sb("projbd", [P, HEADS * MF])
        w1 = sb("w1", [P, 2, FF])
        b1 = sb("b1", [P, FT])
        w2 = sb("w2", [P, FT, C])
        gate_up = sb("gate_up", [P, 2, (E1 + 1) * 2 * I1])
        down = sb("down", [P, E1 + 1, IT, C])
        router1 = sb("router1", [P, 2, E1])
        router1_b = sb("router1_b", [1, E1])
        lora_b = sb("lora_b", [RANK, C])
        ln_cols = sb("ln_cols", [P, 2, 4])
        ln2_cols = sb("ln2_cols", [P, 2, 2])
        ln1_rows = sb("ln1_rows", [P, 2, C])
        wu = sb("wu", [P, 2, 2])
        gscale = sb("gscale", [P, C])
        half = sb("half", [P, TILES])
        eps_t = sb("eps_t", [P, TILES])
        iota8 = sb("iota8", [P, E0])
        decay_row = sb("decay_row", [P, SEGS, SEGW])

        SW = SEGS * SEGW
        WSW = (3 + 2 + 4 + 2) * SW
        ws = sb("ws", [P, WSW])

        def seg(at, n=1):
            v = ws[:, at * SW:(at + n) * SW]
            return v.rearrange("p (n g t) -> p n g t", n=n, g=SEGS)

        K, KU, VV = seg(0), seg(1), seg(2)
        MAXES = [seg(3), seg(4)]
        DECAYS = [seg(5, 2), seg(7, 2)]
        SUMS = [(seg(9 + d), DECAYS[d][:, 1:2]) for d in range(2)]

        def flat(v):
            return v.rearrange("p n g t -> p (n g t)")

        def data(v):
            return v[:, :, :, 1:SEQ + 1]

        BW = TILES * HEADS * MF
        big_a = [sb(f"big_a{s}", [P, BW]) for s in range(STREAMS)]
        big_b = [sb(f"big_b{s}", [P, BW]) for s in range(STREAMS)]
        H = [sb(f"hidden{s}", [P, TILES, C]) for s in range(STREAMS)]
        XA = [sb(f"resid{s}", [P, TILES, C]) for s in range(STREAMS)]
        HV1 = DH + 1
        norm = [sb(f"norm{s}", [P, TILES * HEADS * HV1]) for s in range(STREAMS)]
        NX = [n[:, 0:TILES * C].rearrange("p (t c) -> p t c", t=TILES) for n in norm]
        CV = [n[:].rearrange("p (q e) -> p q e", e=HV1) for n in norm]
        HV = [sb(f"heads{s}", [P, TILES * HEADS, HV1]) for s in range(STREAMS)]
        hT = [sb(f"hT{s}", [P, 2, CHUNK]) for s in range(STREAMS)]
        idx = [sb(f"idx{s}", [P, TILES], I32) for s in range(STREAMS)]
        grow = XA
        glora = [sb(f"glora{s}", [P, TILES, RANK]) for s in range(STREAMS)]
        stats = [sb(f"stats{s}", [P, TILES, 6]) for s in range(STREAMS)]
        mv = [sb(f"mv{s}", [P, TILES, 2]) for s in range(STREAMS)]
        rstd = [sb(f"rstd{s}", [P, 4, TILES]) for s in range(STREAMS)]
        small = [sb(f"small{s}", [P, 10, TILES * E0]) for s in range(STREAMS)]
        idx8 = [sb(f"idx8{s}", [P, TILES, 8], U32) for s in range(STREAMS)]
        wT = [n[0:E0, 0:CHUNK] for n in norm]
        stab = [sb(f"stab{s}", [P, 4, TILES * HEADS]) for s in range(STREAMS)]
        stabT = [sb(f"stabT{s}", [HEADS, 2, 1 + HEADS]) for s in range(STREAMS)]
        CTX = [sb(f"ctx{s}", [P, 2, HEADS // 2, 2 * HV1]) for s in range(STREAMS)]

        PS = [ctx.enter_context(nc.psum_tensor(f"ps{s}", [P, 4, 512], F32)) for s in range(STREAMS)]

        loaded, ident_in, mag_in = sem("weights_loaded"), sem("ident_in"), sem("mag_in")
        proj_set = sem("proj_set")
        const_pool = sem("const_pool")
        const_dve = sem("const_dve")
        const_act = sem("const_act")
        table_in = [sem(f"table_in{b}") for b in range(RING)]
        table_mm = sem("table_mm")
        table_sq = sem("table_sq")
        table_add = sem("table_add")
        norm_pe = sem("norm_pe")
        norm_dve = sem("norm_dve")
        norm_act = sem("norm_act")
        held = sem("held")
        stored = [sem(f"stored{s}") for s in range(STREAMS)]
        idx_in = [sem(f"idx_in{s}") for s in range(STREAMS)]
        row_in = [sem(f"row_in{s}") for s in range(STREAMS)]

        embed_pe = Steps("embed_pe", 2)
        embed_act = Steps("embed_act", 1)
        ln0_dve, ln0_pool = Steps("ln0_dve", 7), Steps("ln0_pool", 5)
        tr = Steps("tr_pe", 6)
        ev = Steps("tr_act", 6)
        kv_pe, kv_act = Steps("kv_pe", 2), Steps("kv_act", 3)
        wkv_dve, wkv_act = Steps("wkv_dve", 26), Steps("wkv_act", 3)
        out_pe, out_dve = Steps("out_pe", 1), Steps("out_dve", 1)
        hadd = Steps("hidden_pool", 2)
        ln_dve, ln_pool = Steps("ln_dve", 4 * 4), Steps("ln_pool", 4)
        ff_pe, ff_act, ff_dve = Steps("ff_pe", 1 + FT + 1), Steps("ff_act", 1 + 2 * FT), Steps("ff_dve", 2)
        moe_pe, moe_dve, moe_act = Steps("moe_pe", 2 + 16 + 1), Steps("moe_dve", 15), Steps("moe_act", 1)
        mix = Steps("mix_dve", 2 * 16 + 1)
        ln3_dve, ln3_pool = Steps("ln3_dve", 8), Steps("ln3_pool", 5)
        feat_act, feat_pe, feat_dve = Steps("feat_act", 1 + TILES), Steps("feat_pe", TILES), Steps("feat_dve", 1 + 3 * TILES)
        stab_pe, stab_dve, stab_act = Steps("stab_pe", 2), Steps("stab_dve", 4), Steps("stab_act", 1)
        ctx_pe, ctx_dve = Steps("ctx_pe", 1), Steps("ctx_dve", 1)
        et_pe, et_act = Steps("et_pe", FT), Steps("et_act", FT)
        attn_pe, attn_dve = Steps("attn_pe", 1), Steps("attn_dve", 3)
        mlp_pe, mlp_act, mlp_dve = Steps("mlp_pe", FT + 1), Steps("mlp_act", FT), Steps("mlp_dve", 1)
        rt_pe, rt_act, rt_dve = Steps("rt_pe", 1), Steps("rt_act", 1), Steps("rt_dve", 8)
        NX1 = E1 + 1
        ex_pe, ex_act, ex_dve = Steps("ex_pe", NX1 * (2 * IT + 1)), Steps("ex_act", NX1 * IT), Steps("ex_dve", NX1 * (IT + 1))

        block = ctx.enter_context(nc.Block())

        tab = [b[:, 0:ROWS * CR].rearrange("p (j c) -> p j c", c=CR) for b in (big_a[0], big_b[0], big_a[1], big_b[1])]
        NSQ = ROWS * C
        squares = [ws[:, 0:NSQ], ws[:, NSQ:2 * NSQ]]
        sqsum = ws[:, 2 * NSQ:3 * NSQ]
        emb_main = a["embeddings"][0:MAIN * P, :].rearrange("(p n j) d -> n p j d", p=P, j=ROWS)
        lora_main = a["lora_a"][0:MAIN * P, :].rearrange("(p n j) d -> n p j d", p=P, j=ROWS)
        gram = PS[0][0:RANK, 0, 0:CR]
        gram_sb = small[0][0:RANK, :, :].rearrange("p a b -> p (a b)")[:, 0:CR]
        cross = big_a[0][0:RANK, 0:C]
        colsum = big_a[1][:, 0:C]
        colmag = big_a[1][:, C:2 * C]

        both = [
            (wk, "WkT"), (wv, "WvT"), (wr, "WrT"), (wo, "WoT"), (wkf, "WkfT"), (wrf, "WrfT"), (router0, "router0T"),
            (experts, "experts"), (w1, "W1"), (gate_up, "gate_up"), (router1, "router1"), (ln_cols, "ln_cols"),
            (ln2_cols, "ln2_cols"), (wu, "wu"),
        ]
        loads = [(t[0:P, 0, :], a[n][0:P, :]) for t, n in both] + [(t[0:C1, 1, :], a[n][P:C, :]) for t, n in both]
        loads += [
            (wo[C1:P, 1, :], a["WoT"][P:C, :]), (wu[C1:P, 1, :], a["wu"][P:C, :]),
            (wvf[:], a["WvfT"].rearrange("(j p) c -> p j c", p=P)),
            (w2[:], a["W2"].rearrange("(j p) c -> p j c", p=P)),
            (down[:], a["down"].rearrange("x (j p) c -> p x j c", p=P)),
            (router0_b[:], a["router0_b"]), (experts_b, a["experts_b"]), (b1[:], a["b1"]), (b2, a["b2"]),
            (router1_b[:], a["router1_b"]), (lora_b[:], a["lora_b"]), (iota8[:], a["iota8"].broadcast_to([P, E0])),
            (ln1_rows[:, 0, :], a["ln1_g"].broadcast_to([P, C])), (ln1_rows[:, 1, :], a["ln1_b"].broadcast_to([P, C])),
        ]
        NORM_STEPS = 12 + SEGS

        @block.sync
        def _(sp):
            sp.dma_start(ident[:], a["ident"]).then_inc(ident_in, 16)
            with sp.Fori(0, LOADS // RING) as it:
                for b in range(RING):
                    sp.wait_ge(table_mm, it * RING + (b + 1))
                    sp.wait_ge(table_sq, it * RING + (b + 1))
                    sp.dma_start(tab[b][:, :, 0:C], emb_main[it * RING + b]).then_inc(table_in[b], 16)
                    sp.dma_start(tab[b][:, :, C:CR], lora_main[it * RING + b]).then_inc(table_in[b], 16)
            sp.wait_ge(table_mm, LOADS + 1)
            sp.wait_ge(table_sq, LOADS + 1)
            sp.dma_start(tab[0][0:TAIL, 0, 0:C], a["embeddings"][MAIN * P:V, :]).then_inc(table_in[0], 16)
            sp.dma_start(tab[0][0:TAIL, 0, C:CR], a["lora_a"][MAIN * P:V, :]).then_inc(table_in[0], 16)

            for s in range(STREAMS):
                sp.sem_inc(idx_in[s], 1)
                sp.sem_inc(stored[s], 1)
            with sp.Fori(0, PASSES) as it:
                for s in range(STREAMS):
                    sp.wait_ge(*embed_pe(s, it * UNIT, 0))
                    sp.dma_start(idx[s][:], a["idx"][it * STREAMS + s]).then_inc(idx_in[s], UNIT)
                for s in range(STREAMS):
                    sp.wait_ge(*ex_dve(s, it * UNIT, NX1 * (IT + 1)))
                    sp.dma_start(out.rearrange("(n t p) c -> n p t c", p=P, t=TILES)[it * STREAMS + s],
                                 H[s][:]).then_inc(stored[s], UNIT)
            for s in range(STREAMS):
                sp.wait_ge(stored[s], UNIT * PASSES + 1)

        @block.gpsimd
        def _(pool):
            def hold(q, value):
                pool.wait_ge(q, value)
                pool.sem_inc(held, 1)

            nc.gpsimd.memset(projbd[:], 0.0).then_inc(const_pool, 1)
            nc.gpsimd.memset(ones[:], 1.0).then_inc(const_pool, 1)
            nc.gpsimd.memset(feat_eps[:], FEAT_EPS).then_inc(const_pool, 1)
            nc.gpsimd.memset(half[:], -0.5).then_inc(const_pool, 1)
            nc.gpsimd.memset(eps_t[:], LN_EPS).then_inc(const_pool, 1)
            for s in range(STREAMS):
                nc.gpsimd.memset(HV[s][:], 1.0).then_inc(const_pool, 1)
                nc.gpsimd.memset(CTX[s][:], 0.0).then_inc(const_pool, 1)
            pool.wait_ge(const_pool, 1)
            for h in range(HEADS):
                r, c = (h * DH, h * MF) if h < HK0 else ((h - HK0) * DH, h * MF)
                pool.dma_start(projbd[r:r + DH, c:c + MF], a["projT"]).then_inc(proj_set, 16)
            for dst, src in loads:
                pool.dma_start(dst, src).then_inc(loaded, 16)
            pool.wait_ge(norm_dve, 1)
            pool.dma_start(colmag, a["magnitude"].broadcast_to([P, C])).then_inc(mag_in, 16)

            for f in (ln0_pool, hadd, ln_pool, ln3_pool):
                f.credit(pool)

            def power(s, i_out, in0, q):
                nc.gpsimd.tensor_tensor(rstd[s][:, i_out, :], in0, half[:], ALU.pow).then_inc(*q)

            with pool.Fori(0, PASSES * UNIT, UNIT) as it:
                for s in range(STREAMS):
                    hold(idx_in[s], it + (UNIT + 1))
                    hold(*ln_dve(s, it, 0))
                    hold(*hadd(s, it, 0))
                    hold(*embed_pe(s, it, 0))
                    for t in range(TILES):
                        off = bass.IndirectOffsetOnAxis(idx[s][:, t:t + 1], 0)
                        pool.indirect_dma_start(out=grow[s][:, t, :], out_offset=None, in_=a["embeddings"],
                                                in_offset=off).then_inc(row_in[s], 16)
                        pool.indirect_dma_start(out=glora[s][:, t, :], out_offset=None, in_=a["lora_a"],
                                                in_offset=off).then_inc(row_in[s], 16)

                def ln_twice(f_dve, f_pool, k_dve):
                    for s in range(STREAMS):
                        pool.wait_ge(*f_dve(s, it, k_dve))
                        power(s, 0, rstd[s][:, 3, :], f_pool.step(s))
                        pool.wait_ge(*f_pool(s, it, 1))
                        nc.gpsimd.tensor_tensor(rstd[s][:, 1, :], rstd[s][:, 0, :], rstd[s][:, 0, :], ALU.mult).then_inc(*f_pool.step(s))
                        pool.wait_ge(*f_pool(s, it, 2))
                        nc.gpsimd.tensor_tensor(rstd[s][:, 1, :], rstd[s][:, 1, :], mv[s][:, :, 1], ALU.mult).then_inc(*f_pool.step(s))
                        pool.wait_ge(*f_pool(s, it, 3))
                        nc.gpsimd.tensor_tensor(rstd[s][:, 1, :], rstd[s][:, 1, :], eps_t[:], ALU.add).then_inc(*f_pool.step(s))
                        pool.wait_ge(*f_pool(s, it, 4))
                        power(s, 2, rstd[s][:, 1, :], f_pool.step(s))

                def ln_once(i):
                    for s in range(STREAMS):
                        pool.wait_ge(*ln_dve(s, it, 4 * i + 3))
                        power(s, 0, rstd[s][:, 3, :], ln_pool.step(s))

                def add_resid(f, k, i):
                    for s in range(STREAMS):
                        pool.wait_ge(*f(s, it, k))
                        nc.gpsimd.tensor_tensor(H[s][:], H[s][:], XA[s][:], ALU.add).then_inc(*hadd.step(s))

                ln_twice(ln0_dve, ln0_pool, 5)
                add_resid(out_dve, 1, 0)
                ln_once(0)
                ln_once(1)
                ln_twice(ln3_dve, ln3_pool, 3)
                add_resid(attn_dve, 3, 1)
                ln_once(2)
                ln_once(3)

        @block.scalar
        def _(act):
            for f in (embed_act, ev, kv_act, wkv_act, ff_act, moe_act, feat_act, stab_act, et_act, mlp_act, rt_act, ex_act):
                f.credit(act)
            act.sem_inc(table_sq, RING)

            with act.Fori(0, LOADS // RING) as it:
                for b in range(RING):
                    act.wait_ge(table_in[b], it * 32 + 32)
                    act.wait_ge(table_add, it * RING + (b + 1))
                    nc.scalar.activation(squares[b % 2].rearrange("p (j c) -> p j c", c=C), tab[b][:, :, 0:C],
                                         ACT.Square).then_inc(table_sq, 1)
            act.wait_ge(table_in[0], LOADS // RING * 32 + 32)
            act.wait_ge(table_add, LOADS + 1)
            nc.scalar.activation(squares[0][0:TAIL, 0:C], tab[0][0:TAIL, 0, 0:C], ACT.Square).then_inc(table_sq, 1)
            act.wait_ge(table_mm, RING + LOADS + 1)
            nc.scalar.activation(gram_sb, gram, ACT.Copy).then_inc(norm_act, 1)
            act.wait_ge(norm_pe, 2)
            nc.scalar.activation(colsum, PS[0][:, 2, 0:C], ACT.Sqrt).then_inc(norm_act, 1)
            def copy_back(i, scale=None, shift=None):
                banks = (3, 0) if i == 0 else (0, 1)
                for s in range(STREAMS):
                    act.wait_ge(*tr(s, it, i + 1))
                    for k, rows in ((0, P), (1, C1)):
                        src, dst = PS[s][0:rows, banks[k], :], hT[s][0:rows, k, :]
                        if scale is None:
                            last = nc.scalar.activation(dst, src, ACT.Copy)
                        else:
                            last = nc.scalar.activation(dst, src, ACT.Identity, bias=shift(k)[0:rows, :], scale=scale(k)[0:rows, :])
                    last.then_inc(*ev.step(s))

            act.wait_ge(loaded, 16 * len(loads))
            act.wait_ge(norm_dve, NORM_STEPS)
            with act.Fori(0, PASSES * UNIT, UNIT) as it:
                for s in range(STREAMS):
                    act.wait_ge(*embed_pe(s, it, 1))
                    nc.scalar.activation(big_a[s][0:RANK, 0:CHUNK], PS[s][0:RANK, 0, :], ACT.Copy).then_inc(*embed_act.step(s))
                copy_back(0, lambda k: ln_cols[:, k, 0:1], lambda k: ln_cols[:, k, 1:2])

                for s in range(STREAMS):
                    act.wait_ge(*kv_pe(s, it, 1))
                    if s == 0:
                        act.wait_ge(*wkv_dve(1, it, 0))
                    else:
                        act.wait_ge(*wkv_dve(0, it, 26))
                    for g, src in ((slice(0, 2), PS[s][:, 1, :]), (slice(2, 3), PS[s][:, 2, 0:SEQ])):
                        src = src.rearrange("p (g t) -> p g t", t=SEQ)
                        nc.scalar.activation(data(K)[:, 0, g, :], src, ACT.Copy)
                        col = 0 if g.start == 0 else 1
                        last = nc.scalar.activation(data(KU)[:, 0, g, :], src, ACT.Identity, bias=wu[:, col, 1:2])
                    last.then_inc(*kv_act.step(s))
                    for g, src in ((slice(0, 2), PS[s][:, 3, :]), (slice(2, 3), PS[s][:, 2, SEQ:2 * SEQ])):
                        last = nc.scalar.activation(data(VV)[:, 0, g, :], src.rearrange("p (g t) -> p g t", t=SEQ), ACT.Copy)
                    last.then_inc(*kv_act.step(s))
                    act.wait_ge(*kv_pe(s, it, 2))
                    er = hT[s][:].rearrange("p a b -> p (a b)")
                    nc.scalar.activation(er[:, 0:CHUNK], PS[s][:, 0, :], ACT.Exp, scale=-1.0)
                    nc.scalar.activation(er[:, CHUNK:CHUNK + SEQ], PS[s][:, 1, 0:SEQ], ACT.Exp, scale=-1.0).then_inc(*kv_act.step(s))
                    for d in range(2):
                        act.wait_ge(*wkv_dve(s, it, 4 + 2 * d))
                        v = data(DECAYS[d]).rearrange("p n g t -> p (n g) t")
                        nc.scalar.activation(v, v, ACT.Exp).then_inc(*wkv_act.step(s))
                    act.wait_ge(*wkv_dve(s, it, 11))
                    v = big_a[s][:, 0:3 * SEGS * SEQ]
                    nc.scalar.activation(v, v, ACT.Exp).then_inc(*wkv_act.step(s))

                copy_back(1, lambda k: ln_cols[:, k, 2:3], lambda k: ln_cols[:, k, 3:4])

                for s in range(STREAMS):
                    act.wait_ge(*ff_pe(s, it, 1))
                    nc.scalar.activation(NX[s].rearrange("p (b t) c -> p b (t c)", b=2), PS[s][:, 2:4, 0:2 * C], ACT.Sigmoid).then_inc(*ff_act.step(s))
                    for j in range(FT):
                        act.wait_ge(*ff_pe(s, it, 2 + j))
                        v = big_a[s][:, j * CHUNK:(j + 1) * CHUNK]
                        nc.scalar.activation(v, PS[s][:, j % 2, :], ACT.Relu).then_inc(*ff_act.step(s))
                        act.wait_ge(*ff_act(s, it, 2 + 2 * j))
                        nc.scalar.activation(v, v, ACT.Square).then_inc(*ff_act.step(s))

                copy_back(2)
                for s in range(STREAMS):
                    act.wait_ge(*moe_dve(s, it, 4))
                    nc.scalar.activation(small[s][:, 3, :], small[s][:, 2, :], ACT.Exp).then_inc(*moe_act.step(s))

                copy_back(3)
                for s in range(STREAMS):
                    nc.scalar.activation(NX[s].rearrange("p t (h d) -> p (t h) d", d=DH), HV[s][:, :, 0:DH], ACT.Square, scale=0.5).then_inc(*feat_act.step(s))
                for t in range(TILES):
                    for s in range(STREAMS):
                        act.wait_ge(*feat_dve(s, it, 1 + 3 * (t + 1)))
                        v = big_a[s][:, t * HEADS * MF:(t + 1) * HEADS * MF]
                        nc.scalar.activation(v, v, ACT.Exp).then_inc(*feat_act.step(s))
                for s in range(STREAMS):
                    act.wait_ge(*stab_dve(s, it, 3))
                    nc.scalar.activation(stab[s][:, 2, :], stab[s][:, 2, :], ACT.Exp).then_inc(*stab_act.step(s))
                for s in range(STREAMS):
                    for j in range(FT):
                        act.wait_ge(*et_pe(s, it, j + 1))
                        nc.scalar.activation(big_b[s][:, j * CHUNK:(j + 1) * CHUNK], PS[s][:, j % 2, :], ACT.Copy, bias=FEAT_EPS).then_inc(*et_act.step(s))

                copy_back(4, lambda k: ln2_cols[:, k, 0:1], lambda k: ln2_cols[:, k, 1:2])
                for s in range(STREAMS):
                    for j in range(FT):
                        act.wait_ge(*mlp_pe(s, it, j + 1))
                        nc.scalar.activation(big_a[s][:, j * CHUNK:(j + 1) * CHUNK], PS[s][:, j % 2, :], ACT.Gelu, bias=b1[:, j:j + 1]).then_inc(*mlp_act.step(s))

                copy_back(5)
                for s in range(STREAMS):
                    act.wait_ge(*rt_pe(s, it, 1))
                    nc.scalar.activation(small[s][:, 0, 0:TILES * E1], PS[s][:, 2, 0:TILES * E1], ACT.Sigmoid).then_inc(*rt_act.step(s))
                for x in range(NX1):
                    for s in range(STREAMS):
                        for j in range(IT):
                            act.wait_ge(*ex_pe(s, it, x * (2 * IT + 1) + 2 * j + 1))
                            if x > 0:
                                act.wait_ge(*ex_dve(s, it, (x - 1) * (IT + 1) + j + 1))
                            nc.scalar.activation(big_a[s][:, j * CHUNK:(j + 1) * CHUNK], PS[s][:, 0, :], ACT.Silu).then_inc(*ex_act.step(s))

        @block.vector
        def _(dve):
            def hold(q, value):
                dve.wait_ge(q, value)
                dve.sem_inc(held, 1)

            for f in (ln0_dve, wkv_dve, out_dve, ln_dve, ff_dve, moe_dve, mix, ln3_dve, feat_dve, stab_dve, ctx_dve, attn_dve, mlp_dve, rt_dve, ex_dve):
                f.credit(dve)
            dve.sem_inc(table_add, 2)
            nc.vector.memset(sqsum, 0.0).then_inc(const_dve, 1)
            dve.wait_ge(const_dve, 1)
            with dve.Fori(0, LOADS // RING) as it:
                for b in range(RING):
                    dve.wait_ge(table_sq, it * RING + (RING + b + 1))
                    dve.wait_ge(table_add, it * RING + (b + 2))
                    nc.vector.tensor_tensor(sqsum, sqsum, squares[b % 2], ALU.add).then_inc(table_add, 1)
            dve.wait_ge(table_sq, RING + LOADS + 1)
            dve.wait_ge(table_add, LOADS + 2)
            nc.vector.tensor_tensor(sqsum[0:TAIL, 0:C], sqsum[0:TAIL, 0:C], squares[0][0:TAIL, 0:C], ALU.add).then_inc(table_add, 1)
            dve.wait_ge(table_add, LOADS + 3)
            dve.wait_ge(table_mm, RING + LOADS + 1)
            nc.vector.tensor_reduce(colsum, sqsum.rearrange("p (j c) -> p c j", c=C), AX.X, ALU.add).then_inc(norm_dve, 1)
            dve.wait_ge(loaded, 16 * len(loads))
            dve.wait_ge(norm_act, 1)
            dve.wait_ge(norm_pe, 1)
            nc.vector.tensor_scalar(cross, gram_sb[:, 0:C], 2.0 / LORA_SCALE, None, ALU.mult).then_inc(norm_dve, 1)
            dve.wait_ge(norm_dve, 2)
            nc.vector.tensor_tensor(cross, cross, PS[0][0:RANK, 1, 0:C], ALU.add).then_inc(norm_dve, 1)
            dve.wait_ge(norm_dve, 3)
            nc.vector.scalar_tensor_tensor(out=cross, in0=cross, scalar=LORA_SCALE * LORA_SCALE, in1=lora_b[:], op0=ALU.mult, op1=ALU.mult).then_inc(norm_dve, 1)
            dve.wait_ge(norm_dve, 4)
            nc.vector.tensor_scalar(lora_b[:], lora_b[:], LORA_SCALE, None, ALU.mult).then_inc(const_dve, 1)
            dve.wait_ge(norm_act, 2)
            nc.vector.tensor_scalar(colsum, colsum, 1e-8, None, ALU.max).then_inc(norm_dve, 1)
            dve.wait_ge(norm_dve, 5)
            nc.vector.reciprocal(colsum, colsum).then_inc(norm_dve, 1)
            dve.wait_ge(norm_dve, 6)
            dve.wait_ge(mag_in, 16)
            nc.vector.tensor_tensor(gscale[:], colsum, colmag, ALU.mult).then_inc(norm_dve, 1)
            nc.vector.memset(ws[:], 0.0).then_inc(norm_dve, 1)
            nc.vector.memset(decay_row[:], 2 * NEG).then_inc(norm_dve, 1)
            nc.vector.tensor_scalar(wu[:], wu[:], 1.0 / SEQ, None, ALU.mult).then_inc(norm_dve, 1)
            dve.wait_ge(proj_set, 16 * HEADS)
            nc.vector.tensor_scalar(projbd[:], projbd[:], float(DH) ** -0.25, None, ALU.mult).then_inc(const_dve, 1)
            dve.wait_ge(norm_dve, 10)
            for edge in (0, SEGW - 1):
                nc.vector.memset(K[:, 0, :, edge], NEG).then_inc(norm_dve, 1)
            for g in range(SEGS):
                nc.vector.tensor_scalar(decay_row[:, g, 1:SEQ + 1], VV[:, 0, g, 1:SEQ + 1], wu[:, g // 2, 0:1], None, ALU.add).then_inc(norm_dve, 1)
            dve.wait_ge(norm_dve, NORM_STEPS)
            dve.wait_ge(const_dve, 3)

            def ln_stats(f, s, it, k, x):
                for t in range(TILES):
                    last = nc.vector.bn_stats(stats[s][:, t, :], x[:, t, :])
                last.then_inc(*f.step(s))
                hold(*f(s, it, k + 1))
                for t in range(TILES):
                    last = nc.vector.bn_aggr(mv[s][:, t, :], stats[s][:, t, :])
                last.then_inc(*f.step(s))
                dve.wait_ge(*f(s, it, k + 2))
                nc.vector.tensor_scalar(rstd[s][:, 3, :], mv[s][:, :, 1], LN_EPS, None, ALU.add).then_inc(*f.step(s))

            def apply(dst, x, s):
                for t in range(TILES):
                    last = nc.vector.tensor_scalar(dst[s][:, t, :], x[s][:, t, :], mv[s][:, t, 0:1], rstd[s][:, 0, t:t + 1], ALU.subtract, ALU.mult)
                return last

            with dve.Fori(0, PASSES * UNIT, UNIT) as it:
                for s in range(STREAMS):
                    dve.wait_ge(row_in[s], it + UNIT)
                    dve.wait_ge(*embed_pe(s, it, 2))
                    dve.wait_ge(stored[s], it + 1)
                    nc.vector.tensor_tensor(H[s][:].rearrange("p (b t) c -> p b (t c)", b=2), grow[s][:].rearrange("p (b t) c -> p b (t c)", b=2),
                                            PS[s][:, 1:3, 0:2 * C], ALU.add).then_inc(*ln0_dve.step(s))
                    dve.wait_ge(*ln0_dve(s, it, 1))
                    nc.vector.tensor_tensor(H[s][:], H[s][:], gscale[:].unsqueeze(1).broadcast_to([P, TILES, C]), ALU.mult).then_inc(*ln0_dve.step(s))
                    dve.wait_ge(*ln0_dve(s, it, 2))
                    ln_stats(ln0_dve, s, it, 2, H[s])
                for s in range(STREAMS):
                    dve.wait_ge(*ln0_pool(s, it, 5))
                    apply(XA, H, s).then_inc(*ln0_dve.step(s))
                    dve.wait_ge(*ln0_dve(s, it, 6))
                    dve.wait_ge(*tr(s, it, 0))
                    for t in range(TILES):
                        last = nc.vector.tensor_scalar(NX[s][:, t, :], XA[s][:, t, :], rstd[s][:, 2, t:t + 1], None, ALU.mult)
                    last.then_inc(*ln0_dve.step(s))

                for s in range(STREAMS):
                    q = wkv_dve
                    mx = big_b[s][:, 2 * SEGS * SEQ:3 * SEGS * SEQ]
                    args = big_a[s][:, 0:3 * SEGS * SEQ].rearrange("p (n g t) -> p n g t", n=3, g=SEGS)
                    mxv = mx.rearrange("p (n g t) -> p n g t", n=1, g=SEGS)
                    dve.wait_ge(*kv_act(s, it, 1))
                    nc.vector.tensor_tensor_scan(flat(MAXES[0]), decay_row[:].rearrange("p g t -> p (g t)"), flat(K), NEG, ALU.add, ALU.max).then_inc(*q.step(s))
                    nc.vector.tensor_tensor_scan(flat(MAXES[1])[:, ::-1], decay_row[:].rearrange("p g t -> p (g t)")[:, ::-1], flat(K)[:, ::-1], NEG, ALU.add, ALU.max).then_inc(*q.step(s))
                    prev = [MAXES[0][:, :, :, 0:SEQ], MAXES[1][:, :, :, 2:SEQ + 2]]
                    for d in range(2):
                        dve.wait_ge(*q(s, it, 1 + d))
                        old, new = data(DECAYS[d])[:, 0], data(DECAYS[d])[:, 1]
                        for g, col in ((slice(0, 2), 0), (slice(2, 3), 1)):
                            last = nc.vector.scalar_tensor_tensor(out=old[:, g], in0=prev[d][:, 0, g], scalar=wu[:, col, 0:1], in1=data(MAXES[d])[:, 0, g],
                                                                  op0=ALU.add, op1=ALU.subtract)
                        last.then_inc(*q.step(s))
                        nc.vector.tensor_tensor(new, data(K)[:, 0], data(MAXES[d])[:, 0], ALU.subtract).then_inc(*q.step(s))
                    nc.vector.tensor_tensor(mxv[:, 0], data(KU)[:, 0], prev[0][:, 0], ALU.max).then_inc(*q.step(s))
                    dve.wait_ge(*q(s, it, 7))
                    nc.vector.tensor_tensor(mxv[:, 0], mxv[:, 0], prev[1][:, 0], ALU.max).then_inc(*q.step(s))
                    dve.wait_ge(*q(s, it, 8))
                    for n, v in enumerate((prev[0][:, 0], prev[1][:, 0], data(KU)[:, 0])):
                        nc.vector.tensor_tensor(args[:, n], v, mxv[:, 0], ALU.subtract).then_inc(*q.step(s))
                    dve.wait_ge(*kv_act(s, it, 2))
                    for d in range(2):
                        e_old, e_new = flat(DECAYS[d][:, 0:1]), flat(DECAYS[d][:, 1:2])
                        num, den = flat(SUMS[d][0]), flat(SUMS[d][1])
                        if d:
                            e_old, e_new, num, den = e_old[:, ::-1], e_new[:, ::-1], num[:, ::-1], den[:, ::-1]
                        dve.wait_ge(*wkv_act(s, it, 1 + d))
                        nc.vector.tensor_tensor(flat(SUMS[d][0]), flat(DECAYS[d][:, 1:2]), flat(VV), ALU.mult).then_inc(*q.step(s))
                        dve.wait_ge(*q(s, it, 12 + 3 * d))
                        nc.vector.tensor_tensor_scan(den, e_old, e_new, 0.0, ALU.mult, ALU.add).then_inc(*q.step(s))
                        nc.vector.tensor_tensor_scan(num, e_old, num, 0.0, ALU.mult, ALU.add).then_inc(*q.step(s))
                    sums = [[v[:, 0, :, 2 * d:2 * d + SEQ] for v in SUMS[d]] for d in range(2)]
                    tot = big_b[s][:, 0:2 * SEGS * SEQ].rearrange("p (n g t) -> p n g t", n=2, g=SEGS)
                    oth = big_b[s][:, 2 * SEGS * SEQ:4 * SEGS * SEQ].rearrange("p (n g t) -> p n g t", n=2, g=SEGS)
                    dve.wait_ge(*wkv_act(s, it, 3))
                    dve.wait_ge(*q(s, it, 17))
                    for d, dst in enumerate((tot, oth)):
                        for n in range(2):
                            last = nc.vector.tensor_tensor(dst[:, n], sums[d][n], args[:, d], ALU.mult)
                        last.then_inc(*q.step(s))
                    dve.wait_ge(*q(s, it, 19))
                    nc.vector.tensor_tensor(big_b[s][:, 0:2 * SEGS * SEQ], big_b[s][:, 0:2 * SEGS * SEQ], big_b[s][:, 2 * SEGS * SEQ:4 * SEGS * SEQ], ALU.add).then_inc(*q.step(s))
                    dve.wait_ge(*q(s, it, 20))
                    nc.vector.tensor_tensor(oth[:, 0], args[:, 2], data(VV)[:, 0], ALU.mult).then_inc(*q.step(s))
                    nc.vector.tensor_tensor(tot[:, 1], tot[:, 1], args[:, 2], ALU.add).then_inc(*q.step(s))
                    dve.wait_ge(*q(s, it, 21))
                    nc.vector.tensor_tensor(tot[:, 0], tot[:, 0], oth[:, 0], ALU.add).then_inc(*q.step(s))
                    dve.wait_ge(*q(s, it, 22))
                    dve.wait_ge(*kv_act(s, it, 3))
                    er = hT[s][:].rearrange("p a b -> p (a b)")[:, 0:SEGS * SEQ]
                    den = big_b[s][:, SEGS * SEQ:2 * SEGS * SEQ]
                    rec = big_b[s][:, 3 * SEGS * SEQ:4 * SEGS * SEQ]
                    nc.vector.scalar_tensor_tensor(out=den, in0=er, scalar=1.0, in1=den, op0=ALU.add, op1=ALU.mult).then_inc(*q.step(s))
                    dve.wait_ge(*q(s, it, 24))
                    nc.vector.reciprocal(rec, den).then_inc(*q.step(s))
                    dve.wait_ge(*q(s, it, 25))
                    nc.vector.tensor_tensor(big_b[s][:, 0:SEGS * SEQ], big_b[s][:, 0:SEGS * SEQ], rec, ALU.mult).then_inc(*q.step(s))

                def two(v):
                    return v.rearrange("p (b t) c -> p b (t c)", b=2)

                for s in range(STREAMS):
                    dve.wait_ge(*out_pe(s, it, 1))
                    nc.vector.tensor_tensor(two(XA[s][:]), two(XA[s][:]), PS[s][:, 2:4, 0:2 * C], ALU.add).then_inc(*out_dve.step(s))
                    dve.wait_ge(*out_dve(s, it, 1))
                    ln_stats(ln_dve, s, it, 0, XA[s])
                for s in range(STREAMS):
                    dve.wait_ge(*ln_pool(s, it, 1))
                    apply(NX, XA, s).then_inc(*ln_dve.step(s))

                for s in range(STREAMS):
                    dve.wait_ge(*ff_pe(s, it, 2 + FT))
                    nc.vector.tensor_tensor(two(NX[s]), two(NX[s]), PS[s][:, 2:4, 0:2 * C], ALU.mult).then_inc(*ff_dve.step(s))
                    dve.wait_ge(*ff_dve(s, it, 1))
                    dve.wait_ge(*hadd(s, it, 1))
                    nc.vector.tensor_tensor(H[s][:], H[s][:], NX[s], ALU.add).then_inc(*ff_dve.step(s))
                    dve.wait_ge(*ff_dve(s, it, 2))
                    ln_stats(ln_dve, s, it, 4, H[s])
                for s in range(STREAMS):
                    dve.wait_ge(*ln_pool(s, it, 2))
                    apply(NX, H, s).then_inc(*ln_dve.step(s))

                for s in range(STREAMS):
                    def sm(n):
                        return small[s][:, n, :].rearrange("p (t e) -> p t e", t=TILES)

                    q = moe_dve
                    dve.wait_ge(*moe_pe(s, it, 1))
                    nc.vector.tensor_copy(small[s][:, 0, :], PS[s][:, 2, 0:TILES * E0]).then_inc(*q.step(s))
                    hold(*q(s, it, 1))
                    for t in range(TILES):
                        last = nc.vector.max(sm(1)[:, t, :], sm(0)[:, t, :])
                    last.then_inc(*q.step(s))
                    hold(*q(s, it, 2))
                    for t in range(TILES):
                        last = nc.vector.max_index(idx8[s][:, t, :], sm(1)[:, t, :], sm(0)[:, t, :])
                    last.then_inc(*q.step(s))
                    nc.vector.tensor_tensor(sm(2), sm(0), sm(1)[:, :, 0:1].broadcast_to([P, TILES, E0]), ALU.subtract).then_inc(*q.step(s))
                    dve.wait_ge(*q(s, it, 3))
                    nc.vector.tensor_copy(sm(4), idx8[s][:]).then_inc(*q.step(s))
                    dve.wait_ge(*q(s, it, 5))
                    iota = iota8[:].unsqueeze(1).broadcast_to([P, TILES, E0])
                    for n in range(2):
                        nc.vector.tensor_tensor(sm(5 + n), iota, sm(4)[:, :, n:n + 1].broadcast_to([P, TILES, E0]), ALU.is_equal).then_inc(*q.step(s))
                    dve.wait_ge(*q(s, it, 7))
                    nc.vector.tensor_tensor(sm(5), sm(5), sm(6), ALU.add).then_inc(*q.step(s))
                    dve.wait_ge(*q(s, it, 8))
                    dve.wait_ge(*moe_act(s, it, 1))
                    nc.vector.tensor_tensor(sm(5), sm(5), sm(3), ALU.mult).then_inc(*q.step(s))
                    nc.vector.tensor_reduce(small[s][:, 7, 0:TILES], sm(3), AX.X, ALU.add).then_inc(*q.step(s))
                    dve.wait_ge(*q(s, it, 9))
                    nc.vector.tensor_reduce(small[s][:, 8, 0:TILES], sm(5), AX.X, ALU.add).then_inc(*q.step(s))
                    dve.wait_ge(*q(s, it, 11))
                    nc.vector.scalar_tensor_tensor(out=small[s][:, 7, 0:TILES], in0=small[s][:, 7, 0:TILES], scalar=1e-9, in1=small[s][:, 8, 0:TILES],
                                                   op0=ALU.mult, op1=ALU.add).then_inc(*q.step(s))
                    dve.wait_ge(*q(s, it, 12))
                    nc.vector.reciprocal(small[s][:, 8, 0:TILES], small[s][:, 7, 0:TILES]).then_inc(*q.step(s))
                    dve.wait_ge(*q(s, it, 13))
                    nc.vector.tensor_tensor(sm(9), sm(5), small[s][:, 8, 0:TILES].unsqueeze(2).broadcast_to([P, TILES, E0]), ALU.mult).then_inc(*q.step(s))
                for s in range(STREAMS):
                    dve.wait_ge(*moe_pe(s, it, 2))
                    nc.vector.tensor_copy(wT[s], PS[s][0:E0, 3, :]).then_inc(*moe_dve.step(s))
                for s in range(STREAMS):
                    w = small[s][:, 9, :].rearrange("p (t e) -> p t e", t=TILES)
                    for e2 in range(E0 // 2):
                        for t in range(TILES):
                            n = e2 * TILES + t
                            dve.wait_ge(*moe_pe(s, it, 2 + n + 1))
                            for half_ in range(2):
                                if half_ or e2:
                                    dve.wait_ge(*mix(s, it, 2 * n + 1 if half_ else 2 * (n - TILES) + 2))
                                e = 2 * e2 + half_
                                ins = nc.vector.scalar_tensor_tensor(out=H[s][:, t, :], in0=PS[s][:, n % 2, half_ * C:(half_ + 1) * C], scalar=w[:, t, e:e + 1],
                                                                     in1=H[s][:, t, :], op0=ALU.mult, op1=ALU.add)
                                ins.then_inc(*mix.step(s))
                    dve.wait_ge(*moe_pe(s, it, 2 + 16 + 1))
                    dve.wait_ge(*mix(s, it, 32))
                    nc.vector.tensor_tensor(two(H[s][:]), two(H[s][:]), PS[s][:, 2:4, 0:2 * C], ALU.add).then_inc(*mix.step(s))
                    dve.wait_ge(*mix(s, it, 33))
                    ln_stats(ln3_dve, s, it, 0, H[s])

                for s in range(STREAMS):
                    q = ln3_dve
                    dve.wait_ge(*ln3_pool(s, it, 5))
                    apply(XA, H, s).then_inc(*q.step(s))
                    dve.wait_ge(*q(s, it, 4))
                    for t in range(TILES):
                        last = nc.vector.tensor_scalar(NX[s][:, t, :], XA[s][:, t, :], rstd[s][:, 2, t:t + 1], None, ALU.mult)
                    last.then_inc(*q.step(s))
                    dve.wait_ge(*q(s, it, 5))
                    nc.vector.tensor_tensor(NX[s], NX[s], ln1_rows[:, 0, :].unsqueeze(1).broadcast_to([P, TILES, C]), ALU.mult).then_inc(*q.step(s))
                    dve.wait_ge(*q(s, it, 6))
                    nc.vector.tensor_tensor(NX[s], NX[s], ln1_rows[:, 1, :].unsqueeze(1).broadcast_to([P, TILES, C]), ALU.add).then_inc(*q.step(s))
                    dve.wait_ge(*q(s, it, 7))
                    nc.vector.tensor_copy(HV[s][:, :, 0:DH], NX[s].rearrange("p t (h d) -> p (t h) d", d=DH)).then_inc(*q.step(s))

                for s in range(STREAMS):
                    dve.wait_ge(*feat_act(s, it, 1))
                    nc.vector.tensor_reduce(stab[s][:, 1, :], NX[s].rearrange("p t (h d) -> p (t h) d", d=DH), AX.X, ALU.add).then_inc(*feat_dve.step(s))
                for t in range(TILES):
                    for s in range(STREAMS):
                        q, k = feat_dve, 1 + 3 * t
                        b = 2 * (t % 2)
                        sl = slice(t * HEADS, (t + 1) * HEADS)
                        uv = PS[s][:, b:b + 2, :].rearrange("p b c -> p (b c)")[:, 0:HEADS * MF].rearrange("p (h m) -> p h m", m=MF)
                        dve.wait_ge(*feat_pe(s, it, t + 1))
                        nc.vector.tensor_reduce(stab[s][:, 0, sl], uv, AX.X, ALU.max).then_inc(*q.step(s))
                        dve.wait_ge(*q(s, it, k + 1))
                        nc.vector.scalar_tensor_tensor(out=stab[s][:, 3, sl], in0=stab[s][:, 1, sl], scalar=0.5, in1=stab[s][:, 0, sl],
                                                       op0=ALU.mult, op1=ALU.add).then_inc(*q.step(s))
                        dve.wait_ge(*q(s, it, k + 2))
                        nc.vector.tensor_tensor(big_a[s][:, t * HEADS * MF:(t + 1) * HEADS * MF].rearrange("p (h m) -> p h m", m=MF), uv,
                                                stab[s][:, 3, sl].unsqueeze(2).broadcast_to([P, HEADS, MF]), ALU.subtract).then_inc(*q.step(s))
                for s in range(STREAMS):
                    dve.wait_ge(*stab_pe(s, it, 1))
                    nc.vector.tensor_reduce(stabT[s][:, :, 0], PS[s][0:HEADS, 0, :].rearrange("h (b n) -> h b n", b=2), AX.X, ALU.max).then_inc(*stab_dve.step(s))
                    dve.wait_ge(*stab_dve(s, it, 1))
                    nc.vector.tensor_tensor(stabT[s][:, :, 1:1 + HEADS], ident[0:HEADS, 0:HEADS].unsqueeze(1).broadcast_to([HEADS, 2, HEADS]),
                                            stabT[s][:, :, 0:1].broadcast_to([HEADS, 2, HEADS]), ALU.mult).then_inc(*stab_dve.step(s))
                for s in range(STREAMS):
                    dve.wait_ge(*stab_pe(s, it, 2))
                    nc.vector.tensor_tensor(stab[s][:, 2, :].rearrange("p (b t h) -> p b t h", b=2, t=2), stab[s][:, 0, :].rearrange("p (b t h) -> p b t h", b=2, t=2),
                                            PS[s][:, 1, 0:2 * HEADS].rearrange("p (b h) -> p b h", b=2).unsqueeze(2).broadcast_to([P, 2, 2, HEADS]),
                                            ALU.subtract).then_inc(*stab_dve.step(s))
                    dve.wait_ge(*stab_act(s, it, 1))
                    nc.vector.tensor_tensor(CV[s], HV[s][:], stab[s][:, 2, :].unsqueeze(2).broadcast_to([P, TILES * HEADS, HV1]), ALU.mult).then_inc(*stab_dve.step(s))
                for s in range(STREAMS):
                    dve.wait_ge(*ctx_pe(s, it, 1))
                    src = PS[s][:, 2, 0:2 * HEADS * HV1].rearrange("p (b j c) -> p b j c", b=2, j=HEADS // 2)
                    for b in range(2):
                        for hh in range(2):
                            rows, cols = slice(hh * MF, (hh + 1) * MF), slice(hh * HV1, (hh + 1) * HV1)
                            last = nc.vector.tensor_copy(CTX[s][rows, b, :, cols], src[rows, b, :, cols])
                    last.then_inc(*ctx_dve.step(s))
                for s in range(STREAMS):
                    dve.wait_ge(*attn_pe(s, it, 1))
                    for b in range(2):
                        src = PS[s][:, 3 - b, 0:2 * HEADS * HV1].rearrange("p (q e) -> p q e", e=HV1)
                        qs = slice(2 * b * HEADS, (2 * b + 2) * HEADS)
                        last = nc.vector.reciprocal(stab[s][:, 1, qs], src[:, :, DH])
                    last.then_inc(*attn_dve.step(s))
                    dve.wait_ge(*attn_dve(s, it, 1))
                    for b in range(2):
                        src = PS[s][:, 3 - b, 0:2 * HEADS * HV1].rearrange("p (q e) -> p q e", e=HV1)
                        qs = slice(2 * b * HEADS, (2 * b + 2) * HEADS)
                        last = nc.vector.tensor_tensor(NX[s].rearrange("p t (h d) -> p (t h) d", d=DH)[:, qs, :], src[:, :, 0:DH],
                                                       stab[s][:, 1, qs].unsqueeze(2).broadcast_to([P, 2 * HEADS, DH]), ALU.mult)
                    last.then_inc(*attn_dve.step(s))
                    dve.wait_ge(*attn_dve(s, it, 2))
                    nc.vector.tensor_tensor(XA[s][:], XA[s][:], NX[s], ALU.add).then_inc(*attn_dve.step(s))
                    dve.wait_ge(*attn_dve(s, it, 3))
                    ln_stats(ln_dve, s, it, 8, XA[s])
                for s in range(STREAMS):
                    dve.wait_ge(*ln_pool(s, it, 3))
                    apply(NX, XA, s).then_inc(*ln_dve.step(s))
                for s in range(STREAMS):
                    dve.wait_ge(*mlp_pe(s, it, FT + 1))
                    dve.wait_ge(*hadd(s, it, 2))
                    nc.vector.tensor_tensor(two(H[s][:]), two(H[s][:]), PS[s][:, 2:4, 0:2 * C], ALU.add).then_inc(*mlp_dve.step(s))
                    dve.wait_ge(*mlp_dve(s, it, 1))
                    ln_stats(ln_dve, s, it, 12, H[s])
                for s in range(STREAMS):
                    dve.wait_ge(*ln_pool(s, it, 4))
                    apply(NX, H, s).then_inc(*ln_dve.step(s))

                for s in range(STREAMS):
                    q = rt_dve
                    pr = small[s][:, 0, 0:TILES * E1].rearrange("p (t e) -> p t e", e=E1)
                    kp = small[s][:, 1, 0:TILES * E1].rearrange("p (t e) -> p t e", e=E1)
                    lo = small[s][:, 2, 0:2 * TILES].rearrange("p (n t) -> p n t", n=2)
                    dve.wait_ge(*rt_act(s, it, 1))
                    nc.vector.tensor_tensor(lo[:, 0, :], pr[:, :, 0], pr[:, :, 1], ALU.min)
                    nc.vector.tensor_tensor(lo[:, 1, :], pr[:, :, 1], pr[:, :, 2], ALU.min).then_inc(*q.step(s))
                    dve.wait_ge(*q(s, it, 1))
                    nc.vector.tensor_tensor(kp[:, :, 2], pr[:, :, 2], lo[:, 0, :], ALU.is_gt)
                    nc.vector.tensor_tensor(kp[:, :, 0], pr[:, :, 0], lo[:, 1, :], ALU.is_ge).then_inc(*q.step(s))
                    dve.wait_ge(*q(s, it, 2))
                    nc.vector.tensor_tensor(lo[:, 0, :], kp[:, :, 0], kp[:, :, 2], ALU.add).then_inc(*q.step(s))
                    dve.wait_ge(*q(s, it, 3))
                    nc.vector.tensor_scalar(kp[:, :, 1], lo[:, 0, :], -1.0, 2.0, ALU.mult, ALU.add).then_inc(*q.step(s))
                    dve.wait_ge(*q(s, it, 4))
                    nc.vector.tensor_tensor(kp, kp, pr, ALU.mult).then_inc(*q.step(s))
                    dve.wait_ge(*q(s, it, 5))
                    nc.vector.tensor_reduce(lo[:, 0, :], kp, AX.X, ALU.add).then_inc(*q.step(s))
                    dve.wait_ge(*q(s, it, 6))
                    nc.vector.reciprocal(lo[:, 1, :], lo[:, 0, :]).then_inc(*q.step(s))
                    dve.wait_ge(*q(s, it, 7))
                    nc.vector.tensor_tensor(kp, kp, lo[:, 1, :].unsqueeze(2).broadcast_to([P, TILES, E1]), ALU.mult).then_inc(*q.step(s))
                for x in range(NX1):
                    for s in range(STREAMS):
                        q, k = ex_dve, x * (IT + 1)
                        for j in range(IT):
                            dve.wait_ge(*ex_pe(s, it, x * (2 * IT + 1) + 2 * j + 2))
                            dve.wait_ge(*ex_act(s, it, x * IT + j + 1))
                            if x > 0:
                                dve.wait_ge(*ex_pe(s, it, x * (2 * IT + 1)))
                            nc.vector.tensor_tensor(big_b[s][:, j * CHUNK:(j + 1) * CHUNK], PS[s][:, 1, :], big_a[s][:, j * CHUNK:(j + 1) * CHUNK],
                                                    ALU.mult).then_inc(*q.step(s))
                        dve.wait_ge(*ex_pe(s, it, (x + 1) * (2 * IT + 1)))
                        if x > 0:
                            dve.wait_ge(*ex_dve(s, it, k))
                        kp = small[s][:, 1, 0:TILES * E1].rearrange("p (t e) -> p t e", e=E1)
                        if x == 0:
                            nc.vector.tensor_tensor(two(H[s][:]), two(H[s][:]), PS[s][:, 2:4, 0:2 * C], ALU.add).then_inc(*q.step(s))
                        else:
                            for t in range(TILES):
                                last = nc.vector.scalar_tensor_tensor(out=H[s][:, t, :], in0=PS[s][:, 2 + t // 2, (t % 2) * C:(t % 2 + 1) * C],
                                                                      scalar=kp[:, t, x - 1:x], in1=H[s][:, t, :], op0=ALU.mult, op1=ALU.add)
                            last.then_inc(*q.step(s))

        @block.tensor
        def _(pe):
            for f in (embed_pe, tr, kv_pe, out_pe, ff_pe, moe_pe, feat_pe, stab_pe, ctx_pe, et_pe, attn_pe, mlp_pe, rt_pe, ex_pe):
                f.credit(pe)
            pe.sem_inc(table_mm, RING)
            pe.wait_ge(const_pool, 3 + 2 + 2 * STREAMS)
            pe.wait_ge(ident_in, 16)
            nc.tensor.matmul(gram, ident[0:1, 1:1 + RANK], HV[0][0:1, :, :].rearrange("p q e -> p (q e)")[:, 0:CR], start=True, stop=False,
                             skip_group_check=True)
            with pe.Fori(0, LOADS // RING) as it:
                for b in range(RING):
                    pe.wait_ge(table_in[b], it * 32 + 32)
                    for j in range(ROWS):
                        last = nc.tensor.matmul(gram, tab[b][:, j, C:CR], tab[b][:, j, :], start=False, stop=False, skip_group_check=True)
                    last.then_inc(table_mm, 1)
            pe.wait_ge(table_in[0], LOADS // RING * 32 + 32)
            nc.tensor.matmul(gram, tab[0][0:TAIL, 0, C:CR], tab[0][0:TAIL, 0, :], start=False, stop=True,
                             skip_group_check=True).then_inc(table_mm, 1)
            pe.wait_ge(norm_act, 1)
            pe.wait_ge(loaded, 16 * len(loads))
            nc.tensor.matmul(PS[0][0:RANK, 1, 0:C], gram_sb[:, C:CR], lora_b[:], start=True, stop=True).then_inc(norm_pe, 1)
            pe.wait_ge(norm_dve, 4)
            nc.tensor.matmul(PS[0][:, 2, 0:C], ones[:], colsum, start=True, stop=False)
            nc.tensor.matmul(PS[0][:, 2, 0:C], ones[0:RANK, :], cross, start=False, stop=True).then_inc(norm_pe, 1)
            pe.wait_ge(const_dve, 3)
            pe.wait_ge(norm_dve, NORM_STEPS)

            def kparts(w, lo, hi):
                return ((w[0:P, 0, lo:hi], P), (w[0:C1, 1, lo:hi], C1))

            def transposes(i, ready, k):
                banks = (3, 0) if i == 0 else (0, 1)
                for s in range(STREAMS):
                    pe.wait_ge(*ready(s, it, k))
                    for t in range(TILES):
                        nc.tensor.transpose(PS[s][0:P, banks[0], t * P:(t + 1) * P], NX[s][:, t, 0:P], ident[:])
                        last = nc.tensor.transpose(PS[s][0:C1, banks[1], t * P:(t + 1) * P], NX[s][:, t, P:C], ident[:])
                    last.then_inc(*tr.step(s))

            def by_channel(dst, w, lo, hi, s, t0=0, t1=CHUNK):
                for k, (part, rows) in enumerate(kparts(w, lo, hi)):
                    last = nc.tensor.matmul(dst, part, hT[s][0:rows, k, t0:t1], start=(k == 0), stop=(k == 1))
                return last

            def by_token(dst, w, lo, hi, s, t, bias=None):
                for k, (part, rows) in enumerate(kparts(w, lo, hi)):
                    last = nc.tensor.matmul(dst, hT[s][0:rows, k, t * P:(t + 1) * P], part, start=(k == 0), stop=(k == 1 and bias is None))
                if bias is not None:
                    last = nc.tensor.matmul(dst, ones[0:1, :], bias, start=False, stop=True)
                return last

            def bank_of(s, t):
                return PS[s][:, 2 + t // 2, (t % 2) * C:(t % 2 + 1) * C]

            with pe.Fori(0, PASSES * UNIT, UNIT) as it:
                for s in range(STREAMS):
                    pe.wait_ge(row_in[s], it + UNIT)
                    pe.wait_ge(*ex_dve(s, it, 0))
                    for t in range(TILES):
                        last = nc.tensor.transpose(PS[s][0:RANK, 0, t * P:(t + 1) * P], glora[s][:, t, :], ident[:])
                    last.then_inc(*embed_pe.step(s))
                for s in range(STREAMS):
                    pe.wait_ge(*embed_act(s, it, 1))
                    for t in range(TILES):
                        last = nc.tensor.matmul(PS[s][:, 1 + t // 2, (t % 2) * C:(t % 2 + 1) * C], big_a[s][0:RANK, t * P:(t + 1) * P], lora_b[:],
                                                start=True, stop=True)
                    last.then_inc(*embed_pe.step(s))
                transposes(0, ln0_dve, 7)

                def last_channels(col, w, bank, s):
                    for b in range(2):
                        last = by_channel(PS[s][b * C1:(b + 1) * C1, bank, col:col + SEQ], w, P, C, s, b * SEQ, (b + 1) * SEQ)
                    return last

                for s in range(STREAMS):
                    pe.wait_ge(*ev(s, it, 1))
                    by_channel(PS[s][:, 1, :], wk, 0, P, s)
                    last_channels(0, wk, 2, s)
                    by_channel(PS[s][:, 3, :], wv, 0, P, s)
                    last_channels(SEQ, wv, 2, s).then_inc(*kv_pe.step(s))
                    by_channel(PS[s][:, 0, :], wr, 0, P, s)
                    pe.wait_ge(*kv_act(s, it, 1))
                    last_channels(0, wr, 1, s).then_inc(*kv_pe.step(s))

                for s in range(STREAMS):
                    pe.wait_ge(*wkv_dve(s, it, 26))
                    for t in range(TILES):
                        b, h = t // 2, t % 2
                        nc.tensor.matmul(bank_of(s, t), big_b[s][:, t * P:(t + 1) * P], wo[:, 0, :], start=True, stop=False)
                        last = nc.tensor.matmul(bank_of(s, t), big_b[s][b * C1:(b + 1) * C1, CHUNK + h * P:CHUNK + (h + 1) * P],
                                                wo[b * C1:(b + 1) * C1, 1, :], start=False, stop=True)
                    last.then_inc(*out_pe.step(s))

                transposes(1, ln_dve, 4)
                for s in range(STREAMS):
                    pe.wait_ge(*ev(s, it, 2))
                    for t in range(TILES):
                        last = by_token(bank_of(s, t), wrf, 0, C, s, t)
                    last.then_inc(*ff_pe.step(s))
                    for j in range(FT):
                        if j >= 2:
                            pe.wait_ge(*ff_act(s, it, 2 + 2 * (j - 2)))
                        by_channel(PS[s][:, j % 2, :], wkf, j * P, (j + 1) * P, s).then_inc(*ff_pe.step(s))
                    pe.wait_ge(*ff_act(s, it, 1 + 2 * FT))
                    for t in range(TILES):
                        for j in range(FT):
                            last = nc.tensor.matmul(bank_of(s, t), big_a[s][:, j * CHUNK + t * P:j * CHUNK + (t + 1) * P], wvf[:, j, :],
                                                    start=(j == 0), stop=(j == FT - 1))
                    last.then_inc(*ff_pe.step(s))

                transposes(2, ln_dve, 8)
                for s in range(STREAMS):
                    pe.wait_ge(*ev(s, it, 3))
                    for t in range(TILES):
                        last = by_token(PS[s][:, 2, t * E0:(t + 1) * E0], router0, 0, E0, s, t, router0_b[:])
                    last.then_inc(*moe_pe.step(s))
                for s in range(STREAMS):
                    pe.wait_ge(*moe_dve(s, it, 14))
                    for t in range(TILES):
                        last = nc.tensor.transpose(PS[s][0:E0, 3, t * P:(t + 1) * P], small[s][:, 9, t * E0:(t + 1) * E0], ident[:])
                    last.then_inc(*moe_pe.step(s))
                for s in range(STREAMS):
                    for e2 in range(E0 // 2):
                        for t in range(TILES):
                            n = e2 * TILES + t
                            if n >= 2:
                                pe.wait_ge(*mix(s, it, 2 * (n - 2) + 2))
                            by_token(PS[s][:, n % 2, 0:2 * C], experts, 2 * e2 * C, 2 * (e2 + 1) * C, s, t).then_inc(*moe_pe.step(s))
                    pe.wait_ge(*moe_dve(s, it, 15))
                    for t in range(TILES):
                        last = nc.tensor.matmul(bank_of(s, t), wT[s][:, t * P:(t + 1) * P], experts_b, start=True, stop=True)
                    last.then_inc(*moe_pe.step(s))

                transposes(3, ln3_dve, 8)
                for t in range(TILES):
                    for s in range(STREAMS):
                        b = 2 * (t % 2)
                        if t == 0:
                            pe.wait_ge(*ev(s, it, 4))
                        if t >= 2:
                            pe.wait_ge(*feat_dve(s, it, 1 + 3 * (t - 1)))
                        nc.tensor.matmul(PS[s][:, b, :], hT[s][:, 0, t * P:(t + 1) * P], projbd[:, 0:HK0 * MF], start=True, stop=True)
                        nc.tensor.matmul(PS[s][:, b + 1, 0:(HEADS - HK0) * MF], hT[s][0:C1, 1, t * P:(t + 1) * P], projbd[0:C1, HK0 * MF:HEADS * MF],
                                         start=True, stop=True).then_inc(*feat_pe.step(s))
                for s in range(STREAMS):
                    pe.wait_ge(*feat_dve(s, it, 1 + 3 * TILES))
                    for t in range(TILES):
                        last = nc.tensor.transpose(PS[s][0:HEADS, 0, t * P:(t + 1) * P], stab[s][:, 0, t * HEADS:(t + 1) * HEADS], ident[:])
                    last.then_inc(*stab_pe.step(s))
                for s in range(STREAMS):
                    pe.wait_ge(*stab_dve(s, it, 2))
                    for b in range(2):
                        last = nc.tensor.matmul(PS[s][:, 1, b * HEADS:(b + 1) * HEADS], ones[0:HEADS, :], stabT[s][:, b, 1:1 + HEADS], start=True, stop=True)
                    last.then_inc(*stab_pe.step(s))
                for s in range(STREAMS):
                    pe.wait_ge(*stab_dve(s, it, 4))
                    pe.wait_ge(*feat_act(s, it, 1 + TILES))
                    w = HEADS * HV1
                    for b in range(2):
                        for t in (2 * b, 2 * b + 1):
                            nc.tensor.matmul(PS[s][:, 2, b * w:(b + 1) * w], feat_eps[:], HV[s][:, t * HEADS:(t + 1) * HEADS, :].rearrange("p q e -> p (q e)"),
                                             start=(t == 2 * b), stop=False, skip_group_check=True)
                        for t in (2 * b, 2 * b + 1):
                            for j in range(HEADS // 2):
                                q = t * HEADS + 2 * j
                                last = nc.tensor.matmul(PS[s][:, 2, b * w + j * 2 * HV1:b * w + (j + 1) * 2 * HV1], big_a[s][:, q * MF:(q + 2) * MF],
                                                        CV[s][:, q:q + 2, :].rearrange("p q e -> p (q e)"), start=False, stop=(t == 2 * b + 1),
                                                        skip_group_check=True)
                    last.then_inc(*ctx_pe.step(s))
                for s in range(STREAMS):
                    for j in range(FT):
                        if j >= 2:
                            pe.wait_ge(*et_act(s, it, j - 1))
                        for t in range(TILES):
                            last = nc.tensor.transpose(PS[s][:, j % 2, t * P:(t + 1) * P], big_a[s][:, t * HEADS * MF + j * P:t * HEADS * MF + (j + 1) * P], ident[:])
                        last.then_inc(*et_pe.step(s))
                for s in range(STREAMS):
                    pe.wait_ge(*ctx_dve(s, it, 1))
                    pe.wait_ge(*et_act(s, it, FT))
                    for t in range(TILES):
                        for j in range(HEADS // 2):
                            col = (t % 2) * HEADS * HV1 + j * 2 * HV1
                            last = nc.tensor.matmul(PS[s][:, 3 - t // 2, col:col + 2 * HV1], big_b[s][:, j * CHUNK + t * P:j * CHUNK + (t + 1) * P],
                                                    CTX[s][:, t // 2, j, :], start=True, stop=True)
                    last.then_inc(*attn_pe.step(s))

                transposes(4, ln_dve, 12)
                for s in range(STREAMS):
                    pe.wait_ge(*ev(s, it, 5))
                    for j in range(FT):
                        if j >= 2:
                            pe.wait_ge(*mlp_act(s, it, j - 1))
                        by_channel(PS[s][:, j % 2, :], w1, j * P, (j + 1) * P, s).then_inc(*mlp_pe.step(s))
                    pe.wait_ge(*mlp_act(s, it, FT))
                    for t in range(TILES):
                        nc.tensor.matmul(bank_of(s, t), ones[32:33, :], b2, start=True, stop=False)
                        for j in range(FT):
                            last = nc.tensor.matmul(bank_of(s, t), big_a[s][:, j * CHUNK + t * P:j * CHUNK + (t + 1) * P], w2[:, j, :],
                                                    start=False, stop=(j == FT - 1))
                    last.then_inc(*mlp_pe.step(s))

                transposes(5, ln_dve, 16)
                for s in range(STREAMS):
                    pe.wait_ge(*ev(s, it, 6))
                    for t in range(TILES):
                        last = by_token(PS[s][:, 2, t * E1:(t + 1) * E1], router1, 0, E1, s, t, router1_b[:])
                    last.then_inc(*rt_pe.step(s))
                for x in range(NX1):
                    for s in range(STREAMS):
                        for j in range(IT):
                            if x or j:
                                pe.wait_ge(*ex_act(s, it, x * IT + j))
                            lo = 2 * x * I1 + j * P
                            by_channel(PS[s][:, 0, :], gate_up, lo, lo + P, s).then_inc(*ex_pe.step(s))
                            if x or j:
                                pe.wait_ge(*ex_dve(s, it, x * (IT + 1) + j - (j == 0)))
                            by_channel(PS[s][:, 1, :], gate_up, lo + I1, lo + I1 + P, s).then_inc(*ex_pe.step(s))
                        if x:
                            pe.wait_ge(*ex_dve(s, it, x * (IT + 1)))
                        else:
                            pe.wait_ge(*rt_act(s, it, 1))
                        pe.wait_ge(*ex_dve(s, it, x * (IT + 1) + IT))
                        for t in range(TILES):
                            for j in range(IT):
                                last = nc.tensor.matmul(bank_of(s, t), big_b[s][:, j * CHUNK + t * P:j * CHUNK + (t + 1) * P], down[:, x, j, :],
                                                        start=(j == 0), stop=(j == IT - 1))
                        last.then_inc(*ex_pe.step(s))


def kernel(**inputs):
    import numpy as np
    import concourse.bacc as bacc
    from concourse.bass_utils import run_bass_kernel_spmd

    g = {n: np.asarray(v) for n, v in inputs.items()}

    def col(*names):
        return np.ascontiguousarray(np.stack([g[n] for n in names], axis=1))

    B, S = g["x"].shape
    C = g["L0_tok_embeddings"].shape[1]
    E0 = g["L0_ffn_router_w"].shape[0]
    arrays = {
        "idx": g["x"].reshape(-1, TILES, P).transpose(0, 2, 1),
        "embeddings": g["L0_tok_embeddings"], "lora_a": g["L0_tok_lora_a"], "lora_b": g["L0_tok_lora_b"],
        "magnitude": g["L0_tok_magnitude"].reshape(1, C),
        "ln_cols": col("L0_attn_ln1_w", "L0_attn_ln1_b", "L0_attn_ln2_w", "L0_attn_ln2_b"),
        "ln2_cols": col("L1_attn_ln2_g", "L1_attn_ln2_b"),
        "ln1_g": g["L1_attn_ln1_g"].reshape(1, C), "ln1_b": g["L1_attn_ln1_b"].reshape(1, C),
        "wu": col("L0_attn_decay", "L0_attn_first"),
        "WkT": g["L0_attn_Wk_a"].T, "WvT": g["L0_attn_Wv_a"].T, "WrT": g["L0_attn_Wr_a"].T, "WoT": g["L0_attn_Wo_a"].T,
        "WkfT": g["L0_attn_Wk_f"].T, "WvfT": g["L0_attn_Wv_f"].T, "WrfT": g["L0_attn_Wr_f"].T,
        "router0T": g["L0_ffn_router_w"].T, "router0_b": g["L0_ffn_router_b"].reshape(1, E0),
        "experts": g["L0_ffn_expert_w"].transpose(2, 0, 1).reshape(C, E0 * C), "experts_b": g["L0_ffn_expert_b"],
        "projT": g["L1_attn_proj"].T, "W1": g["L1_attn_W1"], "b1": g["L1_attn_b1"].reshape(-1, P).T,
        "W2": g["L1_attn_W2"], "b2": g["L1_attn_b2"].reshape(1, C),
        "gate_up": np.concatenate([np.concatenate([x, y], axis=1) for x, y in
                                   [(g["L1_ffn_shared_gate"], g["L1_ffn_shared_up"]), *zip(g["L1_ffn_routed_gate"], g["L1_ffn_routed_up"])]], axis=1),
        "down": np.concatenate([g["L1_ffn_shared_down"][None], g["L1_ffn_routed_down"]], axis=0),
        "router1": g["L1_ffn_router_w"], "router1_b": g["L1_ffn_routing_bias"].reshape(1, -1),
        "ident": np.eye(P, dtype=np.float32), "iota8": np.arange(E0, dtype=np.float32).reshape(1, E0),
    }
    nc = bacc.Bacc("TRN2", target_bir_lowering=False, num_devices=1)
    fed, aps = {}, {}
    for n, v in arrays.items():
        v = np.ascontiguousarray(v)
        fed[f"in_{n}"] = v
        aps[n] = nc.dram_tensor(f"in_{n}", v.shape, mybir.dt.from_np(v.dtype), kind="ExternalInput").ap()
    aps["SEQ"], aps["proj_shape"] = S, g["L1_attn_proj"].shape
    out = nc.dram_tensor("out_0", (B * S, C), F32, kind="ExternalOutput").ap()
    lm_tower(nc, aps, out)
    r = run_bass_kernel_spmd(nc, [fed], core_ids=[0])
    return r.results[0]["out_0"].reshape(B, S, C)
```

```python
from contextlib import ExitStack

import concourse.bass as bass
from concourse import mybir

F32 = mybir.dt.float32
F16 = mybir.dt.float16
I32 = mybir.dt.int32
U32 = mybir.dt.uint32
ALU = mybir.AluOpType
ACT = mybir.ActivationFunctionType
AX = mybir.AxisListType

P = 128
UNIT = 128
STREAMS = 2
WEIGHT_PIECES = 7
TILES = 4
CHUNK = TILES * P
NEG = -1e38
LN_EPS = 1e-5
FEAT_EPS = 1e-4
WSCALE = 64.0


def lm_tower(nc, a, out):
    V, C = a["embeddings"].shape
    RANK = a["lora_a"].shape[1]
    TOKENS = out.shape[0]
    SEQ = a["SEQ"]
    PASSES = TOKENS // (STREAMS * CHUNK)
    LORA_SCALE = 32.0 / RANK
    FF = a["W2"].shape[0]
    FT = FF // P
    E0 = a["experts_b"].shape[0]
    MF, DH = a["proj_shape"]
    HEADS = C // DH
    HK0 = P // DH
    E1 = a["router1_b"].shape[1]
    I1 = a["down"].shape[1]
    IT = I1 // P
    C1 = C - P
    SEGS = CHUNK // SEQ + 1
    SEGW = SEQ + 2
    assert CHUNK == 2 * SEQ and C1 * 2 == P and FT == 6 and SEGS == 3 and 2 * MF == P

    ROWS = 14
    RING = 4
    MAIN = V // P // ROWS * ROWS
    LOADS = MAIN // ROWS
    TAIL = V - MAIN * P
    CR = C + RANK
    assert LOADS % RING == 0 and 0 < TAIL <= P

    with ExitStack() as ctx:
        def sb(name, shape, dt=F32):
            return ctx.enter_context(nc.sbuf_tensor(name, shape, dt))

        def sem(name):
            return ctx.enter_context(nc.semaphore(name))

        class Steps:

            def __init__(self, name, per):
                self.sems, self.per, self.made = [sem(f"{name}_{s}") for s in range(STREAMS)], per, [0] * STREAMS

            def step(self, s):
                self.made[s] = self.made[s] % self.per + 1
                return self.sems[s], (1 if self.made[s] < self.per else UNIT - self.per + 1)

            def __call__(self, s, u, k):
                return self.sems[s], u + (k + 1 if k < self.per else UNIT + 1)

            def credit(self, eng):
                for q in self.sems:
                    eng.sem_inc(q, 1)

        ident = sb("ident", [P, P])
        ones = sb("ones", [P, P])
        feat_eps = sb("feat_eps", [P, P])
        PIECES, PIECE = a["wcat"].shape[0], a["wcat"].shape[2]
        wcat = sb("wcat", [P, 4, PIECES * PIECE], F16)
        COLS, at = {}, 0
        for name, n in (("k", C), ("v", C), ("r", C), ("kf", FF), ("rf", C), ("experts", E0 * C), ("w1", FF),
                        ("gate_up", 2 * I1 * (E1 + 1)), ("router0", E0), ("router1", E1)):
            COLS[name], at = at, at + n
        assert at == PIECES * PIECE and PIECES == LOADS // RING and PIECE <= 2 * TILES * C
        proj0 = sb("proj0", [P, 2, HK0 * MF], F16)
        proj1 = sb("proj1", [P, 2, (HEADS - HK0) * MF], F16)
        wo = sb("wo", [P, 2, C])
        wvf = sb("wvf", [P, FT, C])
        router0_b = sb("router0_b", [1, E0])
        bias_rows = sb("bias_rows", [33, C])
        experts_b, b2 = bias_rows[0:E0, :], bias_rows[32:33, :]
        b1 = sb("b1", [P, FT])
        w2 = sb("w2", [P, FT, C])
        down = sb("down", [P, E1 + 1, IT, C])
        router1_b = sb("router1_b", [1, E1])
        lora_b = sb("lora_b", [RANK, C])
        ln_cols = sb("ln_cols", [P, 2, 4])
        ln2_cols = sb("ln2_cols", [P, 2, 2])
        ln1_rows = sb("ln1_rows", [P, 2, C])
        wu = sb("wu", [P, 2, 2])
        gscale = sb("gscale", [P, C])
        half = sb("half", [P, TILES])
        eps_t = sb("eps_t", [P, TILES])
        iota8 = sb("iota8", [P, E0])
        decay_row = sb("decay_row", [P, SEGS, SEGW])

        SW = SEGS * SEGW
        WSW = (3 + 2 + 4 + 2) * SW
        ws = sb("ws", [P, WSW])

        def seg(at, n=1):
            v = ws[:, at * SW:(at + n) * SW]
            return v.rearrange("p (n g t) -> p n g t", n=n, g=SEGS)

        K, KU, VV = seg(0), seg(1), seg(2)
        MAXES = [seg(3), seg(4)]
        DECAYS = [seg(5, 2), seg(7, 2)]
        SUMS = [(seg(9 + d), DECAYS[d][:, 1:2]) for d in range(2)]

        def flat(v):
            return v.rearrange("p n g t -> p (n g t)")

        def data(v):
            return v[:, :, :, 1:SEQ + 1]

        BW = TILES * HEADS * MF
        big_a = [sb(f"big_a{s}", [P, BW]) for s in range(STREAMS)]
        big_b = [sb(f"big_b{s}", [P, BW]) for s in range(STREAMS)]
        tok = [sb(f"tok{s}", [P, 2, TILES, C]) for s in range(STREAMS)]
        H = [v[:, 0] for v in tok]
        XA = [v[:, 1] for v in tok]
        wpiece = [v[:].rearrange("p a t c -> p (a t c)")[:, 0:PIECE] for v in tok]
        HV1 = DH + 1
        norm = [sb(f"norm{s}", [P, TILES * HEADS * HV1]) for s in range(STREAMS)]
        NX = [n[:, 0:TILES * C].rearrange("p (t c) -> p t c", t=TILES) for n in norm]
        CV = [n[:].rearrange("p (q e) -> p q e", e=HV1) for n in norm]
        HV = [sb(f"heads{s}", [P, TILES * HEADS, HV1]) for s in range(STREAMS)]
        xh = [sb(f"xh{s}", [P, 3, CHUNK], F16) for s in range(STREAMS)]
        exp_r = [v[:].rearrange("p a b -> p (a b)").bitcast(F32) for v in xh]
        idx = [sb(f"idx{s}", [P, TILES], I32) for s in range(STREAMS)]
        grow = XA
        glora = [sb(f"glora{s}", [P, TILES, RANK]) for s in range(STREAMS)]
        stats = [sb(f"stats{s}", [P, TILES, 6]) for s in range(STREAMS)]
        mv = [sb(f"mv{s}", [P, TILES, 2]) for s in range(STREAMS)]
        rstd = [sb(f"rstd{s}", [P, 4, TILES]) for s in range(STREAMS)]
        small = [sb(f"small{s}", [P, 10, TILES * E0]) for s in range(STREAMS)]
        idx8 = [sb(f"idx8{s}", [P, TILES, 8], U32) for s in range(STREAMS)]
        wT = [n[0:E0, 0:CHUNK] for n in norm]
        stab = [sb(f"stab{s}", [P, 4, TILES * HEADS]) for s in range(STREAMS)]
        stabT = [sb(f"stabT{s}", [HEADS, 2, 1 + HEADS]) for s in range(STREAMS)]
        CTX = [sb(f"ctx{s}", [P, 2, HEADS // 2, 2 * HV1]) for s in range(STREAMS)]

        PS = [ctx.enter_context(nc.psum_tensor(f"ps{s}", [P, 4, 512], F32)) for s in range(STREAMS)]

        loaded, ident_in, mag_in = sem("weights_loaded"), sem("ident_in"), sem("mag_in")
        proj_set, proj_dve = sem("proj_set"), sem("proj_dve")
        const_pool = sem("const_pool")
        const_dve = sem("const_dve")
        const_act = sem("const_act")
        table_in = [sem(f"table_in{b}") for b in range(RING)]
        table_mm = sem("table_mm")
        table_sq = sem("table_sq")
        table_add = sem("table_add")
        piece_in, piece_hi, piece_lo = sem("piece_in"), sem("piece_hi"), sem("piece_lo")
        norm_pe = sem("norm_pe")
        norm_dve = sem("norm_dve")
        norm_act = sem("norm_act")
        held = sem("held")
        stored = [sem(f"stored{s}") for s in range(STREAMS)]
        idx_in = [sem(f"idx_in{s}") for s in range(STREAMS)]
        row_in = [sem(f"row_in{s}") for s in range(STREAMS)]

        embed_pe = Steps("embed_pe", 2)
        embed_act = Steps("embed_act", 1)
        ln0_dve, ln0_pool = Steps("ln0_dve", 7), Steps("ln0_pool", 5)
        tr = Steps("tr_pe", 6)
        ev, lo = Steps("tr_act", 6), Steps("lo_dve", 6)
        kv_pe, kv_act = Steps("kv_pe", 2), Steps("kv_act", 3)
        wkv_dve, wkv_act = Steps("wkv_dve", 28), Steps("wkv_act", 3)
        out_pe, out_dve = Steps("out_pe", 1), Steps("out_dve", 1)
        hadd = Steps("hidden_pool", 2)
        ln_dve, ln_pool = Steps("ln_dve", 4 * 4), Steps("ln_pool", 4)
        ff_pe, ff_act, ff_dve = Steps("ff_pe", 1 + FT + 1), Steps("ff_act", 1 + 2 * FT), Steps("ff_dve", 2)
        moe_pe, moe_dve, moe_act = Steps("moe_pe", 2 + 16 + 1), Steps("moe_dve", 15), Steps("moe_act", 1)
        mix = Steps("mix_dve", 2 * 16 + 1)
        ln3_dve, ln3_pool = Steps("ln3_dve", 8), Steps("ln3_pool", 5)
        feat_act, feat_pe, feat_dve = Steps("feat_act", 1 + TILES), Steps("feat_pe", TILES), Steps("feat_dve", 1 + 3 * TILES)
        stab_pe, stab_dve, stab_act = Steps("stab_pe", 2), Steps("stab_dve", 4), Steps("stab_act", 1)
        ctx_pe, ctx_dve = Steps("ctx_pe", 1), Steps("ctx_dve", 1)
        et_pe, et_act = Steps("et_pe", FT), Steps("et_act", FT)
        attn_pe, attn_dve = Steps("attn_pe", 1), Steps("attn_dve", 3)
        mlp_pe, mlp_act, mlp_dve = Steps("mlp_pe", FT + 1), Steps("mlp_act", FT), Steps("mlp_dve", 1)
        rt_pe, rt_act, rt_dve = Steps("rt_pe", 1), Steps("rt_act", 1), Steps("rt_dve", 8)
        NX1 = E1 + 1
        ex_pe, ex_act, ex_dve = Steps("ex_pe", NX1 * (2 * IT + 1)), Steps("ex_act", NX1 * IT), Steps("ex_dve", NX1 * (IT + 1))

        WKV_PARTS = 15
        TR_BANKS = {0: ((3, 0), (1, 2)), 1: ((0, 1), (2, 3)), 2: ((0, 1), (0, 1)), 3: ((0, 1), (0, 1)), 4: ((0, 1), (2, 3)), 5: ((0, 1), (0, 1))}
        CHAIN = [("embed", 0), ("embed", 1), ("norm", 0), ("kv", 0)] + [("wkv", i) for i in range(WKV_PARTS)] + [("out", 0)]
        CHAIN += [("norm", 1), ("mix_r", 0)] + [("mix_k", j) for j in range(FT)] + [("mix_v", 0)]
        CHAIN += [("norm", 2), ("route0", 0), ("route0", 1)] + [("experts", n) for n in range(0, 16, 2)] + [("experts_b", 0)]
        CHAIN += [("norm", 3)] + [("feat", t) for t in range(TILES)] + [("stab", 0), ("stab", 1), ("stab", 2), ("ctx", 0)]
        CHAIN += [("featT", j) for j in range(FT)] + [("attn", 0), ("norm", 4)] + [("mlp", j) for j in range(FT)] + [("mlp_out", 0)]
        CHAIN += [("norm", 5), ("route1", 0)]
        for i in range(NX1 * IT):
            CHAIN += [("gate", i), ("down", i // IT)] if i % IT == IT - 1 else [("gate", i)]
        TO_MID, TO_OLD = CHAIN.index(("mix_k", 1)), CHAIN.index(("norm", 5))
        NEW, MID, OLD = CHAIN[:TO_MID], CHAIN[TO_MID:TO_OLD], CHAIN[TO_OLD:]
        OTHER = OLD[:1] + [("fetch", 0)] + OLD[1:] + NEW
        WEAVE = (
            0, 2, 2, 3, 1, 1, 1, 1, 2, 1, 4, 1, 2, 3, 2, 1, 1, 1, 1, 1, 1, 1, 1, 2, 2, 1, 1, 2, 1, 2, 2, 3, 7, 3, 1, 1, 1,
            1, 3, 4, 1, 2, 2, 4, 1, 1, 2,
        )
        assert sum(WEAVE[0::2]) == len(OTHER) and sum(WEAVE[1::2]) == len(MID)
        ORDER = []
        for i, run_length in enumerate(WEAVE):
            slots, first = (MID if i % 2 else OTHER), sum(WEAVE[i % 2:i:2])
            ORDER += [(1 - i % 2, *slot) for slot in slots[first:first + run_length]]

        def half_pass(mid, old, new):
            for other, name, k in ORDER:
                chunk = (old if (name, k) in OLD else new) if other else mid
                if chunk is not None:
                    yield name, k, *chunk

        def all_passes(eng, stage):
            def run(mid, old, new):
                for slot in half_pass(mid, old, new):
                    stage(*slot)

            end = (PASSES - 1) * UNIT
            run(None, None, (0, 0))
            run((0, 0), None, (1, 0))
            run((1, 0), (0, 0), (0, UNIT))
            with eng.Fori(UNIT, end, UNIT) as u:
                run((0, u), (1, u - UNIT), (1, u))
                run((1, u), (0, u), (0, u + UNIT))
            run((0, end), (1, end - UNIT), (1, end))
            run((1, end), (0, end), None)
            run(None, (1, end), None)

        block = ctx.enter_context(nc.Block())

        projbd = HV[0][:].rearrange("p q e -> p (q e)")[:, 0:HEADS * MF]

        tab = [b[:, 0:ROWS * CR].rearrange("p (j c) -> p j c", c=CR) for b in (big_a[0], big_b[0], big_a[1], big_b[1])]
        NSQ = ROWS * C
        squares = [ws[:, 0:NSQ], ws[:, NSQ:2 * NSQ]]
        sqsum = ws[:, 2 * NSQ:3 * NSQ]
        emb_main = a["embeddings"][0:MAIN * P, :].rearrange("(p n j) d -> n p j d", p=P, j=ROWS)
        lora_main = a["lora_a"][0:MAIN * P, :].rearrange("(p n j) d -> n p j d", p=P, j=ROWS)
        gram = PS[0][0:RANK, 0, 0:CR]
        gram_sb = small[0][0:RANK, :, :].rearrange("p a b -> p (a b)")[:, 0:CR]
        cross = big_a[0][0:RANK, 0:C]
        colsum = big_a[1][:, 0:C]
        colmag = big_a[1][:, C:2 * C]

        both = [(wo, "WoT"), (ln_cols, "ln_cols"), (ln2_cols, "ln2_cols"), (wu, "wu")]
        loads = [(t[0:P, 0, :], a[n][0:P, :]) for t, n in both] + [(t[0:C1, 1, :], a[n][P:C, :]) for t, n in both]
        loads += [
            (wo[C1:P, 1, :], a["WoT"][P:C, :]), (wu[C1:P, 1, :], a["wu"][P:C, :]),
            (wvf[:], a["WvfT"].rearrange("(j p) c -> p j c", p=P)),
            (w2[:], a["W2"].rearrange("(j p) c -> p j c", p=P)),
            (down[:], a["down"].rearrange("x (j p) c -> p x j c", p=P)),
            (router0_b[:], a["router0_b"]), (experts_b, a["experts_b"]), (b1[:], a["b1"]), (b2, a["b2"]),
            (router1_b[:], a["router1_b"]), (lora_b[:], a["lora_b"]), (iota8[:], a["iota8"].broadcast_to([P, E0])),
            (ln1_rows[:, 0, :], a["ln1_g"].broadcast_to([P, C])), (ln1_rows[:, 1, :], a["ln1_b"].broadcast_to([P, C])),
        ]
        NORM_STEPS = 15 + SEGS

        @block.sync
        def _(sp):
            sp.dma_start(ident[:], a["ident"]).then_inc(ident_in, 16)
            with sp.Fori(0, LOADS // RING) as it:
                for b in range(RING):
                    sp.wait_ge(table_mm, it * RING + (b + 1))
                    sp.wait_ge(table_sq, it * RING + (b + 1))
                    sp.dma_start(tab[b][:, :, 0:C], emb_main[it * RING + b]).then_inc(table_in[b], 16)
                    sp.dma_start(tab[b][:, :, C:CR], lora_main[it * RING + b]).then_inc(table_in[b], 16)
                sp.wait_ge(piece_hi, it + 1)
                sp.wait_ge(piece_lo, it + 1)
                sp.dma_start(wpiece[0], a["wcat"][it, 0:P, :]).then_inc(piece_in, 16)
                sp.dma_start(wpiece[1][0:C1], a["wcat"][it, P:C, :]).then_inc(piece_in, 16)
                sp.dma_start(wpiece[1][C1:P], a["wcat"][it, P:C, :]).then_inc(piece_in, 16)
            sp.wait_ge(table_mm, LOADS + 1)
            sp.wait_ge(table_sq, LOADS + 1)
            sp.dma_start(tab[0][0:TAIL, 0, 0:C], a["embeddings"][MAIN * P:V, :]).then_inc(table_in[0], 16)
            sp.dma_start(tab[0][0:TAIL, 0, C:CR], a["lora_a"][MAIN * P:V, :]).then_inc(table_in[0], 16)

            for s in range(STREAMS):
                sp.sem_inc(idx_in[s], 1)
                sp.sem_inc(stored[s], 1)

            def stage(name, k, s, it):
                n = it // UNIT * STREAMS + s
                if name == "fetch":
                    sp.wait_ge(*embed_pe(s, it, 0))
                    sp.dma_start(idx[s][:], a["idx"][n]).then_inc(idx_in[s], UNIT)
                elif name == "down" and k == NX1 - 1:
                    sp.wait_ge(*ex_dve(s, it, NX1 * (IT + 1)))
                    sp.dma_start(out.rearrange("(n t p) c -> n p t c", p=P, t=TILES)[n], H[s]).then_inc(stored[s], UNIT)

            all_passes(sp, stage)
            for s in range(STREAMS):
                sp.wait_ge(stored[s], UNIT * PASSES + 1)

        @block.gpsimd
        def _(pool):
            def hold(q, value):
                pool.wait_ge(q, value)
                pool.sem_inc(held, 1)

            nc.gpsimd.memset(projbd, 0.0).then_inc(const_pool, 1)
            nc.gpsimd.memset(ones[:], 1.0).then_inc(const_pool, 1)
            nc.gpsimd.memset(feat_eps[:], FEAT_EPS).then_inc(const_pool, 1)
            nc.gpsimd.memset(half[:], -0.5).then_inc(const_pool, 1)
            nc.gpsimd.memset(eps_t[:], LN_EPS).then_inc(const_pool, 1)
            nc.gpsimd.memset(HV[1][:], 1.0).then_inc(const_pool, 1)
            for s in range(STREAMS):
                nc.gpsimd.memset(CTX[s][:], 0.0).then_inc(const_pool, 1)
            pool.wait_ge(const_pool, 1)
            for h in range(HEADS):
                for r in ((h * DH,) if h < HK0 else ((h - HK0) * DH, (h - HK0) * DH + C1)):
                    pool.dma_start(projbd[r:r + DH, h * MF:(h + 1) * MF], a["projT"]).then_inc(proj_set, 16)
            for dst, src in loads:
                pool.dma_start(dst, src).then_inc(loaded, 16)
            pool.wait_ge(norm_dve, 1)
            pool.dma_start(colmag, a["magnitude"].broadcast_to([P, C])).then_inc(mag_in, 16)

            for f in (ln0_pool, hadd, ln_pool, ln3_pool):
                f.credit(pool)

            def power(s, i_out, in0, q):
                nc.gpsimd.tensor_tensor(rstd[s][:, i_out, :], in0, half[:], ALU.pow).then_inc(*q)

            def ln_twice(f_dve, f_pool, k_dve, s, it):
                pool.wait_ge(*f_dve(s, it, k_dve))
                power(s, 0, rstd[s][:, 3, :], f_pool.step(s))
                pool.wait_ge(*f_pool(s, it, 1))
                nc.gpsimd.tensor_tensor(rstd[s][:, 1, :], rstd[s][:, 0, :], rstd[s][:, 0, :], ALU.mult).then_inc(*f_pool.step(s))
                pool.wait_ge(*f_pool(s, it, 2))
                nc.gpsimd.tensor_tensor(rstd[s][:, 1, :], rstd[s][:, 1, :], mv[s][:, :, 1], ALU.mult).then_inc(*f_pool.step(s))
                pool.wait_ge(*f_pool(s, it, 3))
                nc.gpsimd.tensor_tensor(rstd[s][:, 1, :], rstd[s][:, 1, :], eps_t[:], ALU.add).then_inc(*f_pool.step(s))
                pool.wait_ge(*f_pool(s, it, 4))
                power(s, 2, rstd[s][:, 1, :], f_pool.step(s))

            def ln_once(i, s, it):
                pool.wait_ge(*ln_dve(s, it, 4 * i + 3))
                power(s, 0, rstd[s][:, 3, :], ln_pool.step(s))

            def add_resid(f, k, s, it):
                pool.wait_ge(*f(s, it, k))
                nc.gpsimd.tensor_tensor(H[s], H[s], XA[s], ALU.add).then_inc(*hadd.step(s))

            def stage(name, k, s, it):
                if name == "fetch":
                    hold(idx_in[s], it + (UNIT + 1))
                    hold(*ln_dve(s, it, 0))
                    hold(*hadd(s, it, 0))
                    hold(*embed_pe(s, it, 0))
                    for t in range(TILES):
                        off = bass.IndirectOffsetOnAxis(idx[s][:, t:t + 1], 0)
                        pool.indirect_dma_start(out=grow[s][:, t, :], out_offset=None, in_=a["embeddings"],
                                                in_offset=off).then_inc(row_in[s], 16)
                        pool.indirect_dma_start(out=glora[s][:, t, :], out_offset=None, in_=a["lora_a"],
                                                in_offset=off).then_inc(row_in[s], 16)
                elif (name, k) == ("embed", 1):
                    ln_twice(ln0_dve, ln0_pool, 5, s, it)
                elif name == "out":
                    add_resid(out_dve, 1, s, it)
                    ln_once(0, s, it)
                elif name == "mix_v":
                    ln_once(1, s, it)
                elif name == "experts_b":
                    ln_twice(ln3_dve, ln3_pool, 3, s, it)
                elif name == "attn":
                    add_resid(attn_dve, 3, s, it)
                    ln_once(2, s, it)
                elif name == "mlp_out":
                    ln_once(3, s, it)

            pool.wait_ge(piece_lo, PIECES + 1)
            all_passes(pool, stage)

        @block.scalar
        def _(act):
            for f in (embed_act, ev, kv_act, wkv_act, ff_act, moe_act, feat_act, stab_act, et_act, mlp_act, rt_act, ex_act):
                f.credit(act)
            act.sem_inc(table_sq, RING)
            act.sem_inc(piece_hi, 1)

            with act.Fori(0, LOADS // RING) as it:
                for b in range(RING):
                    act.wait_ge(table_in[b], it * 32 + 32)
                    act.wait_ge(table_add, it * RING + (b + 1))
                    nc.scalar.activation(squares[b % 2].rearrange("p (j c) -> p j c", c=C), tab[b][:, :, 0:C],
                                         ACT.Square).then_inc(table_sq, 1)
                act.wait_ge(piece_in, it * 48 + 48)
                nc.scalar.activation(wcat[:, 0, bass.ds(it * PIECE, PIECE)], wpiece[0], ACT.Copy, scale=WSCALE)
                nc.scalar.activation(wcat[:, 2, bass.ds(it * PIECE, PIECE)], wpiece[1], ACT.Copy, scale=WSCALE).then_inc(piece_hi, 1)
            act.wait_ge(table_in[0], LOADS // RING * 32 + 32)
            act.wait_ge(table_add, LOADS + 1)
            nc.scalar.activation(squares[0][0:TAIL, 0:C], tab[0][0:TAIL, 0, 0:C], ACT.Square).then_inc(table_sq, 1)
            act.wait_ge(table_mm, RING + LOADS + 1)
            nc.scalar.activation(gram_sb, gram, ACT.Copy).then_inc(norm_act, 1)
            act.wait_ge(norm_pe, 2)
            nc.scalar.activation(colsum, PS[0][:, 2, 0:C], ACT.Sqrt).then_inc(norm_act, 1)
            act.wait_ge(loaded, 16 * len(loads))
            act.wait_ge(norm_dve, NORM_STEPS)
            AFFINE = {0: (ln_cols, 0), 1: (ln_cols, 2), 4: (ln2_cols, 0)}

            def stage(name, k, s, it):
                bank = PS[s]
                if (name, k) == ("embed", 0):
                    act.wait_ge(*embed_pe(s, it, 1))
                    nc.scalar.activation(big_a[s][0:RANK, 0:CHUNK], bank[0:RANK, 0, :], ACT.Copy).then_inc(*embed_act.step(s))

                elif name == "norm":
                    src, full = TR_BANKS[k]
                    act.wait_ge(*tr(s, it, k + 1))
                    for part, rows in ((0, P), (1, C1)):
                        v, dst = bank[0:rows, src[part], :], xh[s][0:rows, 2 * part, :]
                        if k in AFFINE:
                            cols, c = AFFINE[k]
                            sc, sh = cols[0:rows, part, c:c + 1], cols[0:rows, part, c + 1:c + 2]
                            nc.scalar.activation(bank[0:rows, full[part], :], v, ACT.Identity, bias=sh, scale=sc)
                            last = nc.scalar.activation(dst, v, ACT.Identity, bias=sh, scale=sc)
                        else:
                            last = nc.scalar.activation(dst, v, ACT.Copy)
                    last.then_inc(*ev.step(s))

                elif name == "kv":
                    act.wait_ge(*kv_pe(s, it, 1))
                    if s == 0:
                        act.wait_ge(*wkv_dve(1, it, 0))
                    else:
                        act.wait_ge(*wkv_dve(0, it, 28))
                    for g, src in ((slice(0, 2), bank[:, 1, :]), (slice(2, 3), bank[:, 2, 0:SEQ])):
                        src = src.rearrange("p (g t) -> p g t", t=SEQ)
                        nc.scalar.activation(data(K)[:, 0, g, :], src, ACT.Copy, scale=1.0 / WSCALE)
                        col = 0 if g.start == 0 else 1
                        last = nc.scalar.activation(data(KU)[:, 0, g, :], src, ACT.Identity, bias=wu[:, col, 1:2], scale=1.0 / WSCALE)
                    last.then_inc(*kv_act.step(s))
                    for g, src in ((slice(0, 2), bank[:, 3, :]), (slice(2, 3), bank[:, 2, SEQ:2 * SEQ])):
                        last = nc.scalar.activation(data(VV)[:, 0, g, :], src.rearrange("p (g t) -> p g t", t=SEQ), ACT.Copy, scale=1.0 / WSCALE)
                    last.then_inc(*kv_act.step(s))
                    act.wait_ge(*kv_pe(s, it, 2))
                    nc.scalar.activation(exp_r[s][:, 0:CHUNK], bank[:, 0, :], ACT.Exp, scale=-1.0 / WSCALE)
                    nc.scalar.activation(exp_r[s][:, CHUNK:CHUNK + SEQ], bank[:, 1, 0:SEQ], ACT.Exp, scale=-1.0 / WSCALE).then_inc(*kv_act.step(s))

                elif name == "wkv" and k in (2, 3):
                    act.wait_ge(*wkv_dve(s, it, 4 + 2 * (k - 2)))
                    v = data(DECAYS[k - 2]).rearrange("p n g t -> p (n g) t")
                    nc.scalar.activation(v, v, ACT.Exp).then_inc(*wkv_act.step(s))
                elif (name, k) == ("wkv", 5):
                    act.wait_ge(*wkv_dve(s, it, 11))
                    v = big_a[s][:, 0:3 * SEGS * SEQ]
                    nc.scalar.activation(v, v, ACT.Exp).then_inc(*wkv_act.step(s))

                elif name == "mix_r":
                    act.wait_ge(*ff_pe(s, it, 1))
                    nc.scalar.activation(NX[s].rearrange("p (b t) c -> p b (t c)", b=2), bank[:, 2:4, 0:2 * C], ACT.Sigmoid,
                                         scale=1.0 / WSCALE).then_inc(*ff_act.step(s))
                elif name == "mix_k":
                    act.wait_ge(*ff_pe(s, it, 2 + k))
                    v = big_a[s][:, k * CHUNK:(k + 1) * CHUNK]
                    nc.scalar.activation(v, bank[:, k % 2, :], ACT.Relu, scale=1.0 / WSCALE).then_inc(*ff_act.step(s))
                    act.wait_ge(*ff_act(s, it, 2 + 2 * k))
                    nc.scalar.activation(v, v, ACT.Square).then_inc(*ff_act.step(s))

                elif (name, k) == ("route0", 0):
                    act.wait_ge(*moe_dve(s, it, 4))
                    nc.scalar.activation(small[s][:, 3, :], small[s][:, 2, :], ACT.Exp).then_inc(*moe_act.step(s))

                elif name == "feat":
                    if k == 0:
                        act.wait_ge(*tr(s, it, 4))
                        nc.scalar.activation(NX[s].rearrange("p t (h d) -> p (t h) d", d=DH), HV[s][:, :, 0:DH], ACT.Square,
                                             scale=float(DH) ** -0.25).then_inc(*feat_act.step(s))
                    act.wait_ge(*feat_dve(s, it, 1 + 3 * (k + 1)))
                    v = big_a[s][:, k * HEADS * MF:(k + 1) * HEADS * MF]
                    nc.scalar.activation(v, v, ACT.Exp).then_inc(*feat_act.step(s))
                elif (name, k) == ("stab", 2):
                    act.wait_ge(*stab_dve(s, it, 3))
                    nc.scalar.activation(stab[s][:, 2, :], stab[s][:, 2, :], ACT.Exp).then_inc(*stab_act.step(s))
                elif name == "featT":
                    act.wait_ge(*et_pe(s, it, k + 1))
                    nc.scalar.activation(big_b[s][:, k * CHUNK:(k + 1) * CHUNK], bank[:, k % 2, :], ACT.Copy, bias=FEAT_EPS).then_inc(*et_act.step(s))

                elif name == "mlp":
                    act.wait_ge(*mlp_pe(s, it, k + 1))
                    nc.scalar.activation(big_a[s][:, k * CHUNK:(k + 1) * CHUNK], bank[:, k % 2, :], ACT.Gelu, bias=b1[:, k:k + 1],
                                         scale=1.0 / WSCALE).then_inc(*mlp_act.step(s))
                elif name == "route1":
                    act.wait_ge(*rt_pe(s, it, 1))
                    nc.scalar.activation(small[s][:, 0, 0:TILES * E1], bank[:, 2, 0:TILES * E1], ACT.Sigmoid, scale=1.0 / WSCALE).then_inc(*rt_act.step(s))
                elif name == "gate":
                    x, j = divmod(k, IT)
                    act.wait_ge(*ex_pe(s, it, x * (2 * IT + 1) + 2 * j + 1))
                    if x > 0:
                        act.wait_ge(*ex_dve(s, it, (x - 1) * (IT + 1) + j + 1))
                    nc.scalar.activation(big_a[s][:, j * CHUNK:(j + 1) * CHUNK], bank[:, 0, :], ACT.Silu, scale=1.0 / WSCALE).then_inc(*ex_act.step(s))

            all_passes(act, stage)

        @block.vector
        def _(dve):
            def hold(q, value):
                dve.wait_ge(q, value)
                dve.sem_inc(held, 1)

            for f in (ln0_dve, lo, wkv_dve, out_dve, ln_dve, ff_dve, moe_dve, mix, ln3_dve, feat_dve, stab_dve, ctx_dve, attn_dve, mlp_dve, rt_dve, ex_dve):
                f.credit(dve)
            dve.sem_inc(table_add, 2)
            dve.sem_inc(piece_lo, 1)
            nc.vector.memset(sqsum, 0.0).then_inc(const_dve, 1)
            dve.wait_ge(const_dve, 1)
            with dve.Fori(0, LOADS // RING) as it:
                for b in range(RING):
                    dve.wait_ge(table_sq, it * RING + (RING + b + 1))
                    dve.wait_ge(table_add, it * RING + (b + 2))
                    nc.vector.tensor_tensor(sqsum, sqsum, squares[b % 2], ALU.add).then_inc(table_add, 1)
                dve.wait_ge(piece_hi, it + 2)
                nc.vector.scalar_tensor_tensor(out=wcat[:, 1, bass.ds(it * PIECE, PIECE)], in0=wpiece[0], scalar=WSCALE,
                                               in1=wcat[:, 0, bass.ds(it * PIECE, PIECE)], op0=ALU.mult, op1=ALU.subtract)
                nc.vector.scalar_tensor_tensor(out=wcat[:, 3, bass.ds(it * PIECE, PIECE)], in0=wpiece[1], scalar=WSCALE,
                                               in1=wcat[:, 2, bass.ds(it * PIECE, PIECE)], op0=ALU.mult, op1=ALU.subtract).then_inc(piece_lo, 1)
            dve.wait_ge(table_sq, RING + LOADS + 1)
            dve.wait_ge(table_add, LOADS + 2)
            nc.vector.tensor_tensor(sqsum[0:TAIL, 0:C], sqsum[0:TAIL, 0:C], squares[0][0:TAIL, 0:C], ALU.add).then_inc(table_add, 1)
            dve.wait_ge(table_add, LOADS + 3)
            dve.wait_ge(table_mm, RING + LOADS + 1)
            nc.vector.tensor_reduce(colsum, sqsum.rearrange("p (j c) -> p c j", c=C), AX.X, ALU.add).then_inc(norm_dve, 1)
            dve.wait_ge(loaded, 16 * len(loads))
            dve.wait_ge(norm_act, 1)
            dve.wait_ge(norm_pe, 1)
            nc.vector.tensor_scalar(cross, gram_sb[:, 0:C], 2.0 / LORA_SCALE, None, ALU.mult).then_inc(norm_dve, 1)
            dve.wait_ge(norm_dve, 2)
            nc.vector.tensor_tensor(cross, cross, PS[0][0:RANK, 1, 0:C], ALU.add).then_inc(norm_dve, 1)
            dve.wait_ge(norm_dve, 3)
            nc.vector.scalar_tensor_tensor(out=cross, in0=cross, scalar=LORA_SCALE * LORA_SCALE, in1=lora_b[:], op0=ALU.mult, op1=ALU.mult).then_inc(norm_dve, 1)
            dve.wait_ge(norm_dve, 4)
            nc.vector.tensor_scalar(lora_b[:], lora_b[:], LORA_SCALE, None, ALU.mult).then_inc(const_dve, 1)
            dve.wait_ge(proj_set, 16 * (HEADS + HEADS - HK0))
            for dst, src in ((proj0, projbd[:, 0:HK0 * MF]), (proj1, projbd[:, HK0 * MF:HEADS * MF])):
                nc.vector.tensor_scalar(dst[:, 0, :], src, float(DH) ** -0.25, None, ALU.mult).then_inc(proj_dve, 1)
            dve.wait_ge(proj_dve, 2)
            for dst, src in ((proj0, projbd[:, 0:HK0 * MF]), (proj1, projbd[:, HK0 * MF:HEADS * MF])):
                nc.vector.scalar_tensor_tensor(out=dst[:, 1, :], in0=src, scalar=float(DH) ** -0.25, in1=dst[:, 0, :],
                                               op0=ALU.mult, op1=ALU.subtract).then_inc(proj_dve, 1)
            dve.wait_ge(proj_dve, 4)
            nc.vector.memset(HV[0][:], 1.0).then_inc(const_dve, 1)
            for bias in (experts_b, router0_b[:], router1_b[:]):
                nc.vector.tensor_scalar(bias, bias, WSCALE, None, ALU.mult).then_inc(proj_dve, 1)
            dve.wait_ge(norm_act, 2)
            nc.vector.tensor_scalar(colsum, colsum, 1e-8, None, ALU.max).then_inc(norm_dve, 1)
            dve.wait_ge(norm_dve, 5)
            nc.vector.reciprocal(colsum, colsum).then_inc(norm_dve, 1)
            dve.wait_ge(norm_dve, 6)
            dve.wait_ge(mag_in, 16)
            nc.vector.tensor_tensor(gscale[:], colsum, colmag, ALU.mult).then_inc(norm_dve, 1)
            pads = ws[:].rearrange("p (n t) -> p n t", t=SEGW)
            for edge in (0, SEGW - 1):
                nc.vector.memset(pads[:, :, edge], 0.0).then_inc(norm_dve, 1)
            nc.vector.memset(decay_row[:], 0.0).then_inc(norm_dve, 1)
            nc.vector.tensor_scalar(wu[:], wu[:], 1.0 / SEQ, None, ALU.mult).then_inc(norm_dve, 1)
            dve.wait_ge(norm_dve, NORM_STEPS - 4 - SEGS)
            for edge in (0, SEGW - 1):
                nc.vector.memset(K[:, 0, :, edge], NEG).then_inc(norm_dve, 1)
                nc.vector.memset(decay_row[:, :, edge], 2 * NEG).then_inc(norm_dve, 1)
            for g in range(SEGS):
                data_cols = decay_row[:, g, 1:SEQ + 1]
                nc.vector.tensor_scalar(data_cols, data_cols, wu[:, g // 2, 0:1], None, ALU.add).then_inc(norm_dve, 1)
            dve.wait_ge(norm_dve, NORM_STEPS)
            dve.wait_ge(proj_dve, 7)
            dve.wait_ge(const_dve, 3)

            def ln_stats(f, s, it, k, x):
                for t in range(TILES):
                    last = nc.vector.bn_stats(stats[s][:, t, :], x[:, t, :])
                last.then_inc(*f.step(s))
                hold(*f(s, it, k + 1))
                for t in range(TILES):
                    last = nc.vector.bn_aggr(mv[s][:, t, :], stats[s][:, t, :])
                last.then_inc(*f.step(s))
                dve.wait_ge(*f(s, it, k + 2))
                nc.vector.tensor_scalar(rstd[s][:, 3, :], mv[s][:, :, 1], LN_EPS, None, ALU.add).then_inc(*f.step(s))

            def apply(dst, x, s):
                for t in range(TILES):
                    last = nc.vector.tensor_scalar(dst[s][:, t, :], x[s][:, t, :], mv[s][:, t, 0:1], rstd[s][:, 0, t:t + 1], ALU.subtract, ALU.mult)
                return last

            def two(v):
                return v.rearrange("p (b t) c -> p b (t c)", b=2)

            def stage(name, k, s, it):
                bank = PS[s]
                if (name, k) == ("embed", 1):
                    q = ln0_dve
                    dve.wait_ge(row_in[s], it + UNIT)
                    dve.wait_ge(*embed_pe(s, it, 2))
                    dve.wait_ge(stored[s], it + 1)
                    nc.vector.tensor_tensor(two(H[s]), two(grow[s]), bank[:, 1:3, 0:2 * C], ALU.add).then_inc(*q.step(s))
                    dve.wait_ge(*q(s, it, 1))
                    nc.vector.tensor_tensor(H[s], H[s], gscale[:].unsqueeze(1).broadcast_to([P, TILES, C]), ALU.mult).then_inc(*q.step(s))
                    dve.wait_ge(*q(s, it, 2))
                    ln_stats(q, s, it, 2, H[s])

                elif name == "norm":
                    if k == 0:
                        q = ln0_dve
                        dve.wait_ge(*ln0_pool(s, it, 5))
                        apply(XA, H, s).then_inc(*q.step(s))
                        dve.wait_ge(*q(s, it, 6))
                        dve.wait_ge(*tr(s, it, 0))
                        for t in range(TILES):
                            last = nc.vector.tensor_scalar(NX[s][:, t, :], XA[s][:, t, :], rstd[s][:, 2, t:t + 1], None, ALU.mult)
                        last.then_inc(*q.step(s))
                    elif k == 3:
                        q = ln3_dve
                        dve.wait_ge(*ln3_pool(s, it, 5))
                        apply(XA, H, s).then_inc(*q.step(s))
                        dve.wait_ge(*q(s, it, 4))
                        for t in range(TILES):
                            last = nc.vector.tensor_scalar(NX[s][:, t, :], XA[s][:, t, :], rstd[s][:, 2, t:t + 1], None, ALU.mult)
                        last.then_inc(*q.step(s))
                        for n, op in ((0, ALU.mult), (1, ALU.add)):
                            dve.wait_ge(*q(s, it, 5 + n))
                            nc.vector.tensor_tensor(NX[s], NX[s], ln1_rows[:, n, :].unsqueeze(1).broadcast_to([P, TILES, C]), op).then_inc(*q.step(s))
                        dve.wait_ge(*q(s, it, 7))
                        nc.vector.tensor_copy(HV[s][:, :, 0:DH], NX[s].rearrange("p t (h d) -> p (t h) d", d=DH)).then_inc(*q.step(s))
                    else:
                        i = {1: 0, 2: 1, 4: 2, 5: 3}[k]
                        dve.wait_ge(*ln_pool(s, it, i + 1))
                        apply(NX, XA if k in (1, 4) else H, s).then_inc(*ln_dve.step(s))
                    src, full = TR_BANKS[k]
                    dve.wait_ge(*ev(s, it, k + 1))
                    nc.vector.tensor_tensor(xh[s][:, 1, :], bank[:, full[0], :], xh[s][:, 0, :], ALU.subtract)
                    nc.vector.tensor_tensor(xh[s][C1:P, 2, :], bank[0:C1, full[1], :], xh[s][0:C1, 2, :], ALU.subtract).then_inc(*lo.step(s))

                elif name == "wkv":
                    q = wkv_dve
                    n3 = SEGS * SEQ
                    args = big_a[s][:, 0:3 * n3].rearrange("p (n g t) -> p n g t", n=3, g=SEGS)
                    mxv = big_b[s][:, 2 * n3:3 * n3].rearrange("p (g t) -> p g t", g=SEGS)
                    prev = [MAXES[0][:, 0, :, 0:SEQ], MAXES[1][:, 0, :, 2:SEQ + 2]]
                    decay = decay_row[:].rearrange("p g t -> p (g t)")
                    tot = big_b[s][:, 0:2 * n3].rearrange("p (n g t) -> p n g t", n=2, g=SEGS)
                    oth = big_b[s][:, 2 * n3:4 * n3].rearrange("p (n g t) -> p n g t", n=2, g=SEGS)
                    den, rec = big_b[s][:, n3:2 * n3], big_b[s][:, 3 * n3:4 * n3]
                    if k == 0:
                        dve.wait_ge(*kv_act(s, it, 1))
                        nc.vector.tensor_tensor_scan(flat(MAXES[0]), decay, flat(K), NEG, ALU.add, ALU.max).then_inc(*q.step(s))
                    elif k == 1:
                        nc.vector.tensor_tensor_scan(flat(MAXES[1])[:, ::-1], decay[:, ::-1], flat(K)[:, ::-1], NEG, ALU.add, ALU.max).then_inc(*q.step(s))
                    elif k in (2, 3):
                        d = k - 2
                        old, new = data(DECAYS[d])[:, 0], data(DECAYS[d])[:, 1]
                        dve.wait_ge(*q(s, it, 1 + d))
                        for g, col in ((slice(0, 2), 0), (slice(2, 3), 1)):
                            last = nc.vector.scalar_tensor_tensor(out=old[:, g], in0=prev[d][:, g], scalar=wu[:, col, 0:1], in1=data(MAXES[d])[:, 0, g],
                                                                  op0=ALU.add, op1=ALU.subtract)
                        last.then_inc(*q.step(s))
                        nc.vector.tensor_tensor(new, data(K)[:, 0], data(MAXES[d])[:, 0], ALU.subtract).then_inc(*q.step(s))
                    elif k == 4:
                        dve.wait_ge(*q(s, it, 2))
                        nc.vector.tensor_tensor(mxv, data(KU)[:, 0], prev[0], ALU.max).then_inc(*q.step(s))
                        dve.wait_ge(*q(s, it, 7))
                        nc.vector.tensor_tensor(mxv, mxv, prev[1], ALU.max).then_inc(*q.step(s))
                    elif k == 5:
                        dve.wait_ge(*q(s, it, 8))
                        for n, v in enumerate((prev[0], prev[1], data(KU)[:, 0])):
                            nc.vector.tensor_tensor(args[:, n], v, mxv, ALU.subtract).then_inc(*q.step(s))
                    elif k in (6, 7):
                        d = k - 6
                        e_old, e_new = flat(DECAYS[d][:, 0:1]), flat(DECAYS[d][:, 1:2])
                        num = flat(SUMS[d][0])
                        dve.wait_ge(*kv_act(s, it, 2))
                        dve.wait_ge(*wkv_act(s, it, 1 + d))
                        nc.vector.tensor_tensor(num, e_new, flat(VV), ALU.mult).then_inc(*q.step(s))
                        dve.wait_ge(*q(s, it, 12 + 3 * d))
                        if d:
                            e_old, e_new, num = e_old[:, ::-1], e_new[:, ::-1], num[:, ::-1]
                        nc.vector.tensor_tensor_scan(e_new, e_old, e_new, 0.0, ALU.mult, ALU.add).then_inc(*q.step(s))
                        nc.vector.tensor_tensor_scan(num, e_old, num, 0.0, ALU.mult, ALU.add).then_inc(*q.step(s))
                    elif k in (8, 9):
                        d = k - 8
                        dve.wait_ge(*wkv_act(s, it, 3))
                        dve.wait_ge(*q(s, it, 14 + 3 * d))
                        for n in range(2):
                            last = nc.vector.tensor_tensor((tot, oth)[d][:, n], SUMS[d][n][:, 0, :, 2 * d:2 * d + SEQ], args[:, d], ALU.mult)
                        last.then_inc(*q.step(s))
                    elif k == 10:
                        dve.wait_ge(*q(s, it, 19))
                        nc.vector.tensor_tensor(big_b[s][:, 0:2 * n3], big_b[s][:, 0:2 * n3], big_b[s][:, 2 * n3:4 * n3], ALU.add).then_inc(*q.step(s))
                    elif k == 11:
                        dve.wait_ge(*q(s, it, 20))
                        nc.vector.tensor_tensor(oth[:, 0], args[:, 2], data(VV)[:, 0], ALU.mult).then_inc(*q.step(s))
                        nc.vector.tensor_tensor(tot[:, 1], tot[:, 1], args[:, 2], ALU.add).then_inc(*q.step(s))
                        dve.wait_ge(*q(s, it, 21))
                        nc.vector.tensor_tensor(tot[:, 0], tot[:, 0], oth[:, 0], ALU.add).then_inc(*q.step(s))
                    elif k in (12, 13):
                        if k == 12:
                            dve.wait_ge(*q(s, it, 22))
                            dve.wait_ge(*kv_act(s, it, 3))
                            nc.vector.scalar_tensor_tensor(out=den, in0=exp_r[s][:, 0:n3], scalar=1.0, in1=den, op0=ALU.add, op1=ALU.mult).then_inc(*q.step(s))
                            dve.wait_ge(*q(s, it, 24))
                        for n in ((0,) if k == 12 else (1, 2)):
                            nc.vector.reciprocal(rec[:, n * SEQ:(n + 1) * SEQ], den[:, n * SEQ:(n + 1) * SEQ]).then_inc(*q.step(s))
                    else:
                        dve.wait_ge(*q(s, it, 27))
                        nc.vector.tensor_tensor(big_b[s][:, 0:n3], big_b[s][:, 0:n3], rec, ALU.mult).then_inc(*q.step(s))

                elif name == "out":
                    dve.wait_ge(*out_pe(s, it, 1))
                    nc.vector.tensor_tensor(two(XA[s]), two(XA[s]), bank[:, 2:4, 0:2 * C], ALU.add).then_inc(*out_dve.step(s))
                    dve.wait_ge(*out_dve(s, it, 1))
                    ln_stats(ln_dve, s, it, 0, XA[s])

                elif name == "mix_v":
                    dve.wait_ge(*ff_pe(s, it, 2 + FT))
                    nc.vector.tensor_tensor(two(NX[s]), two(NX[s]), bank[:, 2:4, 0:2 * C], ALU.mult).then_inc(*ff_dve.step(s))
                    dve.wait_ge(*ff_dve(s, it, 1))
                    dve.wait_ge(*hadd(s, it, 1))
                    nc.vector.tensor_tensor(H[s], H[s], NX[s], ALU.add).then_inc(*ff_dve.step(s))
                    dve.wait_ge(*ff_dve(s, it, 2))
                    ln_stats(ln_dve, s, it, 4, H[s])

                elif (name, k) == ("route0", 0):
                    def sm(n):
                        return small[s][:, n, :].rearrange("p (t e) -> p t e", t=TILES)

                    def per_tile(n):
                        return small[s][:, n, 0:TILES]

                    q = moe_dve
                    dve.wait_ge(*moe_pe(s, it, 1))
                    nc.vector.tensor_scalar(small[s][:, 0, :], bank[:, 2, 0:TILES * E0], 1.0 / WSCALE, None, ALU.mult).then_inc(*q.step(s))
                    hold(*q(s, it, 1))
                    for t in range(TILES):
                        last = nc.vector.max(sm(1)[:, t, :], sm(0)[:, t, :])
                    last.then_inc(*q.step(s))
                    hold(*q(s, it, 2))
                    for t in range(TILES):
                        last = nc.vector.max_index(idx8[s][:, t, :], sm(1)[:, t, :], sm(0)[:, t, :])
                    last.then_inc(*q.step(s))
                    nc.vector.tensor_tensor(sm(2), sm(0), sm(1)[:, :, 0:1].broadcast_to([P, TILES, E0]), ALU.subtract).then_inc(*q.step(s))
                    dve.wait_ge(*q(s, it, 3))
                    nc.vector.tensor_copy(sm(4), idx8[s][:]).then_inc(*q.step(s))
                    dve.wait_ge(*q(s, it, 5))
                    iota = iota8[:].unsqueeze(1).broadcast_to([P, TILES, E0])
                    for n in range(2):
                        nc.vector.tensor_tensor(sm(5 + n), iota, sm(4)[:, :, n:n + 1].broadcast_to([P, TILES, E0]), ALU.is_equal).then_inc(*q.step(s))
                    dve.wait_ge(*q(s, it, 7))
                    nc.vector.tensor_tensor(sm(5), sm(5), sm(6), ALU.add).then_inc(*q.step(s))
                    dve.wait_ge(*q(s, it, 8))
                    dve.wait_ge(*moe_act(s, it, 1))
                    nc.vector.tensor_tensor(sm(5), sm(5), sm(3), ALU.mult).then_inc(*q.step(s))
                    nc.vector.tensor_reduce(per_tile(7), sm(3), AX.X, ALU.add).then_inc(*q.step(s))
                    dve.wait_ge(*q(s, it, 9))
                    nc.vector.tensor_reduce(per_tile(8), sm(5), AX.X, ALU.add).then_inc(*q.step(s))
                    dve.wait_ge(*q(s, it, 11))
                    nc.vector.scalar_tensor_tensor(out=per_tile(7), in0=per_tile(7), scalar=1e-9, in1=per_tile(8), op0=ALU.mult, op1=ALU.add).then_inc(*q.step(s))
                    dve.wait_ge(*q(s, it, 12))
                    nc.vector.reciprocal(per_tile(8), per_tile(7)).then_inc(*q.step(s))
                    dve.wait_ge(*q(s, it, 13))
                    nc.vector.scalar_tensor_tensor(out=sm(9), in0=sm(5), scalar=1.0 / WSCALE, in1=per_tile(8).unsqueeze(2).broadcast_to([P, TILES, E0]),
                                                   op0=ALU.mult, op1=ALU.mult).then_inc(*q.step(s))
                elif name == "route0":
                    dve.wait_ge(*moe_pe(s, it, 2))
                    nc.vector.tensor_copy(wT[s], bank[0:E0, 3, :]).then_inc(*moe_dve.step(s))
                elif name == "experts":
                    w = small[s][:, 9, :].rearrange("p (t e) -> p t e", t=TILES)
                    for n in (k, k + 1):
                        e2, t = divmod(n, TILES)
                        dve.wait_ge(*moe_pe(s, it, 2 + n + 1))
                        for side in range(2):
                            if side or e2:
                                dve.wait_ge(*mix(s, it, 2 * n + 1 if side else 2 * (n - TILES) + 2))
                            e = 2 * e2 + side
                            nc.vector.scalar_tensor_tensor(out=H[s][:, t, :], in0=bank[:, n % 2, side * C:(side + 1) * C], scalar=w[:, t, e:e + 1],
                                                           in1=H[s][:, t, :], op0=ALU.mult, op1=ALU.add).then_inc(*mix.step(s))
                elif name == "experts_b":
                    dve.wait_ge(*moe_pe(s, it, 2 + 16 + 1))
                    dve.wait_ge(*mix(s, it, 32))
                    nc.vector.tensor_tensor(two(H[s]), two(H[s]), bank[:, 2:4, 0:2 * C], ALU.add).then_inc(*mix.step(s))
                    dve.wait_ge(*mix(s, it, 33))
                    ln_stats(ln3_dve, s, it, 0, H[s])

                elif name == "feat":
                    q = feat_dve
                    if k == 0:
                        dve.wait_ge(*feat_act(s, it, 1))
                        nc.vector.tensor_reduce(stab[s][:, 1, :], NX[s].rearrange("p t (h d) -> p (t h) d", d=DH), AX.X, ALU.add).then_inc(*q.step(s))
                    b, n = 2 * (k % 2), 1 + 3 * k
                    sl = slice(k * HEADS, (k + 1) * HEADS)
                    uv = bank[:, b:b + 2, :].rearrange("p b c -> p (b c)")[:, 0:HEADS * MF].rearrange("p (h m) -> p h m", m=MF)
                    dve.wait_ge(*feat_pe(s, it, k + 1))
                    nc.vector.tensor_reduce(stab[s][:, 0, sl], uv, AX.X, ALU.max).then_inc(*q.step(s))
                    dve.wait_ge(*q(s, it, n + 1))
                    nc.vector.scalar_tensor_tensor(out=stab[s][:, 3, sl], in0=stab[s][:, 1, sl], scalar=0.5, in1=stab[s][:, 0, sl],
                                                   op0=ALU.mult, op1=ALU.add).then_inc(*q.step(s))
                    dve.wait_ge(*q(s, it, n + 2))
                    nc.vector.tensor_tensor(big_a[s][:, k * HEADS * MF:(k + 1) * HEADS * MF].rearrange("p (h m) -> p h m", m=MF), uv,
                                            stab[s][:, 3, sl].unsqueeze(2).broadcast_to([P, HEADS, MF]), ALU.subtract).then_inc(*q.step(s))
                elif (name, k) == ("stab", 0):
                    dve.wait_ge(*stab_pe(s, it, 1))
                    nc.vector.tensor_reduce(stabT[s][:, :, 0], bank[0:HEADS, 0, :].rearrange("h (b n) -> h b n", b=2), AX.X, ALU.max).then_inc(*stab_dve.step(s))
                    dve.wait_ge(*stab_dve(s, it, 1))
                    nc.vector.tensor_tensor(stabT[s][:, :, 1:1 + HEADS], ident[0:HEADS, 0:HEADS].unsqueeze(1).broadcast_to([HEADS, 2, HEADS]),
                                            stabT[s][:, :, 0:1].broadcast_to([HEADS, 2, HEADS]), ALU.mult).then_inc(*stab_dve.step(s))
                elif (name, k) == ("stab", 2):
                    dve.wait_ge(*stab_pe(s, it, 2))
                    nc.vector.tensor_tensor(stab[s][:, 2, :].rearrange("p (b t h) -> p b t h", b=2, t=2), stab[s][:, 0, :].rearrange("p (b t h) -> p b t h", b=2, t=2),
                                            bank[:, 1, 0:2 * HEADS].rearrange("p (b h) -> p b h", b=2).unsqueeze(2).broadcast_to([P, 2, 2, HEADS]),
                                            ALU.subtract).then_inc(*stab_dve.step(s))
                    dve.wait_ge(*stab_act(s, it, 1))
                    nc.vector.tensor_tensor(CV[s], HV[s][:], stab[s][:, 2, :].unsqueeze(2).broadcast_to([P, TILES * HEADS, HV1]), ALU.mult).then_inc(*stab_dve.step(s))
                elif name == "ctx":
                    dve.wait_ge(*ctx_pe(s, it, 1))
                    src = bank[:, 2, 0:2 * HEADS * HV1].rearrange("p (b j c) -> p b j c", b=2, j=HEADS // 2)
                    for b in range(2):
                        for hh in range(2):
                            rows, cols = slice(hh * MF, (hh + 1) * MF), slice(hh * HV1, (hh + 1) * HV1)
                            last = nc.vector.tensor_copy(CTX[s][rows, b, :, cols], src[rows, b, :, cols])
                    last.then_inc(*ctx_dve.step(s))
                elif name == "attn":
                    dve.wait_ge(*attn_pe(s, it, 1))
                    srcs = [bank[:, 3 - b, 0:2 * HEADS * HV1].rearrange("p (q e) -> p q e", e=HV1) for b in range(2)]
                    qs = [slice(2 * b * HEADS, (2 * b + 2) * HEADS) for b in range(2)]
                    for b in range(2):
                        last = nc.vector.reciprocal(stab[s][:, 1, qs[b]], srcs[b][:, :, DH])
                    last.then_inc(*attn_dve.step(s))
                    dve.wait_ge(*attn_dve(s, it, 1))
                    for b in range(2):
                        last = nc.vector.tensor_tensor(NX[s].rearrange("p t (h d) -> p (t h) d", d=DH)[:, qs[b], :], srcs[b][:, :, 0:DH],
                                                       stab[s][:, 1, qs[b]].unsqueeze(2).broadcast_to([P, 2 * HEADS, DH]), ALU.mult)
                    last.then_inc(*attn_dve.step(s))
                    dve.wait_ge(*attn_dve(s, it, 2))
                    nc.vector.tensor_tensor(XA[s], XA[s], NX[s], ALU.add).then_inc(*attn_dve.step(s))
                    dve.wait_ge(*attn_dve(s, it, 3))
                    ln_stats(ln_dve, s, it, 8, XA[s])
                elif name == "mlp_out":
                    dve.wait_ge(*mlp_pe(s, it, FT + 1))
                    dve.wait_ge(*hadd(s, it, 2))
                    nc.vector.tensor_tensor(two(H[s]), two(H[s]), bank[:, 2:4, 0:2 * C], ALU.add).then_inc(*mlp_dve.step(s))
                    dve.wait_ge(*mlp_dve(s, it, 1))
                    ln_stats(ln_dve, s, it, 12, H[s])

                elif name == "route1":
                    q = rt_dve
                    pr = small[s][:, 0, 0:TILES * E1].rearrange("p (t e) -> p t e", e=E1)
                    kp = small[s][:, 1, 0:TILES * E1].rearrange("p (t e) -> p t e", e=E1)
                    low = small[s][:, 2, 0:2 * TILES].rearrange("p (n t) -> p n t", n=2)
                    dve.wait_ge(*rt_act(s, it, 1))
                    nc.vector.tensor_tensor(low[:, 0, :], pr[:, :, 0], pr[:, :, 1], ALU.min)
                    nc.vector.tensor_tensor(low[:, 1, :], pr[:, :, 1], pr[:, :, 2], ALU.min).then_inc(*q.step(s))
                    dve.wait_ge(*q(s, it, 1))
                    nc.vector.tensor_tensor(kp[:, :, 2], pr[:, :, 2], low[:, 0, :], ALU.is_gt)
                    nc.vector.tensor_tensor(kp[:, :, 0], pr[:, :, 0], low[:, 1, :], ALU.is_ge).then_inc(*q.step(s))
                    dve.wait_ge(*q(s, it, 2))
                    nc.vector.tensor_tensor(low[:, 0, :], kp[:, :, 0], kp[:, :, 2], ALU.add).then_inc(*q.step(s))
                    dve.wait_ge(*q(s, it, 3))
                    nc.vector.tensor_scalar(kp[:, :, 1], low[:, 0, :], -1.0, 2.0, ALU.mult, ALU.add).then_inc(*q.step(s))
                    dve.wait_ge(*q(s, it, 4))
                    nc.vector.tensor_tensor(kp, kp, pr, ALU.mult).then_inc(*q.step(s))
                    dve.wait_ge(*q(s, it, 5))
                    nc.vector.tensor_reduce(low[:, 0, :], kp, AX.X, ALU.add).then_inc(*q.step(s))
                    dve.wait_ge(*q(s, it, 6))
                    nc.vector.reciprocal(low[:, 1, :], low[:, 0, :]).then_inc(*q.step(s))
                    dve.wait_ge(*q(s, it, 7))
                    nc.vector.scalar_tensor_tensor(out=kp, in0=kp, scalar=1.0 / WSCALE, in1=low[:, 1, :].unsqueeze(2).broadcast_to([P, TILES, E1]),
                                                   op0=ALU.mult, op1=ALU.mult).then_inc(*q.step(s))
                elif name == "gate":
                    x, j = divmod(k, IT)
                    dve.wait_ge(*ex_pe(s, it, x * (2 * IT + 1) + 2 * j + 2))
                    dve.wait_ge(*ex_act(s, it, x * IT + j + 1))
                    if x > 0:
                        dve.wait_ge(*ex_pe(s, it, x * (2 * IT + 1)))
                    nc.vector.tensor_tensor(big_b[s][:, j * CHUNK:(j + 1) * CHUNK], bank[:, 1, :], big_a[s][:, j * CHUNK:(j + 1) * CHUNK],
                                            ALU.mult).then_inc(*ex_dve.step(s))
                elif name == "down":
                    q = ex_dve
                    kp = small[s][:, 1, 0:TILES * E1].rearrange("p (t e) -> p t e", e=E1)
                    dve.wait_ge(*ex_pe(s, it, (k + 1) * (2 * IT + 1)))
                    if k == 0:
                        nc.vector.scalar_tensor_tensor(out=two(H[s]), in0=bank[:, 2:4, 0:2 * C], scalar=1.0 / WSCALE, in1=two(H[s]),
                                                       op0=ALU.mult, op1=ALU.add).then_inc(*q.step(s))
                    else:
                        dve.wait_ge(*q(s, it, k * (IT + 1)))
                        dve.wait_ge(*rt_dve(s, it, 8))
                        for t in range(TILES):
                            last = nc.vector.scalar_tensor_tensor(out=H[s][:, t, :], in0=bank[:, 2 + t // 2, (t % 2) * C:(t % 2 + 1) * C],
                                                                  scalar=kp[:, t, k - 1:k], in1=H[s][:, t, :], op0=ALU.mult, op1=ALU.add)
                        last.then_inc(*q.step(s))

            all_passes(dve, stage)

        @block.tensor
        def _(pe):
            for f in (embed_pe, tr, kv_pe, out_pe, ff_pe, moe_pe, feat_pe, stab_pe, ctx_pe, et_pe, attn_pe, mlp_pe, rt_pe, ex_pe):
                f.credit(pe)
            pe.sem_inc(table_mm, RING)
            pe.wait_ge(const_pool, 3 + 2 + 1 + STREAMS)
            pe.wait_ge(ident_in, 16)
            nc.tensor.matmul(gram, ident[0:1, 1:1 + RANK], HV[1][0:1, :, :].rearrange("p q e -> p (q e)")[:, 0:CR], start=True, stop=False,
                             skip_group_check=True)
            with pe.Fori(0, LOADS // RING) as it:
                for b in range(RING):
                    pe.wait_ge(table_in[b], it * 32 + 32)
                    for j in range(ROWS):
                        last = nc.tensor.matmul(gram, tab[b][:, j, C:CR], tab[b][:, j, :], start=False, stop=False, skip_group_check=True)
                    last.then_inc(table_mm, 1)
            pe.wait_ge(table_in[0], LOADS // RING * 32 + 32)
            nc.tensor.matmul(gram, tab[0][0:TAIL, 0, C:CR], tab[0][0:TAIL, 0, :], start=False, stop=True,
                             skip_group_check=True).then_inc(table_mm, 1)
            pe.wait_ge(norm_act, 1)
            pe.wait_ge(loaded, 16 * len(loads))
            nc.tensor.matmul(PS[0][0:RANK, 1, 0:C], gram_sb[:, C:CR], lora_b[:], start=True, stop=True).then_inc(norm_pe, 1)
            pe.wait_ge(norm_dve, 4)
            nc.tensor.matmul(PS[0][:, 2, 0:C], ones[:], colsum, start=True, stop=False)
            nc.tensor.matmul(PS[0][:, 2, 0:C], ones[0:RANK, :], cross, start=False, stop=True).then_inc(norm_pe, 1)
            pe.wait_ge(const_dve, 3)
            pe.wait_ge(proj_dve, 7)
            pe.wait_ge(norm_dve, NORM_STEPS)

            def halves(name, lo_, hi_):
                c = slice(COLS[name] + lo_, COLS[name] + hi_)
                return ((wcat[:, 0, c], 0, P), (wcat[:, 0, c], 1, P), (wcat[:, 1, c], 0, P), (wcat[:, 2, c], 2, P), (wcat[0:C1, 3, c], 2, C1))

            def by_channel(dst, terms, s, t0=0, t1=CHUNK):
                for n, (w, plane, rows) in enumerate(terms):
                    last = nc.tensor.matmul(dst, w, xh[s][0:rows, plane, t0:t1], start=(n == 0), stop=(n == len(terms) - 1))
                return last

            def by_token(dst, terms, s, t, bias=None):
                for n, (w, plane, rows) in enumerate(terms):
                    last = nc.tensor.matmul(dst, xh[s][0:rows, plane, t * P:(t + 1) * P], w, start=(n == 0), stop=(n == len(terms) - 1 and bias is None))
                if bias is not None:
                    last = nc.tensor.matmul(dst, ones[0:1, :], bias, start=False, stop=True)
                return last

            def bank_of(s, t):
                return PS[s][:, 2 + t // 2, (t % 2) * C:(t % 2 + 1) * C]

            def last_channels(col, name, bank, s):
                for b in range(2):
                    last = by_channel(PS[s][b * C1:(b + 1) * C1, bank, col:col + SEQ], halves(name, P, C), s, b * SEQ, (b + 1) * SEQ)
                return last

            NORMED = {0: (ln0_dve, 7), 1: (ln_dve, 4), 2: (ln_dve, 8), 3: (ln3_dve, 8), 4: (ln_dve, 12), 5: (ln_dve, 16)}

            def stage(name, k, s, it):
                bank = PS[s]
                if (name, k) == ("embed", 0):
                    pe.wait_ge(row_in[s], it + UNIT)
                    pe.wait_ge(*ex_dve(s, it, 0))
                    for t in range(TILES):
                        last = nc.tensor.transpose(bank[0:RANK, 0, t * P:(t + 1) * P], glora[s][:, t, :], ident[:])
                    last.then_inc(*embed_pe.step(s))
                elif name == "embed":
                    pe.wait_ge(*embed_act(s, it, 1))
                    for t in range(TILES):
                        last = nc.tensor.matmul(bank[:, 1 + t // 2, (t % 2) * C:(t % 2 + 1) * C], big_a[s][0:RANK, t * P:(t + 1) * P], lora_b[:],
                                                start=True, stop=True)
                    last.then_inc(*embed_pe.step(s))

                elif name == "norm":
                    src, _ = TR_BANKS[k]
                    f, n = NORMED[k]
                    pe.wait_ge(*f(s, it, n))
                    for t in range(TILES):
                        nc.tensor.transpose(bank[0:P, src[0], t * P:(t + 1) * P], NX[s][:, t, 0:P], ident[:])
                        last = nc.tensor.transpose(bank[0:C1, src[1], t * P:(t + 1) * P], NX[s][:, t, P:C], ident[:])
                    last.then_inc(*tr.step(s))

                elif name == "kv":
                    pe.wait_ge(*lo(s, it, 1))
                    by_channel(bank[:, 1, :], halves("k", 0, P), s)
                    last_channels(0, "k", 2, s)
                    by_channel(bank[:, 3, :], halves("v", 0, P), s)
                    last_channels(SEQ, "v", 2, s).then_inc(*kv_pe.step(s))
                    by_channel(bank[:, 0, :], halves("r", 0, P), s)
                    pe.wait_ge(*kv_act(s, it, 1))
                    last_channels(0, "r", 1, s).then_inc(*kv_pe.step(s))

                elif name == "out":
                    pe.wait_ge(*wkv_dve(s, it, 28))
                    for t in range(TILES):
                        b, h = t // 2, t % 2
                        nc.tensor.matmul(bank_of(s, t), big_b[s][:, t * P:(t + 1) * P], wo[:, 0, :], start=True, stop=False)
                        last = nc.tensor.matmul(bank_of(s, t), big_b[s][b * C1:(b + 1) * C1, CHUNK + h * P:CHUNK + (h + 1) * P],
                                                wo[b * C1:(b + 1) * C1, 1, :], start=False, stop=True)
                    last.then_inc(*out_pe.step(s))

                elif name == "mix_r":
                    pe.wait_ge(*lo(s, it, 2))
                    for t in range(TILES):
                        last = by_token(bank_of(s, t), halves("rf", 0, C), s, t)
                    last.then_inc(*ff_pe.step(s))
                elif name == "mix_k":
                    if k >= 2:
                        pe.wait_ge(*ff_act(s, it, 2 + 2 * (k - 2)))
                    by_channel(bank[:, k % 2, :], halves("kf", k * P, (k + 1) * P), s).then_inc(*ff_pe.step(s))
                elif name == "mix_v":
                    pe.wait_ge(*ff_act(s, it, 1 + 2 * FT))
                    for t in range(TILES):
                        for j in range(FT):
                            last = nc.tensor.matmul(bank_of(s, t), big_a[s][:, j * CHUNK + t * P:j * CHUNK + (t + 1) * P], wvf[:, j, :],
                                                    start=(j == 0), stop=(j == FT - 1))
                    last.then_inc(*ff_pe.step(s))

                elif (name, k) == ("route0", 0):
                    pe.wait_ge(*lo(s, it, 3))
                    for t in range(TILES):
                        last = by_token(bank[:, 2, t * E0:(t + 1) * E0], halves("router0", 0, E0), s, t, router0_b[:])
                    last.then_inc(*moe_pe.step(s))
                elif name == "route0":
                    pe.wait_ge(*moe_dve(s, it, 14))
                    for t in range(TILES):
                        last = nc.tensor.transpose(bank[0:E0, 3, t * P:(t + 1) * P], small[s][:, 9, t * E0:(t + 1) * E0], ident[:])
                    last.then_inc(*moe_pe.step(s))
                elif name == "experts":
                    for n in (k, k + 1):
                        e2, t = divmod(n, TILES)
                        if n >= 2:
                            pe.wait_ge(*mix(s, it, 2 * (n - 2) + 2))
                        by_token(bank[:, n % 2, 0:2 * C], halves("experts", 2 * e2 * C, 2 * (e2 + 1) * C), s, t).then_inc(*moe_pe.step(s))
                elif name == "experts_b":
                    pe.wait_ge(*moe_dve(s, it, 15))
                    for t in range(TILES):
                        last = nc.tensor.matmul(bank_of(s, t), wT[s][:, t * P:(t + 1) * P], experts_b, start=True, stop=True)
                    last.then_inc(*moe_pe.step(s))

                elif name == "feat":
                    b = 2 * (k % 2)
                    pe.wait_ge(*(lo(s, it, 4) if k < 2 else feat_dve(s, it, 1 + 3 * (k - 1))))
                    x = [xh[s][:, n, k * P:(k + 1) * P] for n in range(3)]
                    for n, (xs, w) in enumerate(((x[0], 0), (x[1], 0), (x[0], 1))):
                        nc.tensor.matmul(bank[:, b, :], xs, proj0[:, w, :], start=(n == 0), stop=(n == 2))
                    dst = bank[:, b + 1, 0:(HEADS - HK0) * MF]
                    nc.tensor.matmul(dst, x[2], proj1[:, 0, :], start=True, stop=False)
                    nc.tensor.matmul(dst, x[2][0:C1], proj1[0:C1, 1, :], start=False, stop=True).then_inc(*feat_pe.step(s))
                elif (name, k) == ("stab", 0):
                    pe.wait_ge(*feat_dve(s, it, 1 + 3 * TILES))
                    for t in range(TILES):
                        last = nc.tensor.transpose(bank[0:HEADS, 0, t * P:(t + 1) * P], stab[s][:, 0, t * HEADS:(t + 1) * HEADS], ident[:])
                    last.then_inc(*stab_pe.step(s))
                elif (name, k) == ("stab", 1):
                    pe.wait_ge(*stab_dve(s, it, 2))
                    for b in range(2):
                        last = nc.tensor.matmul(bank[:, 1, b * HEADS:(b + 1) * HEADS], ones[0:HEADS, :], stabT[s][:, b, 1:1 + HEADS], start=True, stop=True)
                    last.then_inc(*stab_pe.step(s))
                elif name == "ctx":
                    pe.wait_ge(*stab_dve(s, it, 4))
                    pe.wait_ge(*feat_act(s, it, 1 + TILES))
                    w = HEADS * HV1
                    for b in range(2):
                        for t in (2 * b, 2 * b + 1):
                            nc.tensor.matmul(bank[:, 2, b * w:(b + 1) * w], feat_eps[:], HV[s][:, t * HEADS:(t + 1) * HEADS, :].rearrange("p q e -> p (q e)"),
                                             start=(t == 2 * b), stop=False, skip_group_check=True)
                        for t in (2 * b, 2 * b + 1):
                            for j in range(HEADS // 2):
                                q = t * HEADS + 2 * j
                                last = nc.tensor.matmul(bank[:, 2, b * w + j * 2 * HV1:b * w + (j + 1) * 2 * HV1], big_a[s][:, q * MF:(q + 2) * MF],
                                                        CV[s][:, q:q + 2, :].rearrange("p q e -> p (q e)"), start=False, stop=(t == 2 * b + 1),
                                                        skip_group_check=True)
                    last.then_inc(*ctx_pe.step(s))
                elif name == "featT":
                    if k >= 2:
                        pe.wait_ge(*et_act(s, it, k - 1))
                    for t in range(TILES):
                        last = nc.tensor.transpose(bank[:, k % 2, t * P:(t + 1) * P], big_a[s][:, t * HEADS * MF + k * P:t * HEADS * MF + (k + 1) * P], ident[:])
                    last.then_inc(*et_pe.step(s))
                elif name == "attn":
                    pe.wait_ge(*ctx_dve(s, it, 1))
                    pe.wait_ge(*et_act(s, it, FT))
                    for t in range(TILES):
                        for j in range(HEADS // 2):
                            col = (t % 2) * HEADS * HV1 + j * 2 * HV1
                            last = nc.tensor.matmul(bank[:, 3 - t // 2, col:col + 2 * HV1], big_b[s][:, j * CHUNK + t * P:j * CHUNK + (t + 1) * P],
                                                    CTX[s][:, t // 2, j, :], start=True, stop=True)
                    last.then_inc(*attn_pe.step(s))

                elif name == "mlp":
                    pe.wait_ge(*(lo(s, it, 5) if k < 2 else mlp_act(s, it, k - 1)))
                    by_channel(bank[:, k % 2, :], halves("w1", k * P, (k + 1) * P), s).then_inc(*mlp_pe.step(s))
                elif name == "mlp_out":
                    pe.wait_ge(*mlp_act(s, it, FT))
                    for t in range(TILES):
                        nc.tensor.matmul(bank_of(s, t), ones[32:33, :], b2, start=True, stop=False)
                        for j in range(FT):
                            last = nc.tensor.matmul(bank_of(s, t), big_a[s][:, j * CHUNK + t * P:j * CHUNK + (t + 1) * P], w2[:, j, :],
                                                    start=False, stop=(j == FT - 1))
                    last.then_inc(*mlp_pe.step(s))

                elif name == "route1":
                    pe.wait_ge(*lo(s, it, 6))
                    for t in range(TILES):
                        last = by_token(bank[:, 2, t * E1:(t + 1) * E1], halves("router1", 0, E1), s, t, router1_b[:])
                    last.then_inc(*rt_pe.step(s))
                elif name == "gate":
                    x, j = divmod(k, IT)
                    at_ = 2 * x * I1 + j * P
                    if k:
                        pe.wait_ge(*ex_act(s, it, k))
                    by_channel(bank[:, 0, :], halves("gate_up", at_, at_ + P), s).then_inc(*ex_pe.step(s))
                    if k:
                        pe.wait_ge(*ex_dve(s, it, x * (IT + 1) + j - (j == 0)))
                    by_channel(bank[:, 1, :], halves("gate_up", at_ + I1, at_ + I1 + P), s).then_inc(*ex_pe.step(s))
                elif name == "down":
                    pe.wait_ge(*(ex_dve(s, it, k * (IT + 1)) if k else rt_act(s, it, 1)))
                    pe.wait_ge(*ex_dve(s, it, k * (IT + 1) + IT))
                    for t in range(TILES):
                        for j in range(IT):
                            last = nc.tensor.matmul(bank_of(s, t), big_b[s][:, j * CHUNK + t * P:j * CHUNK + (t + 1) * P], down[:, k, j, :],
                                                    start=(j == 0), stop=(j == IT - 1))
                    last.then_inc(*ex_pe.step(s))

            all_passes(pe, stage)


def kernel(**inputs):
    import numpy as np
    import concourse.bacc as bacc
    from concourse.bass_utils import run_bass_kernel_spmd

    g = {n: np.asarray(v) for n, v in inputs.items()}

    def col(*names):
        return np.ascontiguousarray(np.stack([g[n] for n in names], axis=1))

    B, S = g["x"].shape
    C = g["L0_tok_embeddings"].shape[1]
    E0 = g["L0_ffn_router_w"].shape[0]
    arrays = {
        "idx": g["x"].reshape(-1, TILES, P).transpose(0, 2, 1),
        "embeddings": g["L0_tok_embeddings"], "lora_a": g["L0_tok_lora_a"], "lora_b": g["L0_tok_lora_b"],
        "magnitude": g["L0_tok_magnitude"].reshape(1, C),
        "ln_cols": col("L0_attn_ln1_w", "L0_attn_ln1_b", "L0_attn_ln2_w", "L0_attn_ln2_b"),
        "ln2_cols": col("L1_attn_ln2_g", "L1_attn_ln2_b"),
        "ln1_g": g["L1_attn_ln1_g"].reshape(1, C), "ln1_b": g["L1_attn_ln1_b"].reshape(1, C),
        "wu": col("L0_attn_decay", "L0_attn_first"),
        "WoT": g["L0_attn_Wo_a"].T, "WvfT": g["L0_attn_Wv_f"].T, "router0_b": g["L0_ffn_router_b"].reshape(1, E0),
        "experts_b": g["L0_ffn_expert_b"],
        "projT": g["L1_attn_proj"].T, "b1": g["L1_attn_b1"].reshape(-1, P).T,
        "W2": g["L1_attn_W2"], "b2": g["L1_attn_b2"].reshape(1, C),
        "down": np.concatenate([g["L1_ffn_shared_down"][None], g["L1_ffn_routed_down"]], axis=0),
        "router1_b": g["L1_ffn_routing_bias"].reshape(1, -1),
        "ident": np.eye(P, dtype=np.float32), "iota8": np.arange(E0, dtype=np.float32).reshape(1, E0),
    }
    wcat = np.concatenate([
        g["L0_attn_Wk_a"].T, g["L0_attn_Wv_a"].T, g["L0_attn_Wr_a"].T, g["L0_attn_Wk_f"].T, g["L0_attn_Wr_f"].T,
        g["L0_ffn_expert_w"].transpose(2, 0, 1).reshape(C, -1), g["L1_attn_W1"],
        g["L1_ffn_shared_gate"], g["L1_ffn_shared_up"],
        *[w for pair in zip(g["L1_ffn_routed_gate"], g["L1_ffn_routed_up"]) for w in pair],
        g["L0_ffn_router_w"].T, g["L1_ffn_router_w"],
    ], axis=1)
    arrays["wcat"] = wcat.reshape(C, WEIGHT_PIECES, -1).transpose(1, 0, 2)
    nc = bacc.Bacc("TRN2", target_bir_lowering=False, num_devices=1)
    fed, aps = {}, {}
    for n, v in arrays.items():
        v = np.ascontiguousarray(v)
        fed[f"in_{n}"] = v
        aps[n] = nc.dram_tensor(f"in_{n}", v.shape, mybir.dt.from_np(v.dtype), kind="ExternalInput").ap()
    aps["SEQ"], aps["proj_shape"] = S, g["L1_attn_proj"].shape
    out = nc.dram_tensor("out_0", (B * S, C), F32, kind="ExternalOutput").ap()
    lm_tower(nc, aps, out)
    r = run_bass_kernel_spmd(nc, [fed], core_ids=[0])
    return r.results[0]["out_0"].reshape(B, S, C)
```

```python
from contextlib import ExitStack

import concourse.bass as bass
from concourse import mybir

F32 = mybir.dt.float32
F16 = mybir.dt.float16
I32 = mybir.dt.int32
U32 = mybir.dt.uint32
ALU = mybir.AluOpType
ACT = mybir.ActivationFunctionType
AX = mybir.AxisListType

P = 128
UNIT = 128
STREAMS = 2
WEIGHT_PIECES = 7
TILES = 4
CHUNK = TILES * P
NEG = -1e38
LN_EPS = 1e-5
FEAT_EPS = 1e-4
WSCALE = 64.0


def lm_tower(nc, a, out):
    V, C = a["embeddings"].shape
    RANK = a["lora_a"].shape[1]
    TOKENS = out.shape[0]
    SEQ = a["SEQ"]
    PASSES = TOKENS // (STREAMS * CHUNK)
    LORA_SCALE = 32.0 / RANK
    FF = a["W2"].shape[0]
    FT = FF // P
    E0 = a["experts_b"].shape[0]
    MF, DH = a["proj_shape"]
    HEADS = C // DH
    HK0 = P // DH
    E1 = a["router1_b"].shape[1]
    I1 = a["down"].shape[1]
    IT = I1 // P
    C1 = C - P
    SEGS = CHUNK // SEQ + 1
    SEGW = SEQ + 2
    assert CHUNK == 2 * SEQ and C1 * 2 == P and FT == 6 and SEGS == 3 and 2 * MF == P

    ROWS = 14
    RING = 4
    MAIN = V // P // ROWS * ROWS
    LOADS = MAIN // ROWS
    TAIL = V - MAIN * P
    CR = C + RANK
    assert LOADS % RING == 0 and 0 < TAIL <= P

    with ExitStack() as ctx:
        def sb(name, shape, dt=F32):
            return ctx.enter_context(nc.sbuf_tensor(name, shape, dt))

        def sem(name):
            return ctx.enter_context(nc.semaphore(name))

        class Steps:

            def __init__(self, name, per):
                self.sems, self.per, self.made = [sem(f"{name}_{s}") for s in range(STREAMS)], per, [0] * STREAMS

            def step(self, s):
                self.made[s] = self.made[s] % self.per + 1
                return self.sems[s], (1 if self.made[s] < self.per else UNIT - self.per + 1)

            def __call__(self, s, u, k):
                return self.sems[s], u + (k + 1 if k < self.per else UNIT + 1)

            def credit(self, eng):
                for q in self.sems:
                    eng.sem_inc(q, 1)

        ident = sb("ident", [P, P])
        ones = sb("ones", [P, P])
        feat_eps = sb("feat_eps", [P, P])
        PIECES, PIECE = a["wcat"].shape[0], a["wcat"].shape[2]
        wcat = sb("wcat", [P, 4, PIECES * PIECE], F16)
        COLS, at = {}, 0
        for name, n in (("k", C), ("v", C), ("r", C), ("kf", FF), ("rf", C), ("experts", E0 * C), ("w1", FF),
                        ("gate_up", 2 * I1 * (E1 + 1)), ("router0", E0), ("router1", E1)):
            COLS[name], at = at, at + n
        assert at == PIECES * PIECE and PIECES == LOADS // RING and PIECE <= 2 * TILES * C
        proj0 = sb("proj0", [P, 2, HK0 * MF], F16)
        proj1 = sb("proj1", [P, 2, (HEADS - HK0) * MF], F16)
        wo = sb("wo", [P, 2, C])
        wvf = sb("wvf", [P, FT, C])
        router0_b = sb("router0_b", [1, E0])
        bias_rows = sb("bias_rows", [33, C])
        experts_b, b2 = bias_rows[0:E0, :], bias_rows[32:33, :]
        b1 = sb("b1", [P, FT])
        w2 = sb("w2", [P, FT, C])
        down = sb("down", [P, E1 + 1, IT, C])
        router1_b = sb("router1_b", [1, E1])
        lora_b = sb("lora_b", [RANK, C])
        ln_cols = sb("ln_cols", [P, 2, 4])
        ln2_cols = sb("ln2_cols", [P, 2, 2])
        ln1_rows = sb("ln1_rows", [P, 2, C])
        wu = sb("wu", [P, 2, 2])
        gscale = sb("gscale", [P, C])
        half = sb("half", [P, TILES])
        minus = sb("minus", [P, TILES])
        eps_t = sb("eps_t", [P, TILES])
        iota8 = sb("iota8", [P, E0])
        decay_row = sb("decay_row", [P, SEGS, SEGW])

        SW = SEGS * SEGW
        WSW = (3 + 2 + 4 + 2) * SW
        ws = sb("ws", [P, WSW])

        def seg(at, n=1):
            v = ws[:, at * SW:(at + n) * SW]
            return v.rearrange("p (n g t) -> p n g t", n=n, g=SEGS)

        K, KU, VV = seg(0), seg(1), seg(2)
        MAXES = [seg(3), seg(4)]
        DECAYS = [seg(5, 2), seg(7, 2)]
        SUMS = [(seg(9 + d), DECAYS[d][:, 1:2]) for d in range(2)]

        def flat(v):
            return v.rearrange("p n g t -> p (n g t)")

        def data(v):
            return v[:, :, :, 1:SEQ + 1]

        BW = TILES * HEADS * MF
        big_a = [sb(f"big_a{s}", [P, BW]) for s in range(STREAMS)]
        big_b = [sb(f"big_b{s}", [P, BW]) for s in range(STREAMS)]
        tok = [sb(f"tok{s}", [P, 2, TILES, C]) for s in range(STREAMS)]
        H = [v[:, 0] for v in tok]
        XA = [v[:, 1] for v in tok]
        wpiece = [v[:].rearrange("p a t c -> p (a t c)")[:, 0:PIECE] for v in tok]
        HV1 = DH + 1
        norm = [sb(f"norm{s}", [P, TILES * HEADS * HV1]) for s in range(STREAMS)]
        NX = [n[:, 0:TILES * C].rearrange("p (t c) -> p t c", t=TILES) for n in norm]
        CV = [n[:].rearrange("p (q e) -> p q e", e=HV1) for n in norm]
        HV = [sb(f"heads{s}", [P, TILES * HEADS, HV1]) for s in range(STREAMS)]
        xh = [sb(f"xh{s}", [P, 3, CHUNK], F16) for s in range(STREAMS)]
        exp_r = [v[:].rearrange("p a b -> p (a b)").bitcast(F32) for v in xh]
        idx = [sb(f"idx{s}", [P, TILES], I32) for s in range(STREAMS)]
        grow = XA
        glora = [sb(f"glora{s}", [P, TILES, RANK]) for s in range(STREAMS)]
        stats = [sb(f"stats{s}", [P, TILES, 6]) for s in range(STREAMS)]
        mv = [sb(f"mv{s}", [P, TILES, 2]) for s in range(STREAMS)]
        rstd = [sb(f"rstd{s}", [P, 6, TILES]) for s in range(STREAMS)]
        small = [sb(f"small{s}", [P, 10, TILES * E0]) for s in range(STREAMS)]
        idx8 = [sb(f"idx8{s}", [P, TILES, 8], U32) for s in range(STREAMS)]
        wT = [n[0:E0, 0:CHUNK] for n in norm]
        stab = [sb(f"stab{s}", [P, 4, TILES * HEADS]) for s in range(STREAMS)]
        stabT = [sb(f"stabT{s}", [HEADS, 2, 1 + HEADS]) for s in range(STREAMS)]
        CTX = [sb(f"ctx{s}", [P, 2, HEADS // 2, 2 * HV1]) for s in range(STREAMS)]

        PS = [ctx.enter_context(nc.psum_tensor(f"ps{s}", [P, 4, 512], F32)) for s in range(STREAMS)]

        loaded, ident_in, mag_in = sem("weights_loaded"), sem("ident_in"), sem("mag_in")
        proj_set, proj_dve = sem("proj_set"), sem("proj_dve")
        const_pool = sem("const_pool")
        const_dve = sem("const_dve")
        const_act = sem("const_act")
        table_in = [sem(f"table_in{b}") for b in range(RING)]
        table_mm = sem("table_mm")
        table_sq = sem("table_sq")
        table_add = sem("table_add")
        piece_in, piece_hi, piece_lo = sem("piece_in"), sem("piece_hi"), sem("piece_lo")
        norm_pe = sem("norm_pe")
        norm_dve = sem("norm_dve")
        norm_act = sem("norm_act")
        held = sem("held")
        stored = [sem(f"stored{s}") for s in range(STREAMS)]
        idx_in = [sem(f"idx_in{s}") for s in range(STREAMS)]
        row_in = [sem(f"row_in{s}") for s in range(STREAMS)]

        embed_pe = Steps("embed_pe", 2)
        embed_act = Steps("embed_act", 1)
        ln0_dve, ln0_pool = Steps("ln0_dve", 6), Steps("ln0_pool", 8)
        tr = Steps("tr_pe", 12)
        ev, lo = Steps("tr_act", 12), Steps("lo_dve", 6)
        kv_pe, kv_act = Steps("kv_pe", 3), Steps("kv_act", 4)
        wkv_dve, wkv_act, wkv_pool = Steps("wkv_dve", 27), Steps("wkv_act", 3), Steps("wkv_pool", 1)
        out_pe, out_dve = Steps("out_pe", 2), Steps("out_dve", 2)
        hadd = Steps("hidden_pool", 2)
        ln_dve, ln_pool = Steps("ln_dve", 4 * 4), Steps("ln_pool", 4)
        ff_pe, ff_act, ff_dve = Steps("ff_pe", 1 + FT + TILES), Steps("ff_act", 1 + 2 * FT), Steps("ff_dve", 4)
        moe_pe, moe_dve, moe_act = Steps("moe_pe", 2 + 16 + 1), Steps("moe_dve", 15), Steps("moe_act", 1)
        mix = Steps("mix_dve", 2 * 16 + 1)
        ln3_dve, ln3_pool = Steps("ln3_dve", 5), Steps("ln3_pool", 8)
        resid = Steps("resid_act", 3)
        feat_act, feat_pe, feat_dve = Steps("feat_act", 1 + TILES), Steps("feat_pe", TILES), Steps("feat_dve", 1 + 3 * TILES)
        stab_pe, stab_dve, stab_act = Steps("stab_pe", 2), Steps("stab_dve", 4), Steps("stab_act", 1)
        ctx_pe, ctx_dve = Steps("ctx_pe", 2), Steps("ctx_dve", 1)
        et_pe, et_act = Steps("et_pe", FT), Steps("et_act", FT)
        attn_pe, attn_dve = Steps("attn_pe", TILES), Steps("attn_dve", 6)
        mlp_pe, mlp_act, mlp_dve = Steps("mlp_pe", FT + TILES), Steps("mlp_act", FT), Steps("mlp_dve", 2)
        rt_pe, rt_act, rt_dve = Steps("rt_pe", 1), Steps("rt_act", 1), Steps("rt_dve", 8)
        NX1 = E1 + 1
        ex_pe, ex_act, ex_dve = Steps("ex_pe", NX1 * (2 * IT + 2)), Steps("ex_act", NX1 * IT), Steps("ex_dve", NX1 * (IT + 1))
        EXPERTS1 = []
        for i in range(NX1 * IT):
            EXPERTS1 += [("gate", i), ("down_a", i // IT - 1), ("down", i // IT - 1)] if i % IT == 0 and i else [("gate", i)]
        EXPERTS1 += [("down_a", NX1 - 1), ("down", NX1 - 1)]

        def ex_steps(name, k, pe=False):
            made = {"gate": 2, "down_a": 1, "down": 1} if pe else {"gate": 1, "down_a": 0, "down": 1}
            return sum(made[slot[0]] for slot in EXPERTS1[:EXPERTS1.index((name, k)) + 1])

        WKV_PARTS = 15
        TR_BANKS = {0: ((3, 0), (1, 2)), 1: ((0, 1), (2, 3)), 2: ((0, 1), (0, 1)), 3: ((0, 1), (0, 1)), 4: ((0, 1), (2, 3)), 5: ((0, 1), (0, 1))}

        CHAIN = [("embed", 0), ("embed", 1), ("norm", 0), ("lo", 0), ("kv", 0), ("kv", 1), ("kv", 2)] + [("wkv", i) for i in range(WKV_PARTS)] + [("out", 0)]
        CHAIN += [("norm", 1), ("lo", 1), ("mix_r", 0)] + [("mix_k", j) for j in range(FT)] + [("mix_v", t) for t in range(TILES)]
        CHAIN += [("norm", 2), ("lo", 2), ("route0", 0), ("route0", 1)] + [("experts", n) for n in range(0, 16, 2)] + [("experts_b", 0)]
        CHAIN += [("norm", 3), ("lo", 3)] + [("feat", t) for t in range(TILES)] + [("stab", 0), ("featT", 0), ("featT", 1), ("stab", 1), ("featT", 2)]
        CHAIN += [("featT", 3), ("stab", 2), ("featT", 4), ("stab", 3), ("featT", 5), ("ctx", 0), ("ctx", 1)]
        CHAIN += [("attn", t) for t in range(TILES)] + [("norm", 4), ("lo", 4)] + [("mlp", j) for j in range(FT)] + [("mlp_out", t) for t in range(TILES)]
        CHAIN += [("norm", 5), ("lo", 5), ("route1", 0)] + EXPERTS1
        TO_MID, TO_OLD = CHAIN.index(("wkv", 11)), CHAIN.index(("mlp", 4))
        NEW, MID, OLD = CHAIN[:TO_MID], CHAIN[TO_MID:TO_OLD], CHAIN[TO_OLD:]
        OTHER = OLD[:22] + [("fetch", 0)] + OLD[22:] + NEW
        WEAVE = (
            2, 2, 1, 3, 2, 2, 1, 4, 2, 3, 2, 3, 1, 1, 3, 2, 3, 1, 3, 2, 1, 1, 1, 1, 1, 3, 1, 1, 1, 2, 4, 2, 2, 2, 1, 2, 2,
            3, 1, 4, 3, 3, 1, 1, 3, 1, 1, 4, 1, 1, 2, 2, 1, 1, 1, 2,
        )
        assert sum(WEAVE[0::2]) == len(OTHER) and sum(WEAVE[1::2]) == len(MID)
        ORDER = []
        for i, run_length in enumerate(WEAVE):
            slots, first = (MID if i % 2 else OTHER), sum(WEAVE[i % 2:i:2])
            ORDER += [(1 - i % 2, *slot) for slot in slots[first:first + run_length]]

        def half_pass(mid, old, new):
            for other, name, k in ORDER:
                chunk = (old if (name, k) in OLD else new) if other else mid
                if chunk is not None:
                    yield name, k, *chunk

        def all_passes(eng, stage):
            def run(mid, old, new):
                for slot in half_pass(mid, old, new):
                    stage(*slot)

            end = (PASSES - 1) * UNIT
            run(None, None, (0, 0))
            run((0, 0), None, (1, 0))
            run((1, 0), (0, 0), (0, UNIT))
            with eng.Fori(UNIT, end, UNIT) as u:
                run((0, u), (1, u - UNIT), (1, u))
                run((1, u), (0, u), (0, u + UNIT))
            run((0, end), (1, end - UNIT), (1, end))
            run((1, end), (0, end), None)
            run(None, (1, end), None)

        block = ctx.enter_context(nc.Block())

        projbd = HV[0][:].rearrange("p q e -> p (q e)")[:, 0:HEADS * MF]

        tab = [b[:, 0:ROWS * CR].rearrange("p (j c) -> p j c", c=CR) for b in (big_a[0], big_b[0], big_a[1], big_b[1])]
        NSQ = ROWS * C
        squares = [ws[:, 0:NSQ], ws[:, NSQ:2 * NSQ]]
        sqsum = ws[:, 2 * NSQ:3 * NSQ]
        emb_main = a["embeddings"][0:MAIN * P, :].rearrange("(p n j) d -> n p j d", p=P, j=ROWS)
        lora_main = a["lora_a"][0:MAIN * P, :].rearrange("(p n j) d -> n p j d", p=P, j=ROWS)
        gram = PS[0][0:RANK, 0, 0:CR]
        gram_sb = small[0][0:RANK, :, :].rearrange("p a b -> p (a b)")[:, 0:CR]
        cross = big_a[0][0:RANK, 0:C]
        colsum = big_a[1][:, 0:C]
        colmag = big_a[1][:, C:2 * C]

        both = [(wo, "WoT"), (ln_cols, "ln_cols"), (ln2_cols, "ln2_cols"), (wu, "wu")]
        loads = [(t[0:P, 0, :], a[n][0:P, :]) for t, n in both] + [(t[0:C1, 1, :], a[n][P:C, :]) for t, n in both]
        loads += [
            (wo[C1:P, 1, :], a["WoT"][P:C, :]), (wu[C1:P, 1, :], a["wu"][P:C, :]),
            (wvf[:], a["WvfT"].rearrange("(j p) c -> p j c", p=P)),
            (w2[:], a["W2"].rearrange("(j p) c -> p j c", p=P)),
            (down[:], a["down"].rearrange("x (j p) c -> p x j c", p=P)),
            (router0_b[:], a["router0_b"]), (experts_b, a["experts_b"]), (b1[:], a["b1"]), (b2, a["b2"]),
            (router1_b[:], a["router1_b"]), (lora_b[:], a["lora_b"]), (iota8[:], a["iota8"].broadcast_to([P, E0])),
            (ln1_rows[:, 0, :], a["ln1_g"].broadcast_to([P, C])), (ln1_rows[:, 1, :], a["ln1_b"].broadcast_to([P, C])),
        ]
        NORM_STEPS = 7 + 4 + 4 + SEGS

        @block.sync
        def _(sp):
            sp.dma_start(ident[:], a["ident"]).then_inc(ident_in, 16)
            with sp.Fori(0, LOADS // RING) as it:
                for b in range(RING):
                    sp.wait_ge(table_mm, it * RING + (b + 1))
                    sp.wait_ge(table_sq, it * RING + (b + 1))
                    sp.dma_start(tab[b][:, :, 0:C], emb_main[it * RING + b]).then_inc(table_in[b], 16)
                    sp.dma_start(tab[b][:, :, C:CR], lora_main[it * RING + b]).then_inc(table_in[b], 16)
                sp.wait_ge(piece_hi, it + 1)
                sp.wait_ge(piece_lo, it + 1)
                sp.dma_start(wpiece[0], a["wcat"][it, 0:P, :]).then_inc(piece_in, 16)
                sp.dma_start(wpiece[1][0:C1], a["wcat"][it, P:C, :]).then_inc(piece_in, 16)
                sp.dma_start(wpiece[1][C1:P], a["wcat"][it, P:C, :]).then_inc(piece_in, 16)
            sp.wait_ge(table_mm, LOADS + 1)
            sp.wait_ge(table_sq, LOADS + 1)
            sp.dma_start(tab[0][0:TAIL, 0, 0:C], a["embeddings"][MAIN * P:V, :]).then_inc(table_in[0], 16)
            sp.dma_start(tab[0][0:TAIL, 0, C:CR], a["lora_a"][MAIN * P:V, :]).then_inc(table_in[0], 16)

            for s in range(STREAMS):
                sp.sem_inc(idx_in[s], 1)
                sp.sem_inc(stored[s], 1)

            def stage(name, k, s, it):
                n = it // UNIT * STREAMS + s
                if name == "fetch":
                    sp.wait_ge(*embed_pe(s, it, 0))
                    sp.dma_start(idx[s][:], a["idx"][n]).then_inc(idx_in[s], UNIT)
                elif name == "down" and k == NX1 - 1:
                    sp.wait_ge(*ex_dve(s, it, NX1 * (IT + 1)))
                    sp.dma_start(out.rearrange("(n t p) c -> n p t c", p=P, t=TILES)[n], H[s]).then_inc(stored[s], UNIT)

            all_passes(sp, stage)
            for s in range(STREAMS):
                sp.wait_ge(stored[s], UNIT * PASSES + 1)

        @block.gpsimd
        def _(pool):
            def hold(q, value):
                pool.wait_ge(q, value)
                pool.sem_inc(held, 1)

            nc.gpsimd.memset(projbd, 0.0).then_inc(const_pool, 1)
            nc.gpsimd.memset(ones[:], 1.0).then_inc(const_pool, 1)
            nc.gpsimd.memset(feat_eps[:], FEAT_EPS).then_inc(const_pool, 1)
            nc.gpsimd.memset(half[:], -0.5).then_inc(const_pool, 1)
            nc.gpsimd.memset(eps_t[:], LN_EPS).then_inc(const_pool, 1)
            nc.gpsimd.memset(minus[:], -1.0).then_inc(const_pool, 1)
            nc.gpsimd.memset(HV[1][:], 1.0).then_inc(const_pool, 1)
            for s in range(STREAMS):
                nc.gpsimd.memset(CTX[s][:], 0.0).then_inc(const_pool, 1)
            pool.wait_ge(const_pool, 1)
            for h in range(HEADS):
                for r in ((h * DH,) if h < HK0 else ((h - HK0) * DH, (h - HK0) * DH + C1)):
                    pool.dma_start(projbd[r:r + DH, h * MF:(h + 1) * MF], a["projT"]).then_inc(proj_set, 16)
            for dst, src in loads:
                pool.dma_start(dst, src).then_inc(loaded, 16)
            pool.wait_ge(norm_dve, 1)
            pool.dma_start(colmag, a["magnitude"].broadcast_to([P, C])).then_inc(mag_in, 16)

            for f in (ln0_pool, wkv_pool, hadd, ln_pool, ln3_pool):
                f.credit(pool)

            def power(s, i_out, in0, q):
                nc.gpsimd.tensor_tensor(rstd[s][:, i_out, :], in0, half[:], ALU.pow).then_inc(*q)

            def ln_twice(f_dve, f_pool, k_dve, s, it):
                pool.wait_ge(*f_dve(s, it, k_dve))
                power(s, 0, rstd[s][:, 3, :], f_pool.step(s))
                pool.wait_ge(*f_pool(s, it, 1))
                nc.gpsimd.tensor_tensor(rstd[s][:, 1, :], rstd[s][:, 0, :], rstd[s][:, 0, :], ALU.mult).then_inc(*f_pool.step(s))
                pool.wait_ge(*f_pool(s, it, 2))
                nc.gpsimd.tensor_tensor(rstd[s][:, 1, :], rstd[s][:, 1, :], mv[s][:, :, 1], ALU.mult).then_inc(*f_pool.step(s))
                pool.wait_ge(*f_pool(s, it, 3))
                nc.gpsimd.tensor_tensor(rstd[s][:, 1, :], rstd[s][:, 1, :], eps_t[:], ALU.add).then_inc(*f_pool.step(s))
                pool.wait_ge(*f_pool(s, it, 4))
                power(s, 2, rstd[s][:, 1, :], f_pool.step(s))
                pool.wait_ge(*f_pool(s, it, 5))
                nc.gpsimd.tensor_tensor(rstd[s][:, 4, :], rstd[s][:, 0, :], rstd[s][:, 2, :], ALU.mult).then_inc(*f_pool.step(s))
                nc.gpsimd.tensor_tensor(rstd[s][:, 5, :], rstd[s][:, 0, :], mv[s][:, :, 0], ALU.mult).then_inc(*f_pool.step(s))
                pool.wait_ge(*f_pool(s, it, 7))
                nc.gpsimd.tensor_tensor(rstd[s][:, 5, :], rstd[s][:, 5, :], minus[:], ALU.mult).then_inc(*f_pool.step(s))

            def ln_once(i, s, it):
                pool.wait_ge(*ln_dve(s, it, 4 * i + 3))
                power(s, 0, rstd[s][:, 3, :], ln_pool.step(s))

            def add_resid(f, k, s, it):
                pool.wait_ge(*f(s, it, k))
                nc.gpsimd.tensor_tensor(H[s], H[s], XA[s], ALU.add).then_inc(*hadd.step(s))

            def stage(name, k, s, it):
                if name == "fetch":
                    hold(idx_in[s], it + (UNIT + 1))
                    hold(*ln_dve(s, it, 0))
                    hold(*hadd(s, it, 0))
                    hold(*embed_pe(s, it, 0))
                    for t in range(TILES):
                        off = bass.IndirectOffsetOnAxis(idx[s][:, t:t + 1], 0)
                        pool.indirect_dma_start(out=grow[s][:, t, :], out_offset=None, in_=a["embeddings"],
                                                in_offset=off).then_inc(row_in[s], 16)
                        pool.indirect_dma_start(out=glora[s][:, t, :], out_offset=None, in_=a["lora_a"],
                                                in_offset=off).then_inc(row_in[s], 16)
                elif (name, k) == ("embed", 1):
                    ln_twice(ln0_dve, ln0_pool, 5, s, it)
                elif (name, k) == ("wkv", 6):
                    pool.wait_ge(*wkv_act(s, it, 3))
                    pool.wait_ge(*kv_act(s, it, 3))
                    n3 = SEGS * SEQ
                    nc.gpsimd.tensor_tensor(big_a[s][:, 3 * n3:4 * n3].rearrange("p (g t) -> p g t", g=SEGS),
                                            big_a[s][:, 2 * n3:3 * n3].rearrange("p (g t) -> p g t", g=SEGS), data(VV)[:, 0], ALU.mult).then_inc(*wkv_pool.step(s))
                elif name == "out":
                    add_resid(out_dve, 2, s, it)
                    ln_once(0, s, it)
                elif (name, k) == ("mix_v", TILES - 1):
                    ln_once(1, s, it)
                elif name == "experts_b":
                    ln_twice(ln3_dve, ln3_pool, 3, s, it)
                elif (name, k) == ("attn", TILES - 1):
                    add_resid(attn_dve, 6, s, it)
                    ln_once(2, s, it)
                elif (name, k) == ("mlp_out", TILES - 1):
                    ln_once(3, s, it)

            pool.wait_ge(piece_lo, PIECES + 1)
            all_passes(pool, stage)

        @block.scalar
        def _(act):
            for f in (embed_act, ev, resid, kv_act, wkv_act, ff_act, moe_act, feat_act, stab_act, et_act, mlp_act, rt_act, ex_act):
                f.credit(act)
            act.sem_inc(table_sq, RING)
            act.sem_inc(piece_hi, 1)

            with act.Fori(0, LOADS // RING) as it:
                for b in range(RING):
                    act.wait_ge(table_in[b], it * 32 + 32)
                    act.wait_ge(table_add, it * RING + (b + 1))
                    nc.scalar.activation(squares[b % 2].rearrange("p (j c) -> p j c", c=C), tab[b][:, :, 0:C],
                                         ACT.Square).then_inc(table_sq, 1)
                act.wait_ge(piece_in, it * 48 + 48)
                nc.scalar.activation(wcat[:, 0, bass.ds(it * PIECE, PIECE)], wpiece[0], ACT.Copy, scale=WSCALE)
                nc.scalar.activation(wcat[:, 2, bass.ds(it * PIECE, PIECE)], wpiece[1], ACT.Copy, scale=WSCALE).then_inc(piece_hi, 1)
            act.wait_ge(table_in[0], LOADS // RING * 32 + 32)
            act.wait_ge(table_add, LOADS + 1)
            nc.scalar.activation(squares[0][0:TAIL, 0:C], tab[0][0:TAIL, 0, 0:C], ACT.Square).then_inc(table_sq, 1)
            act.wait_ge(table_mm, RING + LOADS + 1)
            nc.scalar.activation(gram_sb, gram, ACT.Copy).then_inc(norm_act, 1)
            act.wait_ge(norm_pe, 2)
            nc.scalar.activation(colsum, PS[0][:, 2, 0:C], ACT.Sqrt).then_inc(norm_act, 1)
            act.wait_ge(loaded, 16 * len(loads))
            act.wait_ge(norm_dve, NORM_STEPS)
            AFFINE = {0: (ln_cols, 0), 1: (ln_cols, 2), 4: (ln2_cols, 0)}

            def stage(name, k, s, it):
                bank = PS[s]
                if (name, k) == ("embed", 0):
                    act.wait_ge(*embed_pe(s, it, 1))
                    nc.scalar.activation(big_a[s][0:RANK, 0:CHUNK], bank[0:RANK, 0, :], ACT.Copy).then_inc(*embed_act.step(s))

                elif name == "norm":
                    src, full = TR_BANKS[k]
                    for part, rows in ((0, P), (1, C1)):
                        act.wait_ge(*tr(s, it, 2 * k + part + 1))
                        v, dst = bank[0:rows, src[part], :], xh[s][0:rows, 2 * part, :]
                        if k in AFFINE:
                            cols, c = AFFINE[k]
                            sc, sh = cols[0:rows, part, c:c + 1], cols[0:rows, part, c + 1:c + 2]
                            nc.scalar.activation(bank[0:rows, full[part], :], v, ACT.Identity, bias=sh, scale=sc)
                            nc.scalar.activation(dst, v, ACT.Identity, bias=sh, scale=sc).then_inc(*ev.step(s))
                        else:
                            nc.scalar.activation(dst, v, ACT.Copy).then_inc(*ev.step(s))
                elif name == "lo":
                    if k == 3:
                        nc.scalar.activation(HV[s][:, :, 0:DH], NX[s].rearrange("p t (h d) -> p (t h) d", d=DH), ACT.Copy).then_inc(*resid.step(s))
                    if k in (0, 3):
                        act.wait_ge(*(ln0_pool if k == 0 else ln3_pool)(s, it, 8))
                        for t in range(TILES):
                            last = nc.scalar.activation(XA[s][:, t, :], H[s][:, t, :], ACT.Identity, bias=rstd[s][:, 5, t:t + 1], scale=rstd[s][:, 0, t:t + 1])
                        last.then_inc(*resid.step(s))

                elif (name, k) == ("kv", 0):
                    act.wait_ge(*kv_pe(s, it, 1))
                    if s == 0:
                        act.wait_ge(*wkv_dve(1, it, 0))
                        act.wait_ge(*wkv_pool(1, it, 0))
                    else:
                        act.wait_ge(*wkv_dve(0, it, 27))
                        act.wait_ge(*wkv_pool(0, it, 1))
                    srcs = [(slice(0, 2), bank[:, 1, :].rearrange("p (g t) -> p g t", t=SEQ)), (slice(2, 3), bank[:, 2:3, 0:SEQ])]
                    for g, src in srcs:
                        last = nc.scalar.activation(data(K)[:, 0, g, :], src, ACT.Copy, scale=1.0 / WSCALE)
                    last.then_inc(*kv_act.step(s))
                    for col, (g, src) in enumerate(srcs):
                        last = nc.scalar.activation(data(KU)[:, 0, g, :], src, ACT.Identity, bias=wu[:, col, 1:2], scale=1.0 / WSCALE)
                    last.then_inc(*kv_act.step(s))
                elif (name, k) == ("kv", 1):
                    act.wait_ge(*kv_pe(s, it, 2))
                    for g, src in ((slice(0, 2), bank[:, 3, :]), (slice(2, 3), bank[:, 2, SEQ:2 * SEQ])):
                        last = nc.scalar.activation(data(VV)[:, 0, g, :], src.rearrange("p (g t) -> p g t", t=SEQ), ACT.Copy, scale=1.0 / WSCALE)
                    last.then_inc(*kv_act.step(s))
                elif name == "kv":
                    act.wait_ge(*kv_pe(s, it, 3))
                    nc.scalar.activation(exp_r[s][:, 0:CHUNK], bank[:, 0, :], ACT.Exp, scale=-1.0 / WSCALE)
                    nc.scalar.activation(exp_r[s][:, CHUNK:CHUNK + SEQ], bank[:, 1, 0:SEQ], ACT.Exp, scale=-1.0 / WSCALE).then_inc(*kv_act.step(s))

                elif name == "wkv" and k in (2, 3):
                    act.wait_ge(*wkv_dve(s, it, 4 + 2 * (k - 2)))
                    v = data(DECAYS[k - 2]).rearrange("p n g t -> p (n g) t")
                    nc.scalar.activation(v, v, ACT.Exp).then_inc(*wkv_act.step(s))
                elif (name, k) == ("wkv", 5):
                    act.wait_ge(*wkv_dve(s, it, 11))
                    v = big_a[s][:, 0:3 * SEGS * SEQ]
                    nc.scalar.activation(v, v, ACT.Exp).then_inc(*wkv_act.step(s))

                elif name == "mix_r":
                    act.wait_ge(*ff_pe(s, it, 1))
                    nc.scalar.activation(NX[s].rearrange("p (b t) c -> p b (t c)", b=2), bank[:, 2:4, 0:2 * C], ACT.Sigmoid,
                                         scale=1.0 / WSCALE).then_inc(*ff_act.step(s))
                elif name == "mix_k":
                    act.wait_ge(*ff_pe(s, it, 2 + k))
                    v = big_a[s][:, k * CHUNK:(k + 1) * CHUNK]
                    nc.scalar.activation(v, bank[:, k % 2, :], ACT.Relu, scale=1.0 / WSCALE).then_inc(*ff_act.step(s))
                    act.wait_ge(*ff_act(s, it, 2 + 2 * k))
                    nc.scalar.activation(v, v, ACT.Square).then_inc(*ff_act.step(s))

                elif (name, k) == ("route0", 0):
                    act.wait_ge(*moe_dve(s, it, 4))
                    nc.scalar.activation(small[s][:, 3, :], small[s][:, 2, :], ACT.Exp).then_inc(*moe_act.step(s))

                elif name == "feat":
                    if k == 0:
                        act.wait_ge(*tr(s, it, 8))
                        act.wait_ge(*resid(s, it, 2))
                        nc.scalar.activation(NX[s].rearrange("p t (h d) -> p (t h) d", d=DH), HV[s][:, :, 0:DH], ACT.Square,
                                             scale=float(DH) ** -0.25).then_inc(*feat_act.step(s))
                    act.wait_ge(*feat_dve(s, it, 1 + 3 * (k + 1)))
                    v = big_a[s][:, k * HEADS * MF:(k + 1) * HEADS * MF]
                    nc.scalar.activation(v, v, ACT.Exp).then_inc(*feat_act.step(s))
                elif (name, k) == ("stab", 2):
                    act.wait_ge(*stab_dve(s, it, 3))
                    nc.scalar.activation(stab[s][:, 2, :], stab[s][:, 2, :], ACT.Exp).then_inc(*stab_act.step(s))
                elif name == "featT":
                    act.wait_ge(*et_pe(s, it, k + 1))
                    nc.scalar.activation(big_b[s][:, k * CHUNK:(k + 1) * CHUNK], bank[:, k % 2, :], ACT.Copy, bias=FEAT_EPS).then_inc(*et_act.step(s))

                elif name == "mlp":
                    act.wait_ge(*mlp_pe(s, it, k + 1))
                    nc.scalar.activation(big_a[s][:, k * CHUNK:(k + 1) * CHUNK], bank[:, k % 2, :], ACT.Gelu, bias=b1[:, k:k + 1],
                                         scale=1.0 / WSCALE).then_inc(*mlp_act.step(s))
                elif name == "route1":
                    act.wait_ge(*rt_pe(s, it, 1))
                    nc.scalar.activation(small[s][:, 0, 0:TILES * E1], bank[:, 2, 0:TILES * E1], ACT.Sigmoid, scale=1.0 / WSCALE).then_inc(*rt_act.step(s))
                elif name == "gate":
                    x, j = divmod(k, IT)
                    act.wait_ge(*ex_pe(s, it, ex_steps("gate", k, pe=True) - 1))
                    if x >= 2:
                        act.wait_ge(*ex_dve(s, it, ex_steps("gate", k - 2 * IT)))
                    at_ = (x % 2 * IT + j) * CHUNK
                    nc.scalar.activation(big_a[s][:, at_:at_ + CHUNK], bank[:, 0, :], ACT.Silu, scale=1.0 / WSCALE).then_inc(*ex_act.step(s))

            all_passes(act, stage)

        @block.vector
        def _(dve):
            def hold(q, value):
                dve.wait_ge(q, value)
                dve.sem_inc(held, 1)

            for f in (ln0_dve, lo, wkv_dve, out_dve, ln_dve, ff_dve, moe_dve, mix, ln3_dve, feat_dve, stab_dve, ctx_dve, attn_dve, mlp_dve, rt_dve, ex_dve):
                f.credit(dve)
            dve.sem_inc(table_add, 2)
            dve.sem_inc(piece_lo, 1)
            nc.vector.memset(sqsum, 0.0).then_inc(const_dve, 1)
            dve.wait_ge(const_dve, 1)
            with dve.Fori(0, LOADS // RING) as it:
                for b in range(RING):
                    dve.wait_ge(table_sq, it * RING + (RING + b + 1))
                    dve.wait_ge(table_add, it * RING + (b + 2))
                    nc.vector.tensor_tensor(sqsum, sqsum, squares[b % 2], ALU.add).then_inc(table_add, 1)
                dve.wait_ge(piece_hi, it + 2)
                nc.vector.scalar_tensor_tensor(out=wcat[:, 1, bass.ds(it * PIECE, PIECE)], in0=wpiece[0], scalar=WSCALE,
                                               in1=wcat[:, 0, bass.ds(it * PIECE, PIECE)], op0=ALU.mult, op1=ALU.subtract)
                nc.vector.scalar_tensor_tensor(out=wcat[:, 3, bass.ds(it * PIECE, PIECE)], in0=wpiece[1], scalar=WSCALE,
                                               in1=wcat[:, 2, bass.ds(it * PIECE, PIECE)], op0=ALU.mult, op1=ALU.subtract).then_inc(piece_lo, 1)
            dve.wait_ge(table_sq, RING + LOADS + 1)
            dve.wait_ge(table_add, LOADS + 2)
            nc.vector.tensor_tensor(sqsum[0:TAIL, 0:C], sqsum[0:TAIL, 0:C], squares[0][0:TAIL, 0:C], ALU.add).then_inc(table_add, 1)
            dve.wait_ge(table_add, LOADS + 3)
            dve.wait_ge(table_mm, RING + LOADS + 1)
            nc.vector.tensor_reduce(colsum, sqsum.rearrange("p (j c) -> p c j", c=C), AX.X, ALU.add).then_inc(norm_dve, 1)
            dve.wait_ge(loaded, 16 * len(loads))
            dve.wait_ge(norm_act, 1)
            dve.wait_ge(norm_pe, 1)
            nc.vector.tensor_scalar(cross, gram_sb[:, 0:C], 2.0 / LORA_SCALE, None, ALU.mult).then_inc(norm_dve, 1)
            dve.wait_ge(norm_dve, 2)
            nc.vector.tensor_tensor(cross, cross, PS[0][0:RANK, 1, 0:C], ALU.add).then_inc(norm_dve, 1)
            dve.wait_ge(norm_dve, 3)
            nc.vector.scalar_tensor_tensor(out=cross, in0=cross, scalar=LORA_SCALE * LORA_SCALE, in1=lora_b[:], op0=ALU.mult, op1=ALU.mult).then_inc(norm_dve, 1)
            dve.wait_ge(norm_dve, 4)
            nc.vector.tensor_scalar(lora_b[:], lora_b[:], LORA_SCALE, None, ALU.mult).then_inc(const_dve, 1)
            dve.wait_ge(proj_set, 16 * (HEADS + HEADS - HK0))
            for dst, src in ((proj0, projbd[:, 0:HK0 * MF]), (proj1, projbd[:, HK0 * MF:HEADS * MF])):
                nc.vector.tensor_scalar(dst[:, 0, :], src, float(DH) ** -0.25, None, ALU.mult).then_inc(proj_dve, 1)
            dve.wait_ge(proj_dve, 2)
            for dst, src in ((proj0, projbd[:, 0:HK0 * MF]), (proj1, projbd[:, HK0 * MF:HEADS * MF])):
                nc.vector.scalar_tensor_tensor(out=dst[:, 1, :], in0=src, scalar=float(DH) ** -0.25, in1=dst[:, 0, :],
                                               op0=ALU.mult, op1=ALU.subtract).then_inc(proj_dve, 1)
            dve.wait_ge(proj_dve, 4)
            nc.vector.memset(HV[0][:], 1.0).then_inc(const_dve, 1)
            for bias in (experts_b, router0_b[:], router1_b[:]):
                nc.vector.tensor_scalar(bias, bias, WSCALE, None, ALU.mult).then_inc(proj_dve, 1)
            dve.wait_ge(norm_act, 2)
            nc.vector.tensor_scalar(colsum, colsum, 1e-8, None, ALU.max).then_inc(norm_dve, 1)
            dve.wait_ge(norm_dve, 5)
            nc.vector.reciprocal(colsum, colsum).then_inc(norm_dve, 1)
            dve.wait_ge(norm_dve, 6)
            dve.wait_ge(mag_in, 16)
            nc.vector.tensor_tensor(gscale[:], colsum, colmag, ALU.mult).then_inc(norm_dve, 1)
            pads = ws[:].rearrange("p (n t) -> p n t", t=SEGW)
            for edge in (0, SEGW - 1):
                nc.vector.memset(pads[:, :, edge], 0.0).then_inc(norm_dve, 1)
            nc.vector.memset(decay_row[:], 0.0).then_inc(norm_dve, 1)
            nc.vector.tensor_scalar(wu[:], wu[:], 1.0 / SEQ, None, ALU.mult).then_inc(norm_dve, 1)
            dve.wait_ge(norm_dve, NORM_STEPS - 4 - SEGS)
            for edge in (0, SEGW - 1):
                nc.vector.memset(K[:, 0, :, edge], NEG).then_inc(norm_dve, 1)
                nc.vector.memset(decay_row[:, :, edge], 2 * NEG).then_inc(norm_dve, 1)
            for g in range(SEGS):
                data_cols = decay_row[:, g, 1:SEQ + 1]
                nc.vector.tensor_scalar(data_cols, data_cols, wu[:, g // 2, 0:1], None, ALU.add).then_inc(norm_dve, 1)
            dve.wait_ge(norm_dve, NORM_STEPS)
            dve.wait_ge(proj_dve, 7)
            dve.wait_ge(const_dve, 3)

            def half_stats(s, b, x):
                for t in range(2 * b, 2 * b + 2 - b):
                    nc.vector.bn_stats(stats[s][:, t, :], x[:, t, :])

            def ln_stats(f, s, it, k, x, t0=0):
                for t in range(t0, TILES):
                    last = nc.vector.bn_stats(stats[s][:, t, :], x[:, t, :])
                last.then_inc(*f.step(s))
                hold(*f(s, it, k + 1))
                for t in range(TILES):
                    last = nc.vector.bn_aggr(mv[s][:, t, :], stats[s][:, t, :])
                last.then_inc(*f.step(s))
                dve.wait_ge(*f(s, it, k + 2))
                nc.vector.tensor_scalar(rstd[s][:, 3, :], mv[s][:, :, 1], LN_EPS, None, ALU.add).then_inc(*f.step(s))

            def apply(dst, x, s):
                for t in range(TILES):
                    last = nc.vector.tensor_scalar(dst[s][:, t, :], x[s][:, t, :], mv[s][:, t, 0:1], rstd[s][:, 0, t:t + 1], ALU.subtract, ALU.mult)
                return last

            def two(v):
                return v.rearrange("p (b t) c -> p b (t c)", b=2)

            def stage(name, k, s, it):
                bank = PS[s]
                if (name, k) == ("embed", 1):
                    q = ln0_dve
                    dve.wait_ge(row_in[s], it + UNIT)
                    dve.wait_ge(*embed_pe(s, it, 2))
                    dve.wait_ge(stored[s], it + 1)
                    nc.vector.tensor_tensor(two(H[s]), two(grow[s]), bank[:, 1:3, 0:2 * C], ALU.add).then_inc(*q.step(s))
                    dve.wait_ge(*q(s, it, 1))
                    nc.vector.tensor_tensor(H[s], H[s], gscale[:].unsqueeze(1).broadcast_to([P, TILES, C]), ALU.mult).then_inc(*q.step(s))
                    dve.wait_ge(*q(s, it, 2))
                    ln_stats(q, s, it, 2, H[s])

                elif name == "norm":
                    if k == 0:
                        dve.wait_ge(*ln0_pool(s, it, 6))
                        dve.wait_ge(*tr(s, it, 0))
                        for t in range(TILES):
                            last = nc.vector.tensor_scalar(NX[s][:, t, :], H[s][:, t, :], mv[s][:, t, 0:1], rstd[s][:, 4, t:t + 1], ALU.subtract, ALU.mult)
                        last.then_inc(*ln0_dve.step(s))
                    elif k == 3:
                        q = ln3_dve
                        for t in range(TILES):
                            last = nc.vector.scalar_tensor_tensor(out=NX[s][:, t, :], in0=H[s][:, t, :], scalar=mv[s][:, t, 0:1], in1=ln1_rows[:, 0, :],
                                                                  op0=ALU.subtract, op1=ALU.mult)
                        last.then_inc(*q.step(s))
                        dve.wait_ge(*q(s, it, 4))
                        dve.wait_ge(*ln3_pool(s, it, 6))
                        for t in range(TILES):
                            last = nc.vector.scalar_tensor_tensor(out=NX[s][:, t, :], in0=NX[s][:, t, :], scalar=rstd[s][:, 4, t:t + 1],
                                                                  in1=ln1_rows[:, 1, :], op0=ALU.mult, op1=ALU.add)
                        last.then_inc(*q.step(s))
                    else:
                        i = {1: 0, 2: 1, 4: 2, 5: 3}[k]
                        dve.wait_ge(*ln_pool(s, it, i + 1))
                        apply(NX, XA if k in (1, 4) else H, s).then_inc(*ln_dve.step(s))
                elif name == "lo":
                    src, full = TR_BANKS[k]
                    dve.wait_ge(*ev(s, it, 2 * k + 1))
                    nc.vector.tensor_tensor(xh[s][:, 1, :], bank[:, full[0], :], xh[s][:, 0, :], ALU.subtract)
                    dve.wait_ge(*ev(s, it, 2 * k + 2))
                    nc.vector.tensor_tensor(xh[s][C1:P, 2, :], bank[0:C1, full[1], :], xh[s][0:C1, 2, :], ALU.subtract).then_inc(*lo.step(s))

                elif name == "wkv":
                    q = wkv_dve
                    n3 = SEGS * SEQ
                    args = big_a[s][:, 0:3 * n3].rearrange("p (n g t) -> p n g t", n=3, g=SEGS)
                    mxv = big_b[s][:, 2 * n3:3 * n3].rearrange("p (g t) -> p g t", g=SEGS)
                    prev = [MAXES[0][:, 0, :, 0:SEQ], MAXES[1][:, 0, :, 2:SEQ + 2]]
                    decay = decay_row[:].rearrange("p g t -> p (g t)")
                    tot = big_b[s][:, 0:2 * n3].rearrange("p (n g t) -> p n g t", n=2, g=SEGS)
                    oth = big_b[s][:, 2 * n3:4 * n3].rearrange("p (n g t) -> p n g t", n=2, g=SEGS)
                    den, rec = big_b[s][:, n3:2 * n3], big_b[s][:, 3 * n3:4 * n3]
                    if k == 0:
                        dve.wait_ge(*kv_act(s, it, 1))
                        nc.vector.tensor_tensor_scan(flat(MAXES[0]), decay, flat(K), NEG, ALU.add, ALU.max).then_inc(*q.step(s))
                    elif k == 1:
                        nc.vector.tensor_tensor_scan(flat(MAXES[1])[:, ::-1], decay[:, ::-1], flat(K)[:, ::-1], NEG, ALU.add, ALU.max).then_inc(*q.step(s))
                    elif k in (2, 3):
                        d = k - 2
                        old, new = data(DECAYS[d])[:, 0], data(DECAYS[d])[:, 1]
                        dve.wait_ge(*q(s, it, 1 + d))
                        for g, col in ((slice(0, 2), 0), (slice(2, 3), 1)):
                            last = nc.vector.scalar_tensor_tensor(out=old[:, g], in0=prev[d][:, g], scalar=wu[:, col, 0:1], in1=data(MAXES[d])[:, 0, g],
                                                                  op0=ALU.add, op1=ALU.subtract)
                        last.then_inc(*q.step(s))
                        nc.vector.tensor_tensor(new, data(K)[:, 0], data(MAXES[d])[:, 0], ALU.subtract).then_inc(*q.step(s))
                    elif k == 4:
                        dve.wait_ge(*q(s, it, 2))
                        dve.wait_ge(*kv_act(s, it, 2))
                        nc.vector.tensor_tensor(mxv, data(KU)[:, 0], prev[0], ALU.max).then_inc(*q.step(s))
                        dve.wait_ge(*q(s, it, 7))
                        nc.vector.tensor_tensor(mxv, mxv, prev[1], ALU.max).then_inc(*q.step(s))
                    elif k == 5:
                        dve.wait_ge(*q(s, it, 8))
                        for n, v in enumerate((prev[0], prev[1], data(KU)[:, 0])):
                            nc.vector.tensor_tensor(args[:, n], v, mxv, ALU.subtract).then_inc(*q.step(s))
                    elif k in (6, 7):
                        d = k - 6
                        e_old, e_new = flat(DECAYS[d][:, 0:1]), flat(DECAYS[d][:, 1:2])
                        num = flat(SUMS[d][0])
                        dve.wait_ge(*kv_act(s, it, 3))
                        dve.wait_ge(*wkv_act(s, it, 1 + d))
                        nc.vector.tensor_tensor(num, e_new, flat(VV), ALU.mult).then_inc(*q.step(s))
                        dve.wait_ge(*q(s, it, 12 + 3 * d))
                        if d:
                            e_old, e_new, num = e_old[:, ::-1], e_new[:, ::-1], num[:, ::-1]
                        nc.vector.tensor_tensor_scan(e_new, e_old, e_new, 0.0, ALU.mult, ALU.add).then_inc(*q.step(s))
                        nc.vector.tensor_tensor_scan(num, e_old, num, 0.0, ALU.mult, ALU.add).then_inc(*q.step(s))
                    elif k in (8, 9):
                        d = k - 8
                        dve.wait_ge(*wkv_act(s, it, 3))
                        dve.wait_ge(*q(s, it, 14 + 3 * d))
                        for n in range(2):
                            last = nc.vector.tensor_tensor((tot, oth)[d][:, n], SUMS[d][n][:, 0, :, 2 * d:2 * d + SEQ], args[:, d], ALU.mult)
                        last.then_inc(*q.step(s))
                    elif k == 10:
                        dve.wait_ge(*q(s, it, 19))
                        nc.vector.tensor_tensor(big_b[s][:, 0:2 * n3], big_b[s][:, 0:2 * n3], big_b[s][:, 2 * n3:4 * n3], ALU.add).then_inc(*q.step(s))
                    elif k == 11:
                        dve.wait_ge(*q(s, it, 20))
                        nc.vector.tensor_tensor(tot[:, 1], tot[:, 1], args[:, 2], ALU.add).then_inc(*q.step(s))
                        dve.wait_ge(*wkv_pool(s, it, 1))
                        nc.vector.tensor_tensor(big_b[s][:, 0:n3], big_b[s][:, 0:n3], big_a[s][:, 3 * n3:4 * n3], ALU.add).then_inc(*q.step(s))
                    elif k in (12, 13):
                        if k == 12:
                            dve.wait_ge(*q(s, it, 21))
                            dve.wait_ge(*kv_act(s, it, 4))
                            nc.vector.scalar_tensor_tensor(out=den, in0=exp_r[s][:, 0:n3], scalar=1.0, in1=den, op0=ALU.add, op1=ALU.mult).then_inc(*q.step(s))
                            dve.wait_ge(*q(s, it, 23))
                        for n in ((0,) if k == 12 else (1, 2)):
                            nc.vector.reciprocal(rec[:, n * SEQ:(n + 1) * SEQ], den[:, n * SEQ:(n + 1) * SEQ]).then_inc(*q.step(s))
                    else:
                        dve.wait_ge(*q(s, it, 26))
                        nc.vector.tensor_tensor(big_b[s][:, 0:n3], big_b[s][:, 0:n3], rec, ALU.mult).then_inc(*q.step(s))

                elif name == "out":
                    for b in range(2):
                        xa = two(XA[s])[:, b, :]
                        dve.wait_ge(*out_pe(s, it, b + 1))
                        dve.wait_ge(*resid(s, it, 1))
                        nc.vector.tensor_tensor(xa, xa, bank[:, 2 + b, 0:2 * C], ALU.add).then_inc(*out_dve.step(s))
                        dve.wait_ge(*out_dve(s, it, b + 1))
                        half_stats(s, b, XA[s])
                    ln_stats(ln_dve, s, it, 0, XA[s], TILES - 1)

                elif name == "mix_v" and k % 2:
                    b = k // 2
                    x, h = two(NX[s])[:, b, :], two(H[s])[:, b, :]
                    dve.wait_ge(*ff_pe(s, it, 1 + FT + k + 1))
                    nc.vector.tensor_tensor(x, x, bank[:, 2 + b, 0:2 * C], ALU.mult).then_inc(*ff_dve.step(s))
                    dve.wait_ge(*ff_dve(s, it, 2 * b + 1))
                    dve.wait_ge(*hadd(s, it, 1))
                    nc.vector.tensor_tensor(h, h, x, ALU.add).then_inc(*ff_dve.step(s))
                    dve.wait_ge(*ff_dve(s, it, 2 * b + 2))
                    half_stats(s, b, H[s])
                    if b:
                        ln_stats(ln_dve, s, it, 4, H[s], TILES - 1)

                elif (name, k) == ("route0", 0):
                    def sm(n):
                        return small[s][:, n, :].rearrange("p (t e) -> p t e", t=TILES)

                    def per_tile(n):
                        return small[s][:, n, 0:TILES]

                    q = moe_dve
                    dve.wait_ge(*moe_pe(s, it, 1))
                    nc.vector.tensor_scalar(small[s][:, 0, :], bank[:, 2, 0:TILES * E0], 1.0 / WSCALE, None, ALU.mult).then_inc(*q.step(s))
                    hold(*q(s, it, 1))
                    for t in range(TILES):
                        last = nc.vector.max(sm(1)[:, t, :], sm(0)[:, t, :])
                    last.then_inc(*q.step(s))
                    hold(*q(s, it, 2))
                    for t in range(TILES):
                        last = nc.vector.max_index(idx8[s][:, t, :], sm(1)[:, t, :], sm(0)[:, t, :])
                    last.then_inc(*q.step(s))
                    nc.vector.tensor_tensor(sm(2), sm(0), sm(1)[:, :, 0:1].broadcast_to([P, TILES, E0]), ALU.subtract).then_inc(*q.step(s))
                    dve.wait_ge(*q(s, it, 3))
                    nc.vector.tensor_copy(sm(4), idx8[s][:]).then_inc(*q.step(s))
                    dve.wait_ge(*q(s, it, 5))
                    iota = iota8[:].unsqueeze(1).broadcast_to([P, TILES, E0])
                    for n in range(2):
                        nc.vector.tensor_tensor(sm(5 + n), iota, sm(4)[:, :, n:n + 1].broadcast_to([P, TILES, E0]), ALU.is_equal).then_inc(*q.step(s))
                    dve.wait_ge(*q(s, it, 7))
                    nc.vector.tensor_tensor(sm(5), sm(5), sm(6), ALU.add).then_inc(*q.step(s))
                    dve.wait_ge(*q(s, it, 8))
                    dve.wait_ge(*moe_act(s, it, 1))
                    nc.vector.tensor_tensor(sm(5), sm(5), sm(3), ALU.mult).then_inc(*q.step(s))
                    nc.vector.tensor_reduce(per_tile(7), sm(3), AX.X, ALU.add).then_inc(*q.step(s))
                    dve.wait_ge(*q(s, it, 9))
                    nc.vector.tensor_reduce(per_tile(8), sm(5), AX.X, ALU.add).then_inc(*q.step(s))
                    dve.wait_ge(*q(s, it, 11))
                    nc.vector.scalar_tensor_tensor(out=per_tile(7), in0=per_tile(7), scalar=1e-9, in1=per_tile(8), op0=ALU.mult, op1=ALU.add).then_inc(*q.step(s))
                    dve.wait_ge(*q(s, it, 12))
                    nc.vector.reciprocal(per_tile(8), per_tile(7)).then_inc(*q.step(s))
                    dve.wait_ge(*q(s, it, 13))
                    nc.vector.scalar_tensor_tensor(out=sm(9), in0=sm(5), scalar=1.0 / WSCALE, in1=per_tile(8).unsqueeze(2).broadcast_to([P, TILES, E0]),
                                                   op0=ALU.mult, op1=ALU.mult).then_inc(*q.step(s))
                elif name == "route0":
                    dve.wait_ge(*moe_pe(s, it, 2))
                    nc.vector.tensor_copy(wT[s], bank[0:E0, 3, :]).then_inc(*moe_dve.step(s))
                elif name == "experts":
                    w = small[s][:, 9, :].rearrange("p (t e) -> p t e", t=TILES)
                    for n in (k, k + 1):
                        e2, t = divmod(n, TILES)
                        dve.wait_ge(*moe_pe(s, it, 2 + n + 1))
                        for side in range(2):
                            if side or e2:
                                dve.wait_ge(*mix(s, it, 2 * n + 1 if side else 2 * (n - TILES) + 2))
                            e = 2 * e2 + side
                            nc.vector.scalar_tensor_tensor(out=H[s][:, t, :], in0=bank[:, n % 2, side * C:(side + 1) * C], scalar=w[:, t, e:e + 1],
                                                           in1=H[s][:, t, :], op0=ALU.mult, op1=ALU.add).then_inc(*mix.step(s))
                elif name == "experts_b":
                    dve.wait_ge(*moe_pe(s, it, 2 + 16 + 1))
                    dve.wait_ge(*mix(s, it, 32))
                    nc.vector.tensor_tensor(two(H[s]), two(H[s]), bank[:, 2:4, 0:2 * C], ALU.add).then_inc(*mix.step(s))
                    dve.wait_ge(*mix(s, it, 33))
                    ln_stats(ln3_dve, s, it, 0, H[s])

                elif name == "feat":
                    q = feat_dve
                    if k == 0:
                        dve.wait_ge(*feat_act(s, it, 1))
                        nc.vector.tensor_reduce(stab[s][:, 1, :], NX[s].rearrange("p t (h d) -> p (t h) d", d=DH), AX.X, ALU.add).then_inc(*q.step(s))
                    b, n = 2 * (k % 2), 1 + 3 * k
                    sl = slice(k * HEADS, (k + 1) * HEADS)
                    uv = bank[:, b:b + 2, :].rearrange("p b c -> p (b c)")[:, 0:HEADS * MF].rearrange("p (h m) -> p h m", m=MF)
                    dve.wait_ge(*feat_pe(s, it, k + 1))
                    nc.vector.tensor_reduce(stab[s][:, 0, sl], uv, AX.X, ALU.max).then_inc(*q.step(s))
                    dve.wait_ge(*q(s, it, n + 1))
                    nc.vector.scalar_tensor_tensor(out=stab[s][:, 3, sl], in0=stab[s][:, 1, sl], scalar=0.5, in1=stab[s][:, 0, sl],
                                                   op0=ALU.mult, op1=ALU.add).then_inc(*q.step(s))
                    dve.wait_ge(*q(s, it, n + 2))
                    nc.vector.tensor_tensor(big_a[s][:, k * HEADS * MF:(k + 1) * HEADS * MF].rearrange("p (h m) -> p h m", m=MF), uv,
                                            stab[s][:, 3, sl].unsqueeze(2).broadcast_to([P, HEADS, MF]), ALU.subtract).then_inc(*q.step(s))
                elif (name, k) == ("stab", 0):
                    dve.wait_ge(*stab_pe(s, it, 1))
                    nc.vector.tensor_reduce(stabT[s][:, :, 0], bank[0:HEADS, 2, :].rearrange("h (b n) -> h b n", b=2), AX.X, ALU.max).then_inc(*stab_dve.step(s))
                    dve.wait_ge(*stab_dve(s, it, 1))
                    nc.vector.tensor_tensor(stabT[s][:, :, 1:1 + HEADS], ident[0:HEADS, 0:HEADS].unsqueeze(1).broadcast_to([HEADS, 2, HEADS]),
                                            stabT[s][:, :, 0:1].broadcast_to([HEADS, 2, HEADS]), ALU.mult).then_inc(*stab_dve.step(s))
                elif (name, k) == ("stab", 2):
                    dve.wait_ge(*stab_pe(s, it, 2))
                    nc.vector.tensor_tensor(stab[s][:, 2, :].rearrange("p (b t h) -> p b t h", b=2, t=2), stab[s][:, 0, :].rearrange("p (b t h) -> p b t h", b=2, t=2),
                                            bank[:, 3, 0:2 * HEADS].rearrange("p (b h) -> p b h", b=2).unsqueeze(2).broadcast_to([P, 2, 2, HEADS]),
                                            ALU.subtract).then_inc(*stab_dve.step(s))
                elif name == "stab" and k == 3:
                    dve.wait_ge(*stab_act(s, it, 1))
                    nc.vector.tensor_tensor(CV[s], HV[s][:], stab[s][:, 2, :].unsqueeze(2).broadcast_to([P, TILES * HEADS, HV1]), ALU.mult).then_inc(*stab_dve.step(s))
                elif (name, k) == ("ctx", 1):
                    dve.wait_ge(*ctx_pe(s, it, 2))
                    src = bank[:, 2, 0:2 * HEADS * HV1].rearrange("p (b j c) -> p b j c", b=2, j=HEADS // 2)
                    for b in range(2):
                        for hh in range(2):
                            rows, cols = slice(hh * MF, (hh + 1) * MF), slice(hh * HV1, (hh + 1) * HV1)
                            last = nc.vector.tensor_copy(CTX[s][rows, b, :, cols], src[rows, b, :, cols])
                    last.then_inc(*ctx_dve.step(s))
                elif name == "attn" and k % 2:
                    b = k // 2
                    src = bank[:, 3 - b, 0:2 * HEADS * HV1].rearrange("p (q e) -> p q e", e=HV1)
                    heads = slice(2 * b * HEADS, (2 * b + 2) * HEADS)
                    x, xa = two(NX[s])[:, b, :], two(XA[s])[:, b, :]
                    dve.wait_ge(*attn_pe(s, it, k + 1))
                    nc.vector.reciprocal(stab[s][:, 1, heads], src[:, :, DH]).then_inc(*attn_dve.step(s))
                    dve.wait_ge(*attn_dve(s, it, 3 * b + 1))
                    nc.vector.tensor_tensor(NX[s].rearrange("p t (h d) -> p (t h) d", d=DH)[:, heads, :], src[:, :, 0:DH],
                                            stab[s][:, 1, heads].unsqueeze(2).broadcast_to([P, 2 * HEADS, DH]), ALU.mult).then_inc(*attn_dve.step(s))
                    dve.wait_ge(*attn_dve(s, it, 3 * b + 2))
                    dve.wait_ge(*resid(s, it, 3))
                    nc.vector.tensor_tensor(xa, xa, x, ALU.add).then_inc(*attn_dve.step(s))
                    dve.wait_ge(*attn_dve(s, it, 3 * b + 3))
                    half_stats(s, b, XA[s])
                    if b:
                        ln_stats(ln_dve, s, it, 8, XA[s], TILES - 1)
                elif name == "mlp_out" and k % 2:
                    b = k // 2
                    h = two(H[s])[:, b, :]
                    dve.wait_ge(*mlp_pe(s, it, FT + k + 1))
                    dve.wait_ge(*hadd(s, it, 2))
                    nc.vector.tensor_tensor(h, h, bank[:, 2 + b, 0:2 * C], ALU.add).then_inc(*mlp_dve.step(s))
                    dve.wait_ge(*mlp_dve(s, it, b + 1))
                    half_stats(s, b, H[s])
                    if b:
                        ln_stats(ln_dve, s, it, 12, H[s], TILES - 1)

                elif name == "route1":
                    q = rt_dve
                    pr = small[s][:, 0, 0:TILES * E1].rearrange("p (t e) -> p t e", e=E1)
                    kp = small[s][:, 1, 0:TILES * E1].rearrange("p (t e) -> p t e", e=E1)
                    low = small[s][:, 2, 0:2 * TILES].rearrange("p (n t) -> p n t", n=2)
                    dve.wait_ge(*rt_act(s, it, 1))
                    nc.vector.tensor_tensor(low[:, 0, :], pr[:, :, 0], pr[:, :, 1], ALU.min)
                    nc.vector.tensor_tensor(low[:, 1, :], pr[:, :, 1], pr[:, :, 2], ALU.min).then_inc(*q.step(s))
                    dve.wait_ge(*q(s, it, 1))
                    nc.vector.tensor_tensor(kp[:, :, 2], pr[:, :, 2], low[:, 0, :], ALU.is_gt)
                    nc.vector.tensor_tensor(kp[:, :, 0], pr[:, :, 0], low[:, 1, :], ALU.is_ge).then_inc(*q.step(s))
                    dve.wait_ge(*q(s, it, 2))
                    nc.vector.tensor_tensor(low[:, 0, :], kp[:, :, 0], kp[:, :, 2], ALU.add).then_inc(*q.step(s))
                    dve.wait_ge(*q(s, it, 3))
                    nc.vector.tensor_scalar(kp[:, :, 1], low[:, 0, :], -1.0, 2.0, ALU.mult, ALU.add).then_inc(*q.step(s))
                    dve.wait_ge(*q(s, it, 4))
                    nc.vector.tensor_tensor(kp, kp, pr, ALU.mult).then_inc(*q.step(s))
                    dve.wait_ge(*q(s, it, 5))
                    nc.vector.tensor_reduce(low[:, 0, :], kp, AX.X, ALU.add).then_inc(*q.step(s))
                    dve.wait_ge(*q(s, it, 6))
                    nc.vector.reciprocal(low[:, 1, :], low[:, 0, :]).then_inc(*q.step(s))
                    dve.wait_ge(*q(s, it, 7))
                    nc.vector.scalar_tensor_tensor(out=kp, in0=kp, scalar=1.0 / WSCALE, in1=low[:, 1, :].unsqueeze(2).broadcast_to([P, TILES, E1]),
                                                   op0=ALU.mult, op1=ALU.mult).then_inc(*q.step(s))
                elif name == "gate":
                    x, j = divmod(k, IT)
                    dve.wait_ge(*ex_pe(s, it, ex_steps("gate", k, pe=True)))
                    dve.wait_ge(*ex_act(s, it, k + 1))
                    if x >= 2:
                        dve.wait_ge(*ex_pe(s, it, ex_steps("down", x - 2, pe=True)))
                    at_ = (x % 2 * IT + j) * CHUNK
                    nc.vector.tensor_tensor(big_b[s][:, at_:at_ + CHUNK], bank[:, 1, :], big_a[s][:, at_:at_ + CHUNK],
                                            ALU.mult).then_inc(*ex_dve.step(s))
                elif name == "down":
                    q = ex_dve
                    kp = small[s][:, 1, 0:TILES * E1].rearrange("p (t e) -> p t e", e=E1)
                    for b, half_name in enumerate(("down_a", "down")):
                        dve.wait_ge(*ex_pe(s, it, ex_steps(half_name, k, pe=True)))
                        if k == 0:
                            h = two(H[s])[:, b, :]
                            last = nc.vector.scalar_tensor_tensor(out=h, in0=bank[:, 2 + b, 0:2 * C], scalar=1.0 / WSCALE, in1=h, op0=ALU.mult, op1=ALU.add)
                        else:
                            if b == 0:
                                dve.wait_ge(*q(s, it, ex_steps("down", k - 1)))
                                dve.wait_ge(*rt_dve(s, it, 8))
                            for t in (2 * b, 2 * b + 1):
                                last = nc.vector.scalar_tensor_tensor(out=H[s][:, t, :], in0=bank[:, 2 + b, (t % 2) * C:(t % 2 + 1) * C],
                                                                      scalar=kp[:, t, k - 1:k], in1=H[s][:, t, :], op0=ALU.mult, op1=ALU.add)
                    last.then_inc(*q.step(s))

            all_passes(dve, stage)

        @block.tensor
        def _(pe):
            for f in (embed_pe, tr, kv_pe, out_pe, ff_pe, moe_pe, feat_pe, stab_pe, ctx_pe, et_pe, attn_pe, mlp_pe, rt_pe, ex_pe):
                f.credit(pe)
            pe.sem_inc(table_mm, RING)
            pe.wait_ge(const_pool, 3 + 3 + 1 + STREAMS)
            pe.wait_ge(ident_in, 16)
            nc.tensor.matmul(gram, ident[0:1, 1:1 + RANK], HV[1][0:1, :, :].rearrange("p q e -> p (q e)")[:, 0:CR], start=True, stop=False,
                             skip_group_check=True)
            with pe.Fori(0, LOADS // RING) as it:
                for b in range(RING):
                    pe.wait_ge(table_in[b], it * 32 + 32)
                    for j in range(ROWS):
                        last = nc.tensor.matmul(gram, tab[b][:, j, C:CR], tab[b][:, j, :], start=False, stop=False, skip_group_check=True)
                    last.then_inc(table_mm, 1)
            pe.wait_ge(table_in[0], LOADS // RING * 32 + 32)
            nc.tensor.matmul(gram, tab[0][0:TAIL, 0, C:CR], tab[0][0:TAIL, 0, :], start=False, stop=True,
                             skip_group_check=True).then_inc(table_mm, 1)
            pe.wait_ge(norm_act, 1)
            pe.wait_ge(loaded, 16 * len(loads))
            nc.tensor.matmul(PS[0][0:RANK, 1, 0:C], gram_sb[:, C:CR], lora_b[:], start=True, stop=True).then_inc(norm_pe, 1)
            pe.wait_ge(norm_dve, 4)
            nc.tensor.matmul(PS[0][:, 2, 0:C], ones[:], colsum, start=True, stop=False)
            nc.tensor.matmul(PS[0][:, 2, 0:C], ones[0:RANK, :], cross, start=False, stop=True).then_inc(norm_pe, 1)
            pe.wait_ge(const_dve, 3)
            pe.wait_ge(proj_dve, 7)
            pe.wait_ge(norm_dve, NORM_STEPS)

            def halves(name, lo_, hi_):
                c = slice(COLS[name] + lo_, COLS[name] + hi_)
                return ((wcat[:, 0, c], 0, P), (wcat[:, 0, c], 1, P), (wcat[:, 1, c], 0, P), (wcat[:, 2, c], 2, P), (wcat[0:C1, 3, c], 2, C1))

            def by_channel(dst, terms, s, t0=0, t1=CHUNK):
                for n, (w, plane, rows) in enumerate(terms):
                    last = nc.tensor.matmul(dst, w, xh[s][0:rows, plane, t0:t1], start=(n == 0), stop=(n == len(terms) - 1))
                return last

            def by_token(dst, terms, s, t, bias=None):
                for n, (w, plane, rows) in enumerate(terms):
                    last = nc.tensor.matmul(dst, xh[s][0:rows, plane, t * P:(t + 1) * P], w, start=(n == 0), stop=(n == len(terms) - 1 and bias is None))
                if bias is not None:
                    last = nc.tensor.matmul(dst, ones[0:1, :], bias, start=False, stop=True)
                return last

            def bank_of(s, t):
                return PS[s][:, 2 + t // 2, (t % 2) * C:(t % 2 + 1) * C]

            def last_channels(col, name, bank, s):
                for b in range(2):
                    last = by_channel(PS[s][b * C1:(b + 1) * C1, bank, col:col + SEQ], halves(name, P, C), s, b * SEQ, (b + 1) * SEQ)
                return last

            NORMED = {0: (ln0_dve, 6), 1: (ln_dve, 4), 2: (ln_dve, 8), 3: (ln3_dve, 5), 4: (ln_dve, 12), 5: (ln_dve, 16)}

            def stage(name, k, s, it):
                bank = PS[s]
                if (name, k) == ("embed", 0):
                    pe.wait_ge(row_in[s], it + UNIT)
                    pe.wait_ge(*ex_dve(s, it, 0))
                    for t in range(TILES):
                        last = nc.tensor.transpose(bank[0:RANK, 0, t * P:(t + 1) * P], glora[s][:, t, :], ident[:])
                    last.then_inc(*embed_pe.step(s))
                elif name == "embed":
                    pe.wait_ge(*embed_act(s, it, 1))
                    for t in range(TILES):
                        last = nc.tensor.matmul(bank[:, 1 + t // 2, (t % 2) * C:(t % 2 + 1) * C], big_a[s][0:RANK, t * P:(t + 1) * P], lora_b[:],
                                                start=True, stop=True)
                    last.then_inc(*embed_pe.step(s))

                elif name == "norm":
                    src, _ = TR_BANKS[k]
                    f, n = NORMED[k]
                    pe.wait_ge(*f(s, it, n))
                    for part, chans in ((0, slice(0, P)), (1, slice(P, C))):
                        for t in range(TILES):
                            last = nc.tensor.transpose(bank[0:chans.stop - chans.start, src[part], t * P:(t + 1) * P], NX[s][:, t, chans], ident[:])
                        last.then_inc(*tr.step(s))

                elif name == "kv":
                    if k == 0:
                        pe.wait_ge(*lo(s, it, 1))
                        by_channel(bank[:, 1, :], halves("k", 0, P), s)
                        last_channels(0, "k", 2, s).then_inc(*kv_pe.step(s))
                    elif k == 1:
                        by_channel(bank[:, 3, :], halves("v", 0, P), s)
                        pe.wait_ge(*kv_act(s, it, 2))
                        last_channels(SEQ, "v", 2, s).then_inc(*kv_pe.step(s))
                    else:
                        by_channel(bank[:, 0, :], halves("r", 0, P), s)
                        last_channels(0, "r", 1, s).then_inc(*kv_pe.step(s))

                elif name == "out":
                    pe.wait_ge(*wkv_dve(s, it, 27))
                    for t in range(TILES):
                        b, h = t // 2, t % 2
                        nc.tensor.matmul(bank_of(s, t), big_b[s][:, t * P:(t + 1) * P], wo[:, 0, :], start=True, stop=False)
                        last = nc.tensor.matmul(bank_of(s, t), big_b[s][b * C1:(b + 1) * C1, CHUNK + h * P:CHUNK + (h + 1) * P],
                                                wo[b * C1:(b + 1) * C1, 1, :], start=False, stop=True)
                        if t % 2:
                            last.then_inc(*out_pe.step(s))

                elif name == "mix_r":
                    pe.wait_ge(*lo(s, it, 2))
                    for t in range(TILES):
                        last = by_token(bank_of(s, t), halves("rf", 0, C), s, t)
                    last.then_inc(*ff_pe.step(s))
                elif name == "mix_k":
                    if k >= 2:
                        pe.wait_ge(*ff_act(s, it, 2 + 2 * (k - 2)))
                    by_channel(bank[:, k % 2, :], halves("kf", k * P, (k + 1) * P), s).then_inc(*ff_pe.step(s))
                elif name == "mix_v":
                    if k == 0:
                        pe.wait_ge(*ff_act(s, it, 1 + 2 * FT))
                    for j in range(FT):
                        last = nc.tensor.matmul(bank_of(s, k), big_a[s][:, j * CHUNK + k * P:j * CHUNK + (k + 1) * P], wvf[:, j, :],
                                                start=(j == 0), stop=(j == FT - 1))
                    last.then_inc(*ff_pe.step(s))

                elif (name, k) == ("route0", 0):
                    pe.wait_ge(*lo(s, it, 3))
                    for t in range(TILES):
                        last = by_token(bank[:, 2, t * E0:(t + 1) * E0], halves("router0", 0, E0), s, t, router0_b[:])
                    last.then_inc(*moe_pe.step(s))
                elif name == "route0":
                    pe.wait_ge(*moe_dve(s, it, 14))
                    for t in range(TILES):
                        last = nc.tensor.transpose(bank[0:E0, 3, t * P:(t + 1) * P], small[s][:, 9, t * E0:(t + 1) * E0], ident[:])
                    last.then_inc(*moe_pe.step(s))
                elif name == "experts":
                    for n in (k, k + 1):
                        e2, t = divmod(n, TILES)
                        if n >= 2:
                            pe.wait_ge(*mix(s, it, 2 * (n - 2) + 2))
                        by_token(bank[:, n % 2, 0:2 * C], halves("experts", 2 * e2 * C, 2 * (e2 + 1) * C), s, t).then_inc(*moe_pe.step(s))
                elif name == "experts_b":
                    pe.wait_ge(*moe_dve(s, it, 15))
                    for t in range(TILES):
                        last = nc.tensor.matmul(bank_of(s, t), wT[s][:, t * P:(t + 1) * P], experts_b, start=True, stop=True)
                    last.then_inc(*moe_pe.step(s))

                elif name == "feat":
                    b = 2 * (k % 2)
                    pe.wait_ge(*(lo(s, it, 4) if k < 2 else feat_dve(s, it, 1 + 3 * (k - 1))))
                    x = [xh[s][:, n, k * P:(k + 1) * P] for n in range(3)]
                    for n, (xs, w) in enumerate(((x[0], 0), (x[1], 0), (x[0], 1))):
                        nc.tensor.matmul(bank[:, b, :], xs, proj0[:, w, :], start=(n == 0), stop=(n == 2))
                    dst = bank[:, b + 1, 0:(HEADS - HK0) * MF]
                    nc.tensor.matmul(dst, x[2], proj1[:, 0, :], start=True, stop=False)
                    nc.tensor.matmul(dst, x[2][0:C1], proj1[0:C1, 1, :], start=False, stop=True).then_inc(*feat_pe.step(s))
                elif (name, k) == ("stab", 0):
                    pe.wait_ge(*feat_dve(s, it, 1 + 3 * TILES))
                    for t in range(TILES):
                        last = nc.tensor.transpose(bank[0:HEADS, 2, t * P:(t + 1) * P], stab[s][:, 0, t * HEADS:(t + 1) * HEADS], ident[:])
                    last.then_inc(*stab_pe.step(s))
                elif (name, k) == ("stab", 1):
                    pe.wait_ge(*stab_dve(s, it, 2))
                    for b in range(2):
                        last = nc.tensor.matmul(bank[:, 3, b * HEADS:(b + 1) * HEADS], ones[0:HEADS, :], stabT[s][:, b, 1:1 + HEADS], start=True, stop=True)
                    last.then_inc(*stab_pe.step(s))
                elif name == "ctx":
                    if k == 0:
                        pe.wait_ge(*stab_dve(s, it, 4))
                        pe.wait_ge(*feat_act(s, it, 1 + TILES))
                    w = HEADS * HV1
                    b = k
                    for t in (2 * b, 2 * b + 1):
                        nc.tensor.matmul(bank[:, 2, b * w:(b + 1) * w], feat_eps[:], HV[s][:, t * HEADS:(t + 1) * HEADS, :].rearrange("p q e -> p (q e)"),
                                         start=(t == 2 * b), stop=False, skip_group_check=True)
                    for t in (2 * b, 2 * b + 1):
                        for j in range(HEADS // 2):
                            q = t * HEADS + 2 * j
                            last = nc.tensor.matmul(bank[:, 2, b * w + j * 2 * HV1:b * w + (j + 1) * 2 * HV1], big_a[s][:, q * MF:(q + 2) * MF],
                                                    CV[s][:, q:q + 2, :].rearrange("p q e -> p (q e)"), start=False, stop=(t == 2 * b + 1),
                                                    skip_group_check=True)
                    last.then_inc(*ctx_pe.step(s))
                elif name == "featT":
                    pe.wait_ge(*(et_act(s, it, k - 1) if k >= 2 else feat_act(s, it, 1 + TILES)))
                    for t in range(TILES):
                        last = nc.tensor.transpose(bank[:, k % 2, t * P:(t + 1) * P], big_a[s][:, t * HEADS * MF + k * P:t * HEADS * MF + (k + 1) * P], ident[:])
                    last.then_inc(*et_pe.step(s))
                elif name == "attn":
                    if k == 0:
                        pe.wait_ge(*ctx_dve(s, it, 1))
                        pe.wait_ge(*et_act(s, it, FT))
                    t = k
                    for j in range(HEADS // 2):
                        col = (t % 2) * HEADS * HV1 + j * 2 * HV1
                        last = nc.tensor.matmul(bank[:, 3 - t // 2, col:col + 2 * HV1], big_b[s][:, j * CHUNK + t * P:j * CHUNK + (t + 1) * P],
                                                CTX[s][:, t // 2, j, :], start=True, stop=True)
                    last.then_inc(*attn_pe.step(s))

                elif name == "mlp":
                    pe.wait_ge(*(lo(s, it, 5) if k < 2 else mlp_act(s, it, k - 1)))
                    by_channel(bank[:, k % 2, :], halves("w1", k * P, (k + 1) * P), s).then_inc(*mlp_pe.step(s))
                elif name == "mlp_out":
                    if k == 0:
                        pe.wait_ge(*mlp_act(s, it, FT))
                    nc.tensor.matmul(bank_of(s, k), ones[32:33, :], b2, start=True, stop=False)
                    for j in range(FT):
                        last = nc.tensor.matmul(bank_of(s, k), big_a[s][:, j * CHUNK + k * P:j * CHUNK + (k + 1) * P], w2[:, j, :],
                                                start=False, stop=(j == FT - 1))
                    last.then_inc(*mlp_pe.step(s))

                elif name == "route1":
                    pe.wait_ge(*lo(s, it, 6))
                    for t in range(TILES):
                        last = by_token(bank[:, 2, t * E1:(t + 1) * E1], halves("router1", 0, E1), s, t, router1_b[:])
                    last.then_inc(*rt_pe.step(s))
                elif name == "gate":
                    x, j = divmod(k, IT)
                    at_ = 2 * x * I1 + j * P
                    if k:
                        pe.wait_ge(*ex_act(s, it, k))
                    by_channel(bank[:, 0, :], halves("gate_up", at_, at_ + P), s).then_inc(*ex_pe.step(s))
                    if k:
                        pe.wait_ge(*ex_dve(s, it, ex_steps("gate", k - 1)))
                    by_channel(bank[:, 1, :], halves("gate_up", at_ + I1, at_ + I1 + P), s).then_inc(*ex_pe.step(s))
                elif name in ("down_a", "down"):
                    if name == "down_a":
                        pe.wait_ge(*(ex_dve(s, it, ex_steps("down", k - 1)) if k else rt_act(s, it, 1)))
                        pe.wait_ge(*ex_dve(s, it, ex_steps("gate", (k + 1) * IT - 1)))
                    for t in ((0, 1) if name == "down_a" else (2, 3)):
                        for j in range(IT):
                            last = nc.tensor.matmul(bank_of(s, t), big_b[s][:, (k % 2 * IT + j) * CHUNK + t * P:(k % 2 * IT + j) * CHUNK + (t + 1) * P], down[:, k, j, :],
                                                    start=(j == 0), stop=(j == IT - 1))
                    last.then_inc(*ex_pe.step(s))

            all_passes(pe, stage)


def kernel(**inputs):
    import numpy as np
    import concourse.bacc as bacc
    from concourse.bass_utils import run_bass_kernel_spmd

    g = {n: np.asarray(v) for n, v in inputs.items()}

    def col(*names):
        return np.ascontiguousarray(np.stack([g[n] for n in names], axis=1))

    B, S = g["x"].shape
    C = g["L0_tok_embeddings"].shape[1]
    E0 = g["L0_ffn_router_w"].shape[0]
    arrays = {
        "idx": g["x"].reshape(-1, TILES, P).transpose(0, 2, 1),
        "embeddings": g["L0_tok_embeddings"], "lora_a": g["L0_tok_lora_a"], "lora_b": g["L0_tok_lora_b"],
        "magnitude": g["L0_tok_magnitude"].reshape(1, C),
        "ln_cols": col("L0_attn_ln1_w", "L0_attn_ln1_b", "L0_attn_ln2_w", "L0_attn_ln2_b"),
        "ln2_cols": col("L1_attn_ln2_g", "L1_attn_ln2_b"),
        "ln1_g": g["L1_attn_ln1_g"].reshape(1, C), "ln1_b": g["L1_attn_ln1_b"].reshape(1, C),
        "wu": col("L0_attn_decay", "L0_attn_first"),
        "WoT": g["L0_attn_Wo_a"].T, "WvfT": g["L0_attn_Wv_f"].T, "router0_b": g["L0_ffn_router_b"].reshape(1, E0),
        "experts_b": g["L0_ffn_expert_b"],
        "projT": g["L1_attn_proj"].T, "b1": g["L1_attn_b1"].reshape(-1, P).T,
        "W2": g["L1_attn_W2"], "b2": g["L1_attn_b2"].reshape(1, C),
        "down": np.concatenate([g["L1_ffn_shared_down"][None], g["L1_ffn_routed_down"]], axis=0),
        "router1_b": g["L1_ffn_routing_bias"].reshape(1, -1),
        "ident": np.eye(P, dtype=np.float32), "iota8": np.arange(E0, dtype=np.float32).reshape(1, E0),
    }
    wcat = np.concatenate([
        g["L0_attn_Wk_a"].T, g["L0_attn_Wv_a"].T, g["L0_attn_Wr_a"].T, g["L0_attn_Wk_f"].T, g["L0_attn_Wr_f"].T,
        g["L0_ffn_expert_w"].transpose(2, 0, 1).reshape(C, -1), g["L1_attn_W1"],
        g["L1_ffn_shared_gate"], g["L1_ffn_shared_up"],
        *[w for pair in zip(g["L1_ffn_routed_gate"], g["L1_ffn_routed_up"]) for w in pair],
        g["L0_ffn_router_w"].T, g["L1_ffn_router_w"],
    ], axis=1)
    arrays["wcat"] = wcat.reshape(C, WEIGHT_PIECES, -1).transpose(1, 0, 2)
    nc = bacc.Bacc("TRN2", target_bir_lowering=False, num_devices=1)
    fed, aps = {}, {}
    for n, v in arrays.items():
        v = np.ascontiguousarray(v)
        fed[f"in_{n}"] = v
        aps[n] = nc.dram_tensor(f"in_{n}", v.shape, mybir.dt.from_np(v.dtype), kind="ExternalInput").ap()
    aps["SEQ"], aps["proj_shape"] = S, g["L1_attn_proj"].shape
    out = nc.dram_tensor("out_0", (B * S, C), F32, kind="ExternalOutput").ap()
    lm_tower(nc, aps, out)
    r = run_bass_kernel_spmd(nc, [fed], core_ids=[0])
    return r.results[0]["out_0"].reshape(B, S, C)
```
